# Optimizing a Trainium2 kernel written in Bass

```python
import numpy as np
import jax
import jax.numpy as jnp

def _softmax(x, axis=-1):
    return jax.nn.softmax(x, axis=axis)

def _gelu(x):
    return jax.nn.gelu(x, approximate=True)

def _silu(x):
    return jax.nn.silu(x)

def _sigmoid(x):
    return jax.nn.sigmoid(x)

def _layernorm(x, axis=-1, eps=1e-05):
    m = jnp.mean(x, axis=axis, keepdims=True)
    v = jnp.var(x, axis=axis, keepdims=True)
    return (x - m) / jnp.sqrt(v + eps)

def _scatter_add(tgt, idx, src, axis=0):
    return tgt.at[idx].add(src)

def _segment_sum(src, seg, n):
    return jax.ops.segment_sum(src, seg, n)
kernel_name = 'mk_hybrid_d1_jaxref_r8_098fc5'

def setup_inputs(seed: int=0):
    np.random.seed(seed)
    _w = jnp.asarray

    def _L0_attn_a_setup():
        import jax, jax.numpy as jnp
        import numpy as np
        B, L, D = (2, 256, 128)
        H, K = (16, 16)
        HD = D // H

        def tisa_bias(offsets, amplitudes, sharpness, seq_len):
            rel = jnp.arange(-(seq_len - 1), seq_len, dtype=jnp.float32)
            diff = offsets[:, :, None] - rel[None, None, :]
            scores = jnp.sum(amplitudes[:, :, None] * jnp.exp(-jnp.abs(sharpness)[:, :, None] * diff * diff), axis=1)
            i = jnp.arange(seq_len)
            idx = i[:, None] - i[None, :] + (seq_len - 1)
            return scores[:, idx]
        key = jax.random.key(seed)
        k1, k2, k3, k4, k5 = jax.random.split(key, 5)
        x = jax.random.normal(k1, (B, L, D), dtype=jnp.float32)
        w_in = jax.random.normal(k2, (3 * D, D), dtype=jnp.float32) * 0.02
        kernel_offsets = jax.random.normal(k3, (H, K), dtype=jnp.float32) * 20.0
        kernel_amplitudes = 0.1 + 0.01 * jax.random.normal(k4, (H, K), dtype=jnp.float32)
        kernel_sharpness = 0.1 + 0.01 * jax.random.normal(k5, (H, K), dtype=jnp.float32)
        return {'x': x, 'w_in': w_in, 'kernel_offsets': kernel_offsets, 'kernel_amplitudes': kernel_amplitudes, 'kernel_sharpness': kernel_sharpness}
    _L0_attn_a_in = _L0_attn_a_setup()

    def _L0_attn_b_setup():
        import jax, jax.numpy as jnp
        import numpy as np
        D_MODEL = 128
        D_STATE = 128
        HEADDIM = 64
        EXPAND = 2
        D_CONV = 4
        D_INNER = EXPAND * D_MODEL
        NHEADS = D_INNER // HEADDIM
        CONV_DIM = D_INNER + 2 * D_STATE
        D_IN_PROJ = 2 * D_INNER + 2 * D_STATE + NHEADS
        BATCH, SEQLEN = (4, 256)
        EPS = 1e-05

        def _mamba3(x, W_in, conv_w, conv_b, dt_bias, A_log, D, norm_w, W_out):
            b, L, _ = x.shape
            zxbcdt = x @ W_in
            z = zxbcdt[..., :D_INNER]
            xBC = zxbcdt[..., D_INNER:D_INNER + CONV_DIM]
            dt = zxbcdt[..., D_INNER + CONV_DIM:]
            xp = jnp.pad(xBC, ((0, 0), (D_CONV - 1, 0), (0, 0)))
            xc = conv_b + sum((conv_w[k] * xp[:, k:k + L] for k in range(D_CONV)))
            xc = jax.nn.silu(xc)
            xh = xc[..., :D_INNER].reshape(b, L, NHEADS, HEADDIM)
            B = xc[..., D_INNER:D_INNER + D_STATE]
            C = xc[..., D_INNER + D_STATE:]
            dt = jax.nn.softplus(dt + dt_bias)
            dA = jnp.exp(dt * -jnp.exp(A_log))

            def step(h, inp):
                xh_t, B_t, C_t, dt_t, dA_t = inp
                h = dA_t[..., None, None] * h + (dt_t[..., None] * xh_t)[..., None] * B_t[:, None, None, :]
                y = jnp.einsum('bhpn,bn->bhp', h, C_t)
                return (h, y)
            tm = lambda a: jnp.swapaxes(a, 0, 1)
            h0 = jnp.zeros((b, NHEADS, HEADDIM, D_STATE), dtype=x.dtype)
            _, ys = jax.lax.scan(step, h0, (tm(xh), tm(B), tm(C), tm(dt), tm(dA)))
            y = jnp.swapaxes(ys, 0, 1)
            y = y + D[None, None, :, None] * xh
            y = y.reshape(b, L, D_INNER)
            y = y * jax.nn.silu(z)
            y = y * jax.lax.rsqrt(jnp.mean(y * y, axis=-1, keepdims=True) + EPS) * norm_w
            return y @ W_out
        key = jax.random.key(seed)
        ks = jax.random.split(key, 6)
        x = jax.random.normal(ks[0], (BATCH, SEQLEN, D_MODEL), dtype=jnp.float32)
        W_in = jax.random.normal(ks[1], (D_MODEL, D_IN_PROJ), dtype=jnp.float32) * 0.02
        conv_w = jax.random.normal(ks[2], (D_CONV, CONV_DIM), dtype=jnp.float32) * 0.1
        conv_b = jnp.zeros((CONV_DIM,), dtype=jnp.float32)
        dt_bias = jax.random.normal(ks[3], (NHEADS,), dtype=jnp.float32) * 0.1
        A_log = jnp.log(jnp.linspace(1.0, 16.0, NHEADS).astype(jnp.float32))
        D = jnp.ones((NHEADS,), dtype=jnp.float32)
        norm_w = jnp.ones((D_INNER,), dtype=jnp.float32)
        W_out = jax.random.normal(ks[4], (D_INNER, D_MODEL), dtype=jnp.float32) * 0.02
        return {'x': x, 'W_in': W_in, 'conv_w': conv_w, 'conv_b': conv_b, 'dt_bias': dt_bias, 'A_log': A_log, 'D': D, 'norm_w': norm_w, 'W_out': W_out}
    _L0_attn_b_in = _L0_attn_b_setup()

    def _L0_ffn_setup():
        import jax, jax.numpy as jnp
        import numpy as np
        H = 128
        E = 64
        K = 8
        G = 8
        TOPK_GROUP = 4
        I_MOE = 64
        I_SHARED = 256
        SCALE = 2.5

        def relu2(x):
            return jnp.square(jax.nn.relu(x))

        def _route(xf, router_w, correction_bias):
            T = xf.shape[0]
            logits = xf @ router_w.T
            scores = jax.nn.sigmoid(logits)
            sfc = scores + correction_bias[None, :]
            grp = sfc.reshape(T, G, E // G)
            top2, _ = jax.lax.top_k(grp, 2)
            group_scores = top2.sum(-1)
            _, gidx = jax.lax.top_k(group_scores, TOPK_GROUP)
            gmask = jnp.zeros((T, G), sfc.dtype).at[jnp.arange(T)[:, None], gidx].set(1.0)
            emask = jnp.repeat(gmask, E // G, axis=1)
            masked = jnp.where(emask > 0, sfc, 0.0)
            _, tidx = jax.lax.top_k(masked, K)
            tw = jnp.take_along_axis(scores, tidx, axis=1)
            tw = tw / (tw.sum(-1, keepdims=True) + 1e-20)
            return (tidx, tw * SCALE)
        key = jax.random.key(seed)
        ks = jax.random.split(key, 7)
        x = jax.random.normal(ks[0], (2, 128, H), dtype=jnp.float32)
        router_w = jax.random.normal(ks[1], (E, H), dtype=jnp.float32) * 0.02
        correction_bias = jax.random.normal(ks[2], (E,), dtype=jnp.float32) * 0.01
        up_w = jax.random.normal(ks[3], (E, H, I_MOE), dtype=jnp.float32) * 0.02
        down_w = jax.random.normal(ks[4], (E, I_MOE, H), dtype=jnp.float32) * 0.02
        shared_up_w = jax.random.normal(ks[5], (H, I_SHARED), dtype=jnp.float32) * 0.02
        shared_down_w = jax.random.normal(ks[6], (I_SHARED, H), dtype=jnp.float32) * 0.02
        return {'x': x, 'router_w': router_w, 'correction_bias': correction_bias, 'up_w': up_w, 'down_w': down_w, 'shared_up_w': shared_up_w, 'shared_down_w': shared_down_w}
    _L0_ffn_in = _L0_ffn_setup()
    _d = {'L0_attn_a_x': _L0_attn_a_in['x'], 'L0_attn_a_w_in': _L0_attn_a_in['w_in'], 'L0_attn_a_kernel_offsets': _L0_attn_a_in['kernel_offsets'], 'L0_attn_a_kernel_amplitudes': _L0_attn_a_in['kernel_amplitudes'], 'L0_attn_a_kernel_sharpness': _L0_attn_a_in['kernel_sharpness'], 'L0_attn_b_W_in': _L0_attn_b_in['W_in'], 'L0_attn_b_conv_w': _L0_attn_b_in['conv_w'], 'L0_attn_b_conv_b': _L0_attn_b_in['conv_b'], 'L0_attn_b_dt_bias': _L0_attn_b_in['dt_bias'], 'L0_attn_b_A_log': _L0_attn_b_in['A_log'], 'L0_attn_b_D': _L0_attn_b_in['D'], 'L0_attn_b_norm_w': _L0_attn_b_in['norm_w'], 'L0_attn_b_W_out': _L0_attn_b_in['W_out'], 'L0_ffn_router_w': _L0_ffn_in['router_w'], 'L0_ffn_correction_bias': _L0_ffn_in['correction_bias'], 'L0_ffn_up_w': _L0_ffn_in['up_w'], 'L0_ffn_down_w': _L0_ffn_in['down_w'], 'L0_ffn_shared_up_w': _L0_ffn_in['shared_up_w'], 'L0_ffn_shared_down_w': _L0_ffn_in['shared_down_w']}
    _x0 = _d['L0_attn_a_x']
    _d['L0_attn_a_x'] = jax.random.normal(jax.random.fold_in(jax.random.key(seed), 1), (2, 1024, 128), dtype=_x0.dtype)
    del _x0
    return _d

def reference(L0_attn_a_x, L0_attn_a_w_in, L0_attn_a_kernel_offsets, L0_attn_a_kernel_amplitudes, L0_attn_a_kernel_sharpness, L0_attn_b_W_in, L0_attn_b_conv_w, L0_attn_b_conv_b, L0_attn_b_dt_bias, L0_attn_b_A_log, L0_attn_b_D, L0_attn_b_norm_w, L0_attn_b_W_out, L0_ffn_router_w, L0_ffn_correction_bias, L0_ffn_up_w, L0_ffn_down_w, L0_ffn_shared_up_w, L0_ffn_shared_down_w):

    def _L0_attn_a_ref(x, w_in, kernel_offsets, kernel_amplitudes, kernel_sharpness):
        import jax, jax.numpy as jnp
        import numpy as np
        B, L, D = (2, 256, 128)
        H, K = (16, 16)
        HD = D // H

        def tisa_bias(offsets, amplitudes, sharpness, seq_len):
            rel = jnp.arange(-(seq_len - 1), seq_len, dtype=jnp.float32)
            diff = offsets[:, :, None] - rel[None, None, :]
            scores = jnp.sum(amplitudes[:, :, None] * jnp.exp(-jnp.abs(sharpness)[:, :, None] * diff * diff), axis=1)
            i = jnp.arange(seq_len)
            idx = i[:, None] - i[None, :] + (seq_len - 1)
            return scores[:, idx]
        b, l, d = x.shape
        proj = jnp.einsum('bld,ed->ble', x, w_in)
        k_, v_, q_ = (proj[..., :d], proj[..., d:2 * d], proj[..., 2 * d:])

        def heads(t):
            return t.reshape(b, l, H, HD).transpose(0, 2, 1, 3)
        q, k, v = (heads(q_), heads(k_), heads(v_))
        bias = tisa_bias(kernel_offsets, kernel_amplitudes, kernel_sharpness, l)
        scale = 1.0 / np.sqrt(HD).astype(np.float32)
        logits = jnp.einsum('bhld,bhmd->bhlm', q, k) * scale + bias[None]
        attn = jax.nn.softmax(logits, axis=-1)
        out = jnp.einsum('bhlm,bhmd->bhld', attn, v)
        return out.transpose(0, 2, 1, 3).reshape(b, l, d)

    def _L0_attn_b_ref(x, W_in, conv_w, conv_b, dt_bias, A_log, D, norm_w, W_out):
        import jax, jax.numpy as jnp
        import numpy as np
        D_MODEL = 128
        D_STATE = 128
        HEADDIM = 64
        EXPAND = 2
        D_CONV = 4
        D_INNER = EXPAND * D_MODEL
        NHEADS = D_INNER // HEADDIM
        CONV_DIM = D_INNER + 2 * D_STATE
        D_IN_PROJ = 2 * D_INNER + 2 * D_STATE + NHEADS
        BATCH, SEQLEN = (4, 256)
        EPS = 1e-05

        def _mamba3(x, W_in, conv_w, conv_b, dt_bias, A_log, D, norm_w, W_out):
            b, L, _ = x.shape
            zxbcdt = x @ W_in
            z = zxbcdt[..., :D_INNER]
            xBC = zxbcdt[..., D_INNER:D_INNER + CONV_DIM]
            dt = zxbcdt[..., D_INNER + CONV_DIM:]
            xp = jnp.pad(xBC, ((0, 0), (D_CONV - 1, 0), (0, 0)))
            xc = conv_b + sum((conv_w[k] * xp[:, k:k + L] for k in range(D_CONV)))
            xc = jax.nn.silu(xc)
            xh = xc[..., :D_INNER].reshape(b, L, NHEADS, HEADDIM)
            B = xc[..., D_INNER:D_INNER + D_STATE]
            C = xc[..., D_INNER + D_STATE:]
            dt = jax.nn.softplus(dt + dt_bias)
            dA = jnp.exp(dt * -jnp.exp(A_log))

            def step(h, inp):
                xh_t, B_t, C_t, dt_t, dA_t = inp
                h = dA_t[..., None, None] * h + (dt_t[..., None] * xh_t)[..., None] * B_t[:, None, None, :]
                y = jnp.einsum('bhpn,bn->bhp', h, C_t)
                return (h, y)
            tm = lambda a: jnp.swapaxes(a, 0, 1)
            h0 = jnp.zeros((b, NHEADS, HEADDIM, D_STATE), dtype=x.dtype)
            _, ys = jax.lax.scan(step, h0, (tm(xh), tm(B), tm(C), tm(dt), tm(dA)))
            y = jnp.swapaxes(ys, 0, 1)
            y = y + D[None, None, :, None] * xh
            y = y.reshape(b, L, D_INNER)
            y = y * jax.nn.silu(z)
            y = y * jax.lax.rsqrt(jnp.mean(y * y, axis=-1, keepdims=True) + EPS) * norm_w
            return y @ W_out
        return x + _mamba3(x, W_in, conv_w, conv_b, dt_bias, A_log, D, norm_w, W_out)

    def _L0_ffn_ref(x, router_w, correction_bias, up_w, down_w, shared_up_w, shared_down_w):
        import jax, jax.numpy as jnp
        import numpy as np
        H = 128
        E = 64
        K = 8
        G = 8
        TOPK_GROUP = 4
        I_MOE = 64
        I_SHARED = 256
        SCALE = 2.5

        def relu2(x):
            return jnp.square(jax.nn.relu(x))

        def _route(xf, router_w, correction_bias):
            T = xf.shape[0]
            logits = xf @ router_w.T
            scores = jax.nn.sigmoid(logits)
            sfc = scores + correction_bias[None, :]
            grp = sfc.reshape(T, G, E // G)
            top2, _ = jax.lax.top_k(grp, 2)
            group_scores = top2.sum(-1)
            _, gidx = jax.lax.top_k(group_scores, TOPK_GROUP)
            gmask = jnp.zeros((T, G), sfc.dtype).at[jnp.arange(T)[:, None], gidx].set(1.0)
            emask = jnp.repeat(gmask, E // G, axis=1)
            masked = jnp.where(emask > 0, sfc, 0.0)
            _, tidx = jax.lax.top_k(masked, K)
            tw = jnp.take_along_axis(scores, tidx, axis=1)
            tw = tw / (tw.sum(-1, keepdims=True) + 1e-20)
            return (tidx, tw * SCALE)
        B, S, Hd = x.shape
        xf = x.reshape(-1, Hd)
        T = xf.shape[0]
        tidx, tw = _route(xf.astype(jnp.float32), router_w, correction_bias)
        combine = jnp.zeros((T, E), xf.dtype).at[jnp.arange(T)[:, None], tidx].add(tw.astype(xf.dtype))

        def body(acc, ew):
            wu, wd, c = ew
            return (acc + c[:, None] * (relu2(xf @ wu) @ wd), None)
        routed, _ = jax.lax.scan(body, jnp.zeros_like(xf), (up_w, down_w, combine.T))
        shared = relu2(xf @ shared_up_w) @ shared_down_w
        return (routed + shared).reshape(B, S, Hd)
    x = L0_attn_a_x
    x = x + _L0_attn_a_ref(_layernorm(x, axis=-1), L0_attn_a_w_in, L0_attn_a_kernel_offsets, L0_attn_a_kernel_amplitudes, L0_attn_a_kernel_sharpness)
    x = x + _L0_ffn_ref(_layernorm(x, axis=-1), L0_ffn_router_w, L0_ffn_correction_bias, L0_ffn_up_w, L0_ffn_down_w, L0_ffn_shared_up_w, L0_ffn_shared_down_w)
    x = x + _L0_attn_b_ref(_layernorm(x, axis=-1), L0_attn_b_W_in, L0_attn_b_conv_w, L0_attn_b_conv_b, L0_attn_b_dt_bias, L0_attn_b_A_log, L0_attn_b_D, L0_attn_b_norm_w, L0_attn_b_W_out)
    x = x + _L0_ffn_ref(_layernorm(x, axis=-1), L0_ffn_router_w, L0_ffn_correction_bias, L0_ffn_up_w, L0_ffn_down_w, L0_ffn_shared_up_w, L0_ffn_shared_down_w)
    return x

_drawn_inputs = setup_inputs


def setup_inputs(seed=0):
    import zlib

    import numpy as np

    out = dict(_drawn_inputs(seed))
    spreads = {'L0_attn_b_conv_b': (0.0, 0.1),
     'L0_attn_b_D': (1.0, 0.2),
     'L0_attn_b_norm_w': (1.0, 0.559)}
    factors = {'L0_attn_a_w_in': 7.484,
     'L0_attn_a_kernel_offsets': 8.0,
     'L0_attn_a_kernel_amplitudes': 8.0,
     'L0_attn_a_kernel_sharpness': 8.0,
     'L0_attn_b_dt_bias': 37.184,
     'L0_attn_b_A_log': 31.32,
     'L0_ffn_router_w': 4.767,
     'L0_ffn_correction_bias': 8.0,
     'L0_ffn_up_w': 4.84,
     'L0_ffn_down_w': 4.413}
    for name, (base, spread) in spreads.items():
        noise = np.random.default_rng([zlib.crc32(name.encode()), seed]).standard_normal(out[name].shape)
        drawn = base * np.exp(spread * noise) if base else spread * noise
        out[name] = jnp.asarray(drawn.astype(out[name].dtype))
    for name, factor in factors.items():
        out[name] = (out[name] * factor).astype(out[name].dtype)
    return out
```

```python
import math
from contextlib import ExitStack

import concourse.bass as bass
from concourse import mybir

ALU = mybir.AluOpType
ACT = mybir.ActivationFunctionType
AX_X = mybir.AxisListType.X
F32 = mybir.dt.float32
BF16 = mybir.dt.bfloat16
F16 = mybir.dt.float16
F32R = mybir.dt.float32r

P = 128
D = 128
T = 2048
NT = T // P
BANK = 512
NQ = T // BANK
QT = BANK // P
LN_EPS = 1e-5


class Chain:

    def __init__(self, eng, sem, base=0):
        self.eng, self.sem, self.base, self.n = eng, sem, base, 0

    def add(self, ins):
        ins.then_inc(self.sem, 1)
        self.n += 1
        return ins

    def sync(self):
        self.eng.wait_ge(self.sem, self.base + self.n)

    def link(self, ins):
        self.add(ins)
        self.sync()


class Machine:

    def __init__(self, nc, ctx):
        self.nc, self.ctx = nc, ctx
        self.sems = []

    def sb(self, name, shape, dt=F32, ctx=None):
        return (ctx or self.ctx).enter_context(self.nc.sbuf_tensor(name, shape, dt))

    def ps(self, name, shape, dt=F32, ctx=None):
        return (ctx or self.ctx).enter_context(self.nc.psum_tensor(name, shape, dt))

    def sem(self, name):
        s = self.nc.alloc_semaphore(name=name)
        self.sems.append(s)
        return s

    def end_stage(self):
        self.nc.clear_and_free_semaphores(self.sems)
        self.sems = []
        self.nc.all_engine_barrier()


def build_constants(m):
    nc = m.nc
    m.ident = m.sb("ident", [P, P])
    m.ident16 = m.sb("ident16", [P, P], F16)
    m.identb = m.sb("identb", [P, P], BF16)
    m.flip = m.sb("flip", [P, P])
    m.flip16 = m.sb("flip16", [P, P], F16)
    m.upto = m.sb("upto", [P, P])
    m.after = m.sb("after", [P, P])
    m.ones = m.sb("ones", [P, P])
    m.before8 = m.sb("before8", [P, 8, 8])
    m.spread = m.sb("spread", [P, 64, 64], F16)
    filled, made = m.sem("const_filled"), m.sem("const_made")
    with nc.Block() as block:
        @block.gpsimd
        def _(pool):
            zero = [m.ident, m.ident16, m.identb, m.flip, m.flip16, m.spread]
            one = [m.upto, m.after, m.ones, m.before8]
            for t in zero:
                nc.gpsimd.memset(t[:], 0.0).then_inc(filled, 1)
            for t in one:
                nc.gpsimd.memset(t[:], 1.0).then_inc(filled, 1)
            pool.wait_ge(filled, len(zero) + len(one))

            def select(t, pattern, base, op, fill, mult):
                nc.gpsimd.affine_select(out=t, in_=t, compare_op=op, fill=fill, base=base,
                                        pattern=pattern, channel_multiplier=mult).then_inc(made, 1)
            for t in (m.ident, m.ident16, m.identb):
                select(t[:], [[-1, P]], 0, ALU.not_equal, 1.0, 1)
            for t in (m.flip, m.flip16):
                select(t[:], [[1, P]], -(P - 1), ALU.not_equal, 1.0, 1)
            select(m.upto[:], [[1, P]], 0, ALU.is_ge, 0.0, -1)
            select(m.after[:], [[-1, P]], -1, ALU.is_ge, 0.0, 1)
            select(m.before8[:], [[1, 8], [-1, 8]], -1, ALU.is_ge, 0.0, 0)
            select(m.spread[:], [[-1, 64], [0, 64]], 0, ALU.not_equal, 1.0, 1)
            pool.wait_ge(made, 9)
            select(m.spread[:], [[-1, 64], [0, 64]], -64, ALU.not_equal, 1.0, 1)
            pool.wait_ge(made, 10)


class LayerNorm:

    def __init__(self, m, tag, xn, xnT, bank):
        self.m, self.xn, self.xnT, self.bank = m, xn, xnT, bank
        self.stats = m.sb(f"{tag}_stats", [P, NT, 6], ctx=m.stage)
        self.tmp = m.sb(f"{tag}_tmp", [P, 8, NT], ctx=m.stage)
        self.stat = m.sem(f"{tag}_ln_order")
        self.var = m.sem(f"{tag}_var_ready")
        self.std = m.sem(f"{tag}_std_ready")
        self.norm = m.sem(f"{tag}_xn_ready")
        self.turned = m.sem(f"{tag}_turned")
        self.ready = m.sem(f"{tag}_xnT_ready")

    def vector(self, v):
        m, nc = self.m, self.m.nc
        ch = Chain(v, self.stat)
        for t in range(NT):
            ch.add(nc.vector.bn_stats(self.stats[:, t, :], m.x[:, t, :]))
        ch.sync()
        me, mo = self.stats[:, :, 1], self.stats[:, :, 4]
        qe, qo = self.stats[:, :, 2], self.stats[:, :, 5]
        mean, dif, sq, m2, var, rstd = (self.tmp[:, i, :] for i in (0, 1, 2, 3, 4, 6))
        tt, ts = nc.vector.tensor_tensor, nc.vector.tensor_scalar
        ch.add(tt(mean, me, mo, ALU.add))
        ch.add(tt(dif, me, mo, ALU.subtract))
        ch.link(tt(m2, qe, qo, ALU.add))
        ch.link(tt(sq, dif, dif, ALU.mult))
        ch.add(ts(mean, mean, 0.5, None, ALU.mult))
        ch.link(nc.vector.scalar_tensor_tensor(out=var, in0=sq, scalar=D / 4.0, in1=m2,
                                               op0=ALU.mult, op1=ALU.add))
        ts(var, var, 1.0 / D, LN_EPS, ALU.mult, ALU.add).then_inc(self.var, 1)
        v.wait_ge(self.std, 1)
        ch.link(nc.vector.reciprocal(rstd, self.tmp[:, 5, :]))
        for t in range(NT):
            ts(self.xn[:, t, :], m.x[:, t, :], mean[:, t:t + 1], rstd[:, t:t + 1],
               ALU.subtract, ALU.mult).then_inc(self.norm, 1)

    def scalar_root(self, a):
        a.wait_ge(self.var, 1)
        self.m.nc.scalar.activation(self.tmp[:, 5, :], self.tmp[:, 4, :], ACT.Sqrt).then_inc(self.std, 1)

    def scalar_copy(self, a):
        for q in range(NQ):
            a.wait_ge(self.turned, q + 1)
            self.m.nc.scalar.copy(self.xnT[:, q * BANK:(q + 1) * BANK],
                                  self.bank(q)).then_inc(self.ready, 1)

    def tensor(self, pe):
        for q in range(NQ):
            pe.wait_ge(self.norm, QT * (q + 1))
            if q >= 2:
                pe.wait_ge(self.ready, q - 1)
            for k in range(QT):
                last = self.m.nc.tensor.transpose(self.bank(q)[:, k * P:(k + 1) * P],
                                                  self.xn[:, QT * q + k, :], self.m.ident[:])
            last.then_inc(self.turned, 1)


E_ALL = 64
PAIRS = E_ALL // 2
HID = 64
GROUPS = 8
GE = E_ALL // GROUPS
TOP_GROUPS = 4
TOP_K = 8
ROUTE_SCALE = 2.5
SHARED = 2


def moe_ffn(m, tag, router_w, correction_bias, up_w, down_w, shared_up_w, shared_down_w, out=None):
    nc = m.nc
    with ExitStack() as stage:
        m.stage = stage

        def sb(name, shape, dt=F32):
            return m.sb(f"{tag}_{name}", shape, dt, stage)

        def sem(name):
            return m.sem(f"{tag}_{name}")

        xn, xnT = sb("xn", [P, NT, D]), sb("xnT", [D, T])
        acc = m.ps(f"{tag}_acc", [P, NQ, BANK], ctx=stage)
        hid = m.ps(f"{tag}_hid", [P, 2, BANK], ctx=stage)
        cw = m.ps(f"{tag}_cw", [P, 2, BANK], ctx=stage)
        cw16 = cw[:].bitcast(F16)
        rw = sb("rw", [E_ALL, D])
        rwT = sb("rwT", [D, E_ALL])
        cbias = sb("cbias", [P, E_ALL])
        xh, xl = sb("x_high", [D, T], F32R), sb("x_low", [D, T], F32R)
        shu = sb("shu", [D, SHARED * P])
        shu_h, shu_l = sb("shu_high", [D, SHARED * P], F32R), sb("shu_low", [D, SHARED * P], F32R)
        wu_h, wu_l = sb("wu_high", [D, 2, 2 * HID], F32R), sb("wu_low", [D, 2, 2 * HID], F32R)
        shd = sb("shd", [P, SHARED, D])
        wu = sb("wu", [D, 2, 2 * HID])
        wd = sb("wd", [2 * HID, 2, D])
        score = sb("score", [P, NT, E_ALL])
        sfc = sb("sfc", [P, NT, E_ALL])
        masked = sb("masked", [P, NT, E_ALL])
        struck = sb("struck", [P, NT, E_ALL])
        top = sb("top", [P, NT, TOP_K])
        pairA, pairB = sb("pairA", [P, NT * GROUPS, 4]), sb("pairB", [P, NT * GROUPS, 4])
        quadA, quadB = sb("quadA", [P, NT * GROUPS, 2]), sb("quadB", [P, NT * GROUPS, 2])
        quadC = sb("quadC", [P, NT * GROUPS, 2])
        gbest = sb("gbest", [P, 4, NT * GROUPS])
        gsum = sb("gsum", [P, NT, GROUPS])
        cmp1, cmp2 = sb("cmp1", [P, NT, GROUPS, GROUPS]), sb("cmp2", [P, NT, GROUPS, GROUPS])
        rank = sb("rank", [P, NT, GROUPS])
        wsum = sb("wsum", [P, 2, NT])
        chl = sb("chl", [P, NT, 2, E_ALL], F16)
        cT = sb("cT", [P, T], F16)
        relu = sb("relu", [P, 2, BANK])
        gated = sb("gated", [P, 2, BANK])
        act = sb("act", [P, 4, BANK])
        outT = sb("outT", [P, NQ, BANK])

        ln = LayerNorm(m, tag, xn, xnT, lambda q: cw[:, q % 2, :])
        small_in = sem("small_in")
        up_in = [sem("even_up_in"), sem("odd_up_in")]
        down_in = [sem("even_down_in"), sem("odd_down_in")]
        rw_turned, rw_ready = sem("rw_turned"), sem("rw_ready")
        logits_ready, score_ready = sem("logits_ready"), sem("score_ready")
        route = sem("route_order")
        ch_ready = sem("weights_ready")
        cT_turned, cT_ready = sem("cT_turned"), sem("cT_ready")
        up_done, cw_done, down_done = sem("up_done"), sem("cw_done"), sem("down_done")
        relu_ready, gate_done, act_ready = sem("relu_ready"), sem("gate_done"), sem("act_ready")
        shared_ready = sem("shared_ready")
        x_high, x_low = sem("x_high_ready"), sem("x_low_ready")
        w_high, w_low = sem("w_high_ready"), sem("w_low_ready")
        shu_high, shu_low = sem("shu_high_ready"), sem("shu_low_ready")
        outT_ready, out_turned, x_ready = sem("outT_ready"), sem("out_turned"), sem("x_ready")
        stored = sem("stored")

        NS = SHARED * NQ
        NR = PAIRS * NQ

        with nc.Block() as block:
            @block.sync
            def _(sp):
                sp.dma_start(rw[:], router_w).then_inc(small_in, 16)
                sp.dma_start(cbias[:], correction_bias.rearrange("(a e) -> a e", a=1).broadcast_to([P, E_ALL])).then_inc(small_in, 16)
                sp.dma_start(shu[:], shared_up_w).then_inc(small_in, 16)
                sp.dma_start(shd[:], shared_down_w.rearrange("(s p) d -> p s d", p=P)).then_inc(small_in, 16)

                def load_up(pair, slot):
                    sp.dma_start(wu[:, slot, :].rearrange("p (e i) -> p e i", e=2),
                                 up_w[bass.ds(2 * pair, 2), :, :].rearrange("e d i -> d e i")).then_inc(up_in[slot], 16)

                def load_down(pair, slot):
                    sp.dma_start(wd[:, slot, :],
                                 down_w[bass.ds(2 * pair, 2), :, :].rearrange("e i d -> (e i) d")).then_inc(down_in[slot], 16)
                for p in range(2):
                    load_up(p, p)
                    load_down(p, p)
                with sp.Fori(0, PAIRS // 2 - 1) as i:
                    for j in range(2):
                        sp.wait_ge(w_low, 2 * i + j + 1)
                        load_up(2 * i + 2 + j, j)
                        sp.wait_ge(down_done, NS + 8 * i + 4 * j + 4)
                        load_down(2 * i + 2 + j, j)
                if out is not None:
                    for q in range(NQ):
                        sp.wait_ge(x_ready, q + 1)
                        sp.dma_start(out[q], m.x[:, QT * q:QT * (q + 1), :]).then_inc(stored, 16)
                    sp.wait_ge(stored, 16 * NQ)

            @block.tensor
            def _(pe):
                mm = nc.tensor.matmul
                pe.wait_ge(small_in, 64)
                nc.tensor.transpose(hid[:, 0, 0:E_ALL], rw[:], m.ident[0:E_ALL, 0:E_ALL]).then_inc(rw_turned, 1)
                ln.tensor(pe)
                pe.wait_ge(rw_ready, 1)
                for t in range(NT):
                    pe.wait_ge(ln.ready, t // QT + 1)
                    last = mm(hid[:, t // 8, (t % 8) * E_ALL:(t % 8 + 1) * E_ALL],
                              xnT[:, t * P:(t + 1) * P], rwT[:], start=True, stop=True)
                last.then_inc(logits_ready, 1)

                def up(w_hi, w_lo, q, n):
                    cols = slice(q * BANK, (q + 1) * BANK)
                    mm(hid[:, n % 2, :], w_hi, xh[:, cols], start=True, stop=False)
                    mm(hid[:, n % 2, :], w_hi, xl[:, cols], start=False, stop=False)
                    mm(hid[:, n % 2, :], w_lo, xh[:, cols], start=False, stop=True).then_inc(up_done, 1)

                def down(w, q, n, start, stop):
                    mm(acc[:, q, :], w, act[:, n % 4, :], start=start, stop=stop,
                       skip_group_check=True).then_inc(down_done, 1)

                pe.wait_ge(score_ready, 1)
                pe.wait_ge(shu_low, 1)
                pe.wait_ge(x_low, NQ)
                for n in range(NS):
                    if n >= 2:
                        pe.wait_ge(relu_ready, n - 1)
                    blk = slice((n // NQ) * P, (n // NQ + 1) * P)
                    up(shu_h[:, blk], shu_l[:, blk], n % NQ, n)
                    if n >= 2:
                        k = n - 2
                        pe.wait_ge(shared_ready, k + 1)
                        down(shd[:, k // NQ, :], k % NQ, k, k < NQ, False)
                for k in range(NS - 2, NS):
                    pe.wait_ge(shared_ready, k + 1)
                    down(shd[:, k // NQ, :], k % NQ, k, False, False)
                pe.wait_ge(ch_ready, 1)
                for t in range(NT):
                    last = nc.tensor.transpose(cw16[:, t // 8, (t % 8) * P:(t % 8 + 1) * P],
                                               chl[:, t, :, :].rearrange("p a e -> p (a e)"), m.ident16[:])
                    if t % 8 == 7:
                        last.then_inc(cT_turned, 1)
                pe.wait_ge(cT_ready, 2)

                for n in range(2):
                    pe.wait_ge(relu_ready, NS + n - 1)
                    pe.wait_ge(w_low, 1)
                    up(wu_h[:, 0, :], wu_l[:, 0, :], n, n)
                    mm(cw[:, n % 2, :], m.spread[:, 0:2, :].rearrange("p e j -> p (e j)"),
                       cT[:, n * BANK:(n + 1) * BANK], start=True, stop=True).then_inc(cw_done, 1)
                with pe.Fori(0, PAIRS // 2 - 1) as i:
                    for k in range(8):
                        a = k + 2
                        if a == 4:
                            pe.wait_ge(w_low, 2 * i + 2)
                        if a == 8:
                            pe.wait_ge(w_low, 2 * i + 3)
                        pe.wait_ge(relu_ready, 8 * i + (NS + a - 1))
                        up(wu_h[:, (a // 4) % 2, :], wu_l[:, (a // 4) % 2, :], a % 4, a)
                        pe.wait_ge(gate_done, 8 * i + (a - 1))
                        mm(cw[:, a % 2, :],
                           m.spread[:, bass.ds(4 * i + 2 * (a // 4), 2), :].rearrange("p e j -> p (e j)"),
                           cT[:, (a % 4) * BANK:(a % 4 + 1) * BANK], start=True, stop=True).then_inc(cw_done, 1)
                        pe.wait_ge(act_ready, 8 * i + (k + 1))
                        if k % 4 == 0:
                            pe.wait_ge(down_in[k // 4], 16 * i + 16)
                        down(wd[:, k // 4, :], k % 4, k, False, False)
                n0 = NR - 8
                for k in range(8):
                    a = k + 2
                    if a == 4:
                        pe.wait_ge(w_low, PAIRS)
                    if a < 8:
                        pe.wait_ge(relu_ready, NS + n0 + a - 1)
                        up(wu_h[:, (a // 4) % 2, :], wu_l[:, (a // 4) % 2, :], a % 4, a)
                        pe.wait_ge(gate_done, n0 + a - 1)
                        e = E_ALL - 4 + 2 * (a // 4)
                        mm(cw[:, a % 2, :], m.spread[:, e:e + 2, :].rearrange("p e j -> p (e j)"),
                           cT[:, (a % 4) * BANK:(a % 4 + 1) * BANK], start=True, stop=True).then_inc(cw_done, 1)
                    pe.wait_ge(act_ready, n0 + k + 1)
                    if k % 4 == 0:
                        pe.wait_ge(down_in[k // 4], 8 * PAIRS)
                    down(wd[:, k // 4, :], k % 4, k, False, k >= 4)
                for q in range(NQ):
                    pe.wait_ge(outT_ready, q + 1)
                    if q >= 2:
                        pe.wait_ge(x_ready, q - 1)
                    for k in range(QT):
                        last = nc.tensor.transpose(hid[:, q % 2, k * P:(k + 1) * P],
                                                   outT[:, q, k * P:(k + 1) * P], m.ident[:])
                    last.then_inc(out_turned, 1)

            @block.scalar
            def _(a):
                ln.scalar_root(a)
                a.wait_ge(rw_turned, 1)
                nc.scalar.copy(rwT[:], hid[:, 0, 0:E_ALL]).then_inc(rw_ready, 1)
                ln.scalar_copy(a)
                a.wait_ge(small_in, 64)
                nc.scalar.copy(shu_h[:], shu[:]).then_inc(shu_high, 1)
                a.wait_ge(ln.ready, NQ)
                for q in range(NQ):
                    cols = slice(q * BANK, (q + 1) * BANK)
                    nc.scalar.copy(xh[:, cols], xnT[:, cols]).then_inc(x_high, 1)

                def split(slot, count, pairs):
                    a.wait_ge(up_in[slot], count)
                    if pairs is not None:
                        a.wait_ge(w_low, pairs)
                    nc.scalar.copy(wu_h[:, slot, :], wu[:, slot, :]).then_inc(w_high, 1)
                split(0, 16, None)
                split(1, 16, None)
                a.wait_ge(logits_ready, 1)
                nc.scalar.activation(score[:].rearrange("p t e -> p (t e)"),
                                     hid[:].rearrange("p a b -> p (a b)"), ACT.Sigmoid).then_inc(score_ready, 1)
                for n in range(NS):
                    a.wait_ge(up_done, n + 1)
                    if n >= 2:
                        a.wait_ge(shared_ready, n - 1)
                    nc.scalar.activation(relu[:, n % 2, :], hid[:, n % 2, :], ACT.Relu).then_inc(relu_ready, 1)
                    a.wait_ge(relu_ready, n + 1)
                    if n >= 4:
                        a.wait_ge(down_done, n - 3)
                    nc.scalar.activation(act[:, n % 4, :], relu[:, n % 2, :], ACT.Square).then_inc(shared_ready, 1)
                for h in range(2):
                    a.wait_ge(cT_turned, h + 1)
                    nc.scalar.copy(cT[:, h * 1024:(h + 1) * 1024], cw16[:, h, :]).then_inc(cT_ready, 1)
                a.wait_ge(shared_ready, NS)

                def eight(n, pair, count, next_split, first=False):
                    for k in range(8):
                        a.wait_ge(up_done, n + (NS + k + 1))
                        if k >= 2 or not first:
                            a.wait_ge(act_ready, n + (k - 1))
                        nc.scalar.activation(relu[:, k % 2, :], hid[:, k % 2, :], ACT.Relu).then_inc(relu_ready, 1)
                        if k == 0 and not first:
                            split(1, count, pair)
                        if k == 4 and next_split:
                            split(0, 32 if first else count + 16, pair + 1)
                eight(0, 1, 0, True, first=True)
                with a.Fori(0, PAIRS // 2 - 2) as i:
                    eight(8 * i + 8, 2 * i + 3, 16 * i + 32, True)
                eight(NR - 8, PAIRS - 1, 8 * PAIRS, False)
                for q in range(NQ):
                    a.wait_ge(down_done, NS + NR - NQ + q + 1)
                    nc.scalar.copy(outT[:, q, :], acc[:, q, :]).then_inc(outT_ready, 1)

            @block.gpsimd
            def _(pool):
                pool.wait_ge(shu_high, 1)
                nc.gpsimd.tensor_tensor(shu_l[:], shu[:], shu_h[:].bitcast(F32), ALU.subtract).then_inc(shu_low, 1)
                for q in range(NQ):
                    cols = slice(q * BANK, (q + 1) * BANK)
                    pool.wait_ge(x_high, q + 1)
                    nc.gpsimd.tensor_tensor(xl[:, cols], xnT[:, cols], xh[:, cols].bitcast(F32),
                                            ALU.subtract).then_inc(x_low, 1)

            @block.vector
            def _(v):
                ln.vector(v)
                tt, ts = nc.vector.tensor_tensor, nc.vector.tensor_scalar
                ch = Chain(v, route)
                v.wait_ge(small_in, 64)
                v.wait_ge(score_ready, 1)
                ch.link(tt(sfc[:], score[:], cbias[:].unsqueeze(1).broadcast_to([P, NT, E_ALL]), ALU.add))
                s = sfc[:].rearrange("p t (g e) -> p (t g) e", g=GROUPS)
                ch.add(tt(pairA[:], s[:, :, 0:4], s[:, :, 4:8], ALU.max))
                ch.link(tt(pairB[:], s[:, :, 0:4], s[:, :, 4:8], ALU.min))
                ch.add(tt(quadA[:], pairA[:, :, 0:2], pairA[:, :, 2:4], ALU.max))
                ch.add(tt(quadB[:], pairA[:, :, 0:2], pairA[:, :, 2:4], ALU.min))
                ch.link(tt(quadC[:], pairB[:, :, 0:2], pairB[:, :, 2:4], ALU.max))
                ch.link(tt(quadB[:], quadB[:], quadC[:], ALU.max))
                ch.add(tt(gbest[:, 0, :], quadA[:, :, 0], quadA[:, :, 1], ALU.max))
                ch.add(tt(gbest[:, 1, :], quadA[:, :, 0], quadA[:, :, 1], ALU.min))
                ch.link(tt(gbest[:, 2, :], quadB[:, :, 0], quadB[:, :, 1], ALU.max))
                ch.link(tt(gbest[:, 3, :], gbest[:, 1, :], gbest[:, 2, :], ALU.max))
                ch.link(tt(gsum[:].rearrange("p t g -> p (t g)"), gbest[:, 0, :], gbest[:, 3, :], ALU.add))
                shape = [P, NT, GROUPS, GROUPS]
                other = gsum[:].unsqueeze(2).broadcast_to(shape)
                own = gsum[:].unsqueeze(3).broadcast_to(shape)
                ch.add(tt(cmp1[:], other, own, ALU.is_gt))
                ch.link(tt(cmp2[:], other, own, ALU.is_equal))
                ch.link(tt(cmp2[:], cmp2[:], m.before8[:].unsqueeze(1).broadcast_to(shape), ALU.mult))
                ch.link(tt(cmp1[:], cmp1[:], cmp2[:], ALU.add))
                ch.link(nc.vector.tensor_reduce(rank[:], cmp1[:], AX_X, ALU.add))
                ch.link(ts(rank[:], rank[:], TOP_GROUPS - 0.5, None, ALU.is_lt))
                ch.link(tt(masked[:].rearrange("p t (g e) -> p (t g) e", g=GROUPS), s,
                           rank[:].rearrange("p t g -> p (t g)").unsqueeze(2).broadcast_to([P, NT * GROUPS, GE]),
                           ALU.mult))
                for t in range(NT):
                    ch.add(nc.vector.max(top[:, t, :], masked[:, t, :]))
                ch.sync()
                for t in range(NT):
                    ch.add(nc.vector.match_replace(struck[:, t, :], top[:, t, :], masked[:, t, :], -1e30))
                ch.sync()
                ch.link(tt(struck[:], struck[:], masked[:], ALU.not_equal))
                ch.link(tt(masked[:], score[:], struck[:], ALU.mult))
                ch.link(nc.vector.tensor_reduce(wsum[:, 0, :], masked[:], AX_X, ALU.add))
                ch.link(ts(wsum[:, 0, :], wsum[:, 0, :], 1e-20, None, ALU.add))
                ch.link(nc.vector.reciprocal(wsum[:, 1, :], wsum[:, 0, :]))
                ch.link(tt(struck[:], masked[:], wsum[:, 1, :].unsqueeze(2).broadcast_to([P, NT, E_ALL]), ALU.mult))
                ch.link(ts(masked[:], struck[:], ROUTE_SCALE, None, ALU.mult))
                ch.link(nc.vector.tensor_copy(chl[:, :, 0, :], masked[:]))
                tt(chl[:, :, 1, :], masked[:], chl[:, :, 0, :], ALU.subtract).then_inc(ch_ready, 1)

                def unit(k, relu_n, cw_n, gate_n, act_n, down_n):
                    v.wait_ge(relu_ready, relu_n)
                    v.wait_ge(cw_done, cw_n)
                    if act_n is not None:
                        v.wait_ge(act_ready, act_n)
                    tt(gated[:, k % 2, :], relu[:, k % 2, :], cw[:, k % 2, :], ALU.mult).then_inc(gate_done, 1)
                    v.wait_ge(gate_done, gate_n)
                    v.wait_ge(down_done, down_n)
                    tt(act[:, k % 4, :], gated[:, k % 2, :], relu[:, k % 2, :], ALU.mult).then_inc(act_ready, 1)

                def split(slot, pairs):
                    v.wait_ge(w_high, pairs)
                    tt(wu_l[:, slot, :], wu[:, slot, :], wu_h[:, slot, :].bitcast(F32), ALU.subtract).then_inc(w_low, 1)
                split(0, 1)
                split(1, 2)

                def eight(n, pair, next_split, first=False):
                    for k in range(8):
                        unit(k, n + (NS + k + 1), n + (k + 1), n + (k + 1),
                             n + (k - 1) if k >= 2 or not first else None, n + (NS + k - 3))
                        if k == 0 and not first:
                            split(1, pair + 1)
                        if k == 4 and next_split:
                            split(0, pair + 2)
                eight(0, 1, True, first=True)
                with v.Fori(0, PAIRS // 2 - 2) as i:
                    eight(8 * i + 8, 2 * i + 3, True)
                eight(NR - 8, PAIRS - 1, False)
                for q in range(NQ):
                    v.wait_ge(out_turned, q + 1)
                    rows = m.x[:, QT * q:QT * (q + 1), :].rearrange("p t d -> p (t d)")
                    tt(rows, hid[:, q % 2, :], rows, ALU.add).then_inc(x_ready, 1)
                v.wait_ge(x_ready, NQ)


HEADS = 16
HD = D // HEADS
KERNELS = 16
BATCH = 2
L = T // BATCH
LT = L // P
G4 = 4
ITERS = BATCH * HEADS // G4
PIECES = 3
QK_ROWS = PIECES * PIECES * HD
K_ROWS = 96
TABW = 2 * L - P
CHUNKS = 4
CW = TABW // CHUNKS
STEPS = 2 * LT
UNITS = G4 * LT * 2
UNIT_AT = 2
PER_STEP = 6
STACK_DMAS = 2 * PIECES * PIECES + 1


def step_columns(s):
    lh, mb = s // LT, LT - 1 - s % LT
    return lh * BANK - mb * P + (LT - 1) * P


def attention(m, w_in, offsets, amplitudes, sharpness):
    nc = m.nc
    with ExitStack() as stage:
        m.stage = stage

        def sb(name, shape, dt=F32, ctx=stage):
            return m.sb(f"at_{name}", shape, dt, ctx)

        def sem(name):
            return m.sem(f"at_{name}")

        kd = nc.dram_tensor("k_parts", [PIECES, D, T], BF16).ap()
        qd = nc.dram_tensor("q_parts", [PIECES, D, T], BF16).ap()
        bias_d = nc.dram_tensor("bias_rows", [3, HEADS, 2 * L], F16).ap()
        bias_rev, bias_hi, bias_lo = (bias_d[k] for k in range(3))

        s1 = m.ps("at_rows", [P, 2, BANK], ctx=stage)
        s2 = m.ps("at_cols", [P, 2, 2, BANK], ctx=stage)
        pv = m.ps("at_pv", [P, BANK], ctx=stage)
        tp = m.ps("at_tp", [P, BANK], ctx=stage)

        v_nat = sb("v_nat", [P, NT, D])
        prologue(m, sb, sem, s1, s2, pv, tp, w_in, offsets, amplitudes, sharpness,
                 kd, qd, bias_hi, bias_lo, bias_rev, v_nat)
        attend(m, sb, sem, s1, s2, pv, tp, kd, qd, bias_hi, bias_lo, bias_rev, v_nat)


def prologue(m, sb, sem, s1, s2, pv, tp, w_in, offsets, amplitudes, sharpness,
             kd, qd, bias_hi, bias_lo, bias_rev, v_nat):
    nc = m.nc
    with ExitStack() as pro:
        def psb(name, shape, dt=F32):
            return sb(name, shape, dt, pro)
        m.stage = pro
        xn, xnT = psb("xn", [P, NT, D]), psb("xnT", [D, T])
        wraw, wT = psb("wraw", [P, 3, D]), psb("wT", [D, 3, D])
        HK = HEADS * KERNELS
        C = 2 * L // P
        off, amp, shp = psb("off", [P, HK]), psb("amp", [P, HK]), psb("shp", [P, HK])
        ramp_i = psb("ramp_i", [P, C], mybir.dt.int32)
        ramp = psb("ramp", [P, C])
        dif, gau = psb("dif", [P, HK, C]), psb("gau", [P, HK, C])
        bias = psb("bias", [P, HEADS, C])
        b_hi, b_lo = (psb(n, [P, HEADS, C], F16) for n in ("b_hi", "b_lo"))
        proj = psb("proj", [P, 2, BANK])
        rest = psb("rest", [P, 2, BANK])
        parts = psb("parts", [P, 2, PIECES, BANK], BF16)

        ln = LayerNorm(m, "at", xn, xnT, lambda q: s1[:, q % 2, :])
        w_loaded, small_loaded = sem("w_loaded"), sem("small_loaded")
        w_turned, w_ready = sem("w_turned"), sem("w_ready")
        ramp_made, diff_ready, gauss_ready = sem("ramp_made"), sem("diff_ready"), sem("gauss_ready")
        order = sem("bias_order")
        bias_ready, parts_made = sem("bias_ready"), sem("bias_parts")
        bias_out = sem("bias_out")
        proj_done, proj_copied = sem("proj_done"), sem("proj_copied")
        split = sem("split_order")
        parts_ready = sem("parts_ready")
        stored = [sem("parts_out_even"), sem("parts_out_odd")]
        v_done, v_copied = sem("v_done"), sem("v_copied")
        KINDS = 2 * NQ

        with nc.Block() as block:
            @block.sync
            def _(sp):
                sp.dma_start(wraw[:], w_in.rearrange("(a e) d -> e a d", a=3)).then_inc(w_loaded, 16)
                for t, src in ((off, offsets), (amp, amplitudes), (shp, sharpness)):
                    sp.dma_start(t[:], src.rearrange("(a h) k -> a (h k)", a=1).broadcast_to([P, HK])
                                 ).then_inc(small_loaded, 16)
                for n in range(KINDS):
                    sp.wait_ge(parts_ready, n + 1)
                    dst = (kd, qd)[n % 2]
                    q = n // 2
                    sp.dma_start(dst[:, :, q * BANK:(q + 1) * BANK].rearrange("a e c -> e a c"),
                                 parts[:, n % 2, :, :]).then_inc(stored[n % 2], 16)
                sp.wait_ge(parts_made, 2)
                for t, dst in ((b_hi, bias_hi), (b_lo, bias_lo)):
                    sp.dma_start(dst.rearrange("h (p c) -> p h c", p=P), t[:]).then_inc(bias_out, 16)
                sp.wait_ge(bias_out, 32)
                for s in stored:
                    sp.wait_ge(s, 16 * NQ)

            @block.gpsimd
            def _(pool):
                nc.gpsimd.iota(ramp_i[:], [[1, C]], base=1 - L, channel_multiplier=C).then_inc(ramp_made, 1)
                pool.wait_ge(ramp_made, 1)
                nc.gpsimd.tensor_copy(ramp[:], ramp_i[:]).then_inc(ramp_made, 1)
                pool.wait_ge(ramp_made, 2)

            @block.tensor
            def _(pe):
                mm = nc.tensor.matmul
                pe.wait_ge(w_loaded, 16)
                for a in range(3):
                    last = nc.tensor.transpose(tp[:, a * P:(a + 1) * P], wraw[:, a, :], m.ident[:])
                last.then_inc(w_turned, 1)
                ln.tensor(pe)
                pe.wait_ge(w_ready, 1)
                for n in range(KINDS):
                    q = n // 2
                    pe.wait_ge(ln.ready, q + 1)
                    if n >= 4:
                        pe.wait_ge(proj_copied, n - 3)
                    mm(s2[:, (n % 4) // 2, n % 2, :], wT[:, (0, 2)[n % 2], :],
                       xnT[:, q * BANK:(q + 1) * BANK], start=True, stop=True).then_inc(proj_done, 1)
                for g in range(NQ):
                    if g >= 2:
                        pe.wait_ge(v_copied, g - 1)
                    for k in range(QT):
                        t = g * QT + k
                        last = mm(s1[:, g % 2, k * P:(k + 1) * P], xnT[:, t * P:(t + 1) * P], wT[:, 1, :],
                                  start=True, stop=True)
                    last.then_inc(v_done, 1)

            @block.scalar
            def _(a):
                ln.scalar_root(a)
                a.wait_ge(w_turned, 1)
                nc.scalar.copy(wT[:].rearrange("p a d -> p (a d)"), tp[:, 0:3 * D]).then_inc(w_ready, 1)
                ln.scalar_copy(a)
                scales = (1.0, 1.0 / math.sqrt(HD))
                for n in range(KINDS):
                    a.wait_ge(proj_done, n + 1)
                    if n >= 2:
                        a.wait_ge(parts_ready, n - 1)
                    nc.scalar.mul(proj[:, n % 2, :], s2[:, (n % 4) // 2, n % 2, :],
                                  scales[n % 2]).then_inc(proj_copied, 1)
                for g in range(NQ):
                    a.wait_ge(v_done, g + 1)
                    nc.scalar.copy(v_nat[:, g * QT:(g + 1) * QT, :].rearrange("p t d -> p (t d)"),
                                   s1[:, g % 2, :]).then_inc(v_copied, 1)
                a.wait_ge(diff_ready, 1)
                nc.scalar.activation(gau[:], dif[:], ACT.Exp).then_inc(gauss_ready, 1)

            @block.vector
            def _(v):
                tt, ts = nc.vector.tensor_tensor, nc.vector.tensor_scalar
                ln.vector(v)
                ch = Chain(v, split)
                for n in range(KINDS):
                    b = n % 2
                    v.wait_ge(proj_copied, n + 1)
                    if n >= 2:
                        v.wait_ge(stored[b], 16 * (n // 2))
                    ch.link(nc.vector.tensor_copy(parts[:, b, 0, :], proj[:, b, :]))
                    ch.link(tt(rest[:, 0, :], proj[:, b, :], parts[:, b, 0, :], ALU.subtract))
                    ch.link(nc.vector.tensor_copy(parts[:, b, 1, :], rest[:, 0, :]))
                    ch.link(tt(rest[:, 1, :], rest[:, 0, :], parts[:, b, 1, :], ALU.subtract))
                    nc.vector.tensor_copy(parts[:, b, 2, :], rest[:, 1, :]).then_inc(parts_ready, 1)
                    v.wait_ge(parts_ready, n + 1)
                v.wait_ge(small_loaded, 48)
                v.wait_ge(ramp_made, 2)
                ch = Chain(v, order)
                shape = [P, HK, C]

                def wide(t):
                    return t[:].unsqueeze(2).broadcast_to(shape)
                ch.add(tt(dif[:], wide(off), ramp[:].unsqueeze(1).broadcast_to(shape), ALU.subtract))
                ch.link(nc.vector.scalar_tensor_tensor(out=shp[:], in0=shp[:], scalar=-1.0, in1=shp[:],
                                                       op0=ALU.mult, op1=ALU.min))
                ch.link(tt(gau[:], dif[:], wide(shp), ALU.mult))
                tt(dif[:], gau[:], dif[:], ALU.mult).then_inc(diff_ready, 1)
                v.wait_ge(gauss_ready, 1)
                ch.link(tt(dif[:], gau[:], wide(amp), ALU.mult))
                nc.vector.tensor_reduce(bias[:], dif[:].rearrange("p (h k) c -> p h c k", h=HEADS),
                                        AX_X, ALU.add).then_inc(bias_ready, 1)
                v.wait_ge(bias_ready, 1)
                nc.vector.tensor_copy(b_hi[:], bias[:]).then_inc(parts_made, 1)
                v.wait_ge(parts_made, 1)
                tt(b_lo[:], bias[:], b_hi[:], ALU.subtract).then_inc(parts_made, 1)
                v.wait_ge(parts_made, 2)


def attend(m, sb, sem, s1, s2, pv, tp, kd, qd, bias_hi, bias_lo, bias_rev, v_nat):
    nc = m.nc
    q_st = sb("q_stack", [K_ROWS, 2, G4, L], BF16)
    k_st = sb("k_stack", [K_ROWS, 2, G4, L], BF16)
    t_hi, t_lo = sb("table_hi", [P, G4, TABW], F16), sb("table_lo", [P, G4, TABW], F16)
    t_max = sb("table_max", [P, G4, TABW], F16)
    prob = sb("prob", [P, 2, G4, BANK])
    vst = sb("v_stack", [P, 2, LT, G4, 32])
    zrow = sb("zero_rows", [K_ROWS, P], BF16)
    mx = sb("maxima", [P, G4 * LT, 2])
    mtop = sb("mtop", [P, 3, G4 * LT])
    negm = sb("negm", [P, PIECES, G4 * LT], BF16)
    negT = sb("negT", [PIECES * G4 * LT, P], BF16)
    oT = sb("oT", [P, BANK])
    rden = sb("rden", [P, QT, G4])
    onorm = sb("onorm", [P, QT, G4, HD])
    tpb = tp[:].bitcast(BF16)

    preset = sem("preset")
    stack_in = [sem("stack_in_even"), sem("stack_in_odd")]
    zero_in = sem("zero_in")
    max_tab_in = [sem(f"max_tab_in{h}") for h in range(G4)]
    tab_in = [sem(f"tab_in{c}") for c in range(CHUNKS)]
    rows_ready, max_done = sem("rows_ready"), sem("max_done")
    m_order, negm_ready, neg_turned, neg_copied = sem("m_order"), sem("negm_ready"), sem("neg_turned"), sem("neg_copied")
    max_in = [sem("max_in_even"), sem("max_in_odd")]
    cols_ready, exp_done, pv_done = sem("cols_ready"), sem("exp_done"), sem("pv_done")
    oT_ready, o_turned, o_read, x_added = sem("oT_ready"), sem("o_turned"), sem("o_read"), sem("x_added")
    o_order = sem("o_order")
    v_ready = sem("v_ready")

    unit_steps = [range(max(0, (s - UNIT_AT) * PER_STEP), min(UNITS, (s - UNIT_AT + 1) * PER_STEP))
                  if s >= UNIT_AT else range(0) for s in range(STEPS)]
    M_STEP = STEPS - 2
    O_STEP = (10, 2)

    def reads(s, c):
        a = step_columns(s)
        return a < (c + 1) * CW and a + BANK > c * CW
    last_read = [max(s for s in range(STEPS) if reads(s, c)) for c in range(CHUNKS)]
    first_read = [min(s for s in range(STEPS) if reads(s, c)) for c in range(CHUNKS)]

    def toeplitz(row, g4, h0, nh, c0, n, shift):
        a = row[bass.ds(g4 + h0, nh), c0 + shift:c0 + shift + n]
        return bass.AP(tensor=a.tensor, offset=a.offset, ap=[[1, P], [2 * L, nh], [1, n]])

    def load_max_table(sp, g4, h):
        sp.dma_start(t_max[:, h:h + 1, :], toeplitz(bias_hi, g4, h, 1, 0, TABW, 0)).then_inc(max_tab_in[h], 16)

    def load_table(sp, g4, c):
        for t, row in ((t_hi, bias_hi), (t_lo, bias_lo)):
            sp.dma_start(t[:, :, c * CW:(c + 1) * CW], toeplitz(row, g4, 0, G4, c * CW, CW, 0)).then_inc(tab_in[c], 16)

    def load_stack(sp, g4, b):
        cols = slice(b * L, (b + 1) * L)
        for a in range(PIECES):
            for c in range(PIECES):
                r = (a * PIECES + c) * HD
                for st, dram, part in ((q_st, qd, a), (k_st, kd, c)):
                    src = dram[part, bass.ds(g4 * HD, G4 * HD), cols]
                    sp.dma_start(st[r:r + HD, b, :, :],
                                 src.rearrange("(h d) l -> d h l", h=G4)).then_inc(stack_in[b], 16)
        sp.dma_start(q_st[QK_ROWS:QK_ROWS + PIECES, b, :, :].rearrange("p h (t l) -> p (h t) l", l=P),
                     zrow[:]).then_inc(stack_in[b], 16)

    with nc.Block() as block:
        @block.sync
        def _(sp):
            sp.wait_ge(preset, 6)
            load_stack(sp, 0, 0)
            for h in range(G4):
                load_max_table(sp, 0, h)
            for c in range(CHUNKS):
                load_table(sp, 0, c)
            load_stack(sp, 0, 1)
            with sp.Fori(0, ITERS // 2 - 1) as i:
                for h in range(G4):
                    sp.wait_ge(max_done, 2 * UNITS * i + (UNITS + (h + 1) * UNITS // G4))
                    load_max_table(sp, G4 * i + G4, h)
                sp.wait_ge(cols_ready, 2 * 2 * STEPS * i + 2 * STEPS)
                load_stack(sp, G4 * i + G4, 0)
                for c in range(CHUNKS):
                    sp.wait_ge(cols_ready, 2 * 2 * STEPS * i + (2 * STEPS + 2 * last_read[c] + 2))
                    load_table(sp, G4 * i + G4, c)
                sp.wait_ge(cols_ready, 2 * 2 * STEPS * i + 4 * STEPS)
                load_stack(sp, G4 * i + G4, 1)

        @block.gpsimd
        def _(pool):
            fills = [(q_st[64:K_ROWS], 0.0), (k_st[64:K_ROWS], 1.0), (zrow[:], 0.0),
                     (vst[:, :, :, :, 0:HD], 0.0), (vst[:, :, :, :, HD:HD + 1], 1.0),
                     (vst[:, :, :, :, HD + 1:32], 0.0)]
            for n, (t, value) in enumerate(fills):
                nc.gpsimd.memset(t, value).then_inc(preset, 1)
                pool.wait_ge(preset, n + 1)


            def take_v(b, c0):
                nc.gpsimd.tensor_copy(
                    vst[:, b, :, :, 0:HD],
                    v_nat[:, b * LT:(b + 1) * LT, bass.ds(c0, G4 * HD)].rearrange("p t (h d) -> p t h d", h=G4)
                ).then_inc(v_ready, 1)
            take_v(0, 0)
            take_v(1, 0)
            with pool.Fori(0, ITERS // 2 - 1) as i:
                for b in range(2):
                    pool.wait_ge(pv_done, 2 * STEPS * i + (b + 1) * STEPS)
                    take_v(b, G4 * HD * i + G4 * HD)

        def pe_unit(pe, k, it, b, g_count):
            h, lb, mh = k // (2 * LT), k // 2 % LT, k % 2
            if k == 0:
                pe.wait_ge(stack_in[b], 16 * STACK_DMAS * g_count)
            first = isinstance(it, int) and it == 0
            if not (first and k < 2):
                pe.wait_ge(max_done, UNITS * it + (k - 1))
            nc.tensor.matmul(s1[:, k % 2, :], q_st[:, b, h, lb * P:(lb + 1) * P],
                             k_st[:, b, h, mh * BANK:(mh + 1) * BANK], start=True, stop=True).then_inc(rows_ready, 1)

        def pe_turn_max(pe, it):
            pe.wait_ge(negm_ready, it + 1)
            if not (isinstance(it, int) and it == 0):
                pe.wait_ge(o_read, 2 * it - 1)
            nc.tensor.transpose(tpb[0:PIECES * G4 * LT, 0:P], negm[:].rearrange("p a n -> p (a n)"),
                                m.identb[:]).then_inc(neg_turned, 1)

        def pe_cols(pe, s, h, it, b, g_count):
            n = STEPS * it + s
            hp, j = h // 2, h % 2
            first = isinstance(it, int) and it == 0 and s == 0
            if s == 0 and h == 0:
                pe.wait_ge(max_in[b], 16 * g_count)
            if b == 0 and h == 0:
                for c in range(CHUNKS):
                    if first_read[c] == s:
                        pe.wait_ge(tab_in[c], 32 * g_count)
            if not first and j == 0:
                pe.wait_ge(exp_done, 2 * n + (hp - 1))
            lh, mb = s // LT, LT - 1 - s % LT
            c = step_columns(s)
            out = s2[:, hp, j, :]
            nc.tensor.matmul(out, k_st[:, b, h, mb * P:(mb + 1) * P],
                             q_st[:, b, h, lh * BANK:(lh + 1) * BANK], start=True, stop=False)
            nc.tensor.matmul(out, m.flip16[:], t_hi[:, h, c:c + BANK], start=False, stop=False)
            last = nc.tensor.matmul(out, m.flip16[:], t_lo[:, h, c:c + BANK], start=False, stop=True)
            if j == 1:
                last.then_inc(cols_ready, 1)

        def pe_pv(pe, s, it, b):
            n = STEPS * it + s
            mb = LT - 1 - s % LT
            pe.wait_ge(exp_done, 2 * n + 2)
            if s == 0:
                pe.wait_ge(v_ready, it + 1)
            if s % LT == 0 and not (isinstance(it, int) and it == 0 and s == 0):
                pe.wait_ge(oT_ready, 2 * it + s // LT)
            for h in range(G4):
                last = nc.tensor.matmul(pv[32 * h:32 * h + 32, :], vst[:, b, mb, h, :], prob[:, s % 2, h, :],
                                        start=(s % LT == 0), stop=(s % LT == LT - 1))
            last.then_inc(pv_done, 1)

        def pe_out(pe, k, wait_neg):
            pe.wait_ge(oT_ready, k + 1)
            if wait_neg is not None:
                pe.wait_ge(neg_copied, wait_neg)
            if not (isinstance(k, int) and k == 0):
                pe.wait_ge(o_read, k)
            for t in range(QT):
                last = nc.tensor.transpose(tp[:, t * P:(t + 1) * P], oT[:, t * P:(t + 1) * P], m.ident[:])
            last.then_inc(o_turned, 1)

        def pe_iteration(pe, it, b, g_count, nxt_count, first=False, final=False):
            for s in range(STEPS):
                units = [] if final else list(unit_steps[s])
                if s == M_STEP and not final:
                    pe_turn_max(pe, it + 1)
                def unit(n):
                    if n < len(units):
                        pe_unit(pe, units[n], it + 1, 1 - b, nxt_count)
                for h in range(G4):
                    if h == 2:
                        if s > 0:
                            pe_pv(pe, s - 1, it, b)
                        elif not first:
                            pe_pv(pe, STEPS - 1, it - 1, 1 - b)
                        unit(2)
                    pe_cols(pe, s, h, it, b, g_count)
                    unit((0, 1, 3, 4)[h])
                unit(5)
                if s == O_STEP[0]:
                    pe_out(pe, 2 * it, None)
                if s == O_STEP[1] and not first:
                    pe_out(pe, 2 * it - 1, it + 1)

        @block.tensor
        def _(pe):
            for k in range(UNITS):
                pe_unit(pe, k, 0, 0, 1)
            pe_turn_max(pe, 0)
            pe_iteration(pe, 0, 0, 1, 1, first=True)
            with pe.Fori(0, ITERS // 2 - 1) as i:
                pe_iteration(pe, 2 * i + 1, 1, i + 1, i + 2)
                pe_iteration(pe, 2 * i + 2, 0, i + 2, i + 2)
            pe_iteration(pe, ITERS - 1, 1, ITERS // 2, None, final=True)
            pe_pv(pe, STEPS - 1, ITERS - 1, 1)
            pe_out(pe, 2 * ITERS - 1, None)

        def act_negT(a, it, b):
            a.wait_ge(neg_turned, it + 1)
            if not (isinstance(it, int) and it < 1):
                a.wait_ge(max_in[1 - b], 16 * it_half(it, 1 - b))
            nc.scalar.copy(negT[:], tpb[0:PIECES * G4 * LT, 0:P]).then_inc(neg_copied, 1)
            a.wait_ge(neg_copied, it + 1)
            a.dma_start(q_st[QK_ROWS:QK_ROWS + PIECES, b, :, :].rearrange("p h (t l) -> p (h t) l", l=P),
                        negT[:]).then_inc(max_in[b], 16)

        def it_half(it, other):
            return halves[0]
        halves = [None]

        def act_iteration(a, it, b, other_count, first=False, final=False):
            for s in range(STEPS):
                n = STEPS * it + s
                if s == M_STEP and not final:
                    halves[0] = other_count
                    act_negT(a, it + 1, 1 - b)
                for hp in range(2):
                    a.wait_ge(cols_ready, 2 * n + (hp + 1))
                    if not (first and s < 2):
                        a.wait_ge(pv_done, n - 1)
                    nc.scalar.activation(prob[:, s % 2, 2 * hp:2 * hp + 2, :], s2[:, hp, :, :],
                                         ACT.Exp).then_inc(exp_done, 1)
                if s == LT:
                    act_oT(a, 2 * it, STEPS * it + LT)
                if s == 0 and not first:
                    act_oT(a, 2 * it - 1, STEPS * it)

        def act_oT(a, k, products):
            a.wait_ge(pv_done, products)
            if not (isinstance(k, int) and k == 0):
                a.wait_ge(o_turned, k)
            nc.scalar.copy(oT[:], pv[:]).then_inc(oT_ready, 1)

        @block.scalar
        def _(a):
            a.wait_ge(neg_turned, 1)
            nc.scalar.copy(negT[:], tpb[0:PIECES * G4 * LT, 0:P]).then_inc(neg_copied, 1)
            a.wait_ge(neg_copied, 1)
            a.dma_start(q_st[QK_ROWS:QK_ROWS + PIECES, 0, :, :].rearrange("p h (t l) -> p (h t) l", l=P),
                        negT[:]).then_inc(max_in[0], 16)
            act_iteration(a, 0, 0, 1, first=True)
            with a.Fori(0, ITERS // 2 - 1) as i:
                act_iteration(a, 2 * i + 1, 1, i + 1)
                act_iteration(a, 2 * i + 2, 0, i + 2)
            act_iteration(a, ITERS - 1, 1, None, final=True)
            act_oT(a, 2 * ITERS - 1, STEPS * ITERS)

        def dve_unit(v, k, it, g_count):
            h, lb, mh = k // (2 * LT), k // 2 % LT, k % 2
            if k % (2 * LT) == 0 and g_count is not None:
                v.wait_ge(max_tab_in[h], 16 * g_count)
            if isinstance(it, int):
                v.wait_ge(rows_ready, UNITS * it + (k + 1))
            else:
                v.wait_ge(rows_ready, next_rows)
                v.reg_add(next_rows, next_rows, 1)
            c = lb * P - mh * BANK + L - BANK
            nc.vector.tensor_tensor_reduce(out=s1[:, k % 2, :], in0=s1[:, k % 2, :],
                                           in1=t_max[:, h, c:c + BANK][:, ::-1], scale=1.0, scalar=-3.0e38,
                                           op0=ALU.add, op1=ALU.max,
                                           accum_out=mx[:, k // 2, k % 2:k % 2 + 1]).then_inc(max_done, 1)

        M_OPS = 6

        def dve_negm(v, it):
            tt, stt = nc.vector.tensor_tensor, nc.vector.scalar_tensor_tensor
            v.wait_ge(max_done, UNITS * it + UNITS)
            ch = Chain(v, m_order, (M_OPS - 1) * it)
            if not (isinstance(it, int) and it == 0):
                v.wait_ge(neg_turned, it)
            ch.link(nc.vector.tensor_reduce(mtop[:, 0, :], mx[:], AX_X, ALU.max))
            ch.link(nc.vector.tensor_scalar(negm[:, 0, :], mtop[:, 0, :], -1.0, None, ALU.mult))
            ch.link(stt(out=mtop[:, 1, :], in0=mtop[:, 0, :], scalar=-1.0, in1=negm[:, 0, :],
                        op0=ALU.mult, op1=ALU.subtract))
            ch.link(nc.vector.tensor_copy(negm[:, 1, :], mtop[:, 1, :]))
            ch.link(tt(mtop[:, 2, :], mtop[:, 1, :], negm[:, 1, :], ALU.subtract))
            nc.vector.tensor_copy(negm[:, 2, :], mtop[:, 2, :]).then_inc(negm_ready, 1)

        def dve_out(v, k, b, lh, c0):
            t4 = tp[:].rearrange("p (t h e) -> p t h e", t=QT, h=G4)
            v.wait_ge(o_turned, k + 1)
            if not (isinstance(k, int) and k == 0):
                v.wait_ge(x_added, k)
            nc.vector.reciprocal(rden[:], t4[:, :, :, HD]).then_inc(o_order, 1)
            v.wait_ge(o_order, k + 1)
            nc.vector.tensor_tensor(onorm[:], t4[:, :, :, 0:HD],
                                    rden[:].unsqueeze(3).broadcast_to([P, QT, G4, HD]), ALU.mult).then_inc(o_read, 1)
            v.wait_ge(o_read, k + 1)
            rows = m.x[:, b * LT + lh * QT:b * LT + (lh + 1) * QT, bass.ds(c0, G4 * HD)]
            nc.vector.tensor_tensor(rows, rows, onorm[:].rearrange("p t h e -> p t (h e)"),
                                    ALU.add).then_inc(x_added, 1)

        def dve_iteration(v, it, b, c0, prev_c0, nxt_count, first=False, final=False):
            for s in range(STEPS):
                if s == O_STEP[1] + 1 and not first:
                    dve_out(v, 2 * it - 1, 1 - b, 1, prev_c0)
                if s == O_STEP[0] + 1:
                    dve_out(v, 2 * it, b, 0, c0)
                if not final:
                    for k in unit_steps[s]:
                        dve_unit(v, k, it + 1, nxt_count)
                    if len(unit_steps[s]) and unit_steps[s][-1] == UNITS - 1:
                        dve_negm(v, it + 1)

        next_rows = nc.vector.alloc_register("next_rows")

        @block.vector
        def _(v):
            for k in range(UNITS):
                dve_unit(v, k, 0, 1)
            dve_negm(v, 0)
            W = G4 * HD
            dve_iteration(v, 0, 0, 0, None, None, first=True)
            v.reg_mov(next_rows, 2 * UNITS + 1)
            with v.Fori(0, ITERS // 2 - 1) as i:
                dve_iteration(v, 2 * i + 1, 1, W * i, W * i, i + 2)
                dve_iteration(v, 2 * i + 2, 0, W * i + W, W * i, None)
            dve_iteration(v, ITERS - 1, 1, W * (ITERS // 2 - 1), W * (ITERS // 2 - 1), None, final=True)
            dve_out(v, 2 * ITERS - 1, 1, 1, W * (ITERS // 2 - 1))
            v.wait_ge(x_added, 2 * ITERS)


INNER = 256
STATE = 128
SH = 4
SP_ = INNER // SH
CONV = 4
CB = (INNER + 2 * STATE) // P
SEQS = 2
SEQ = T // SEQS
CHUNKS_ = SEQ // P
RMS_EPS = 1e-5
DECAY_FLOOR = -1e5


def mamba(m, W_in, conv_w, conv_b, dt_bias, A_log, Dskip, norm_w, W_out):
    nc = m.nc
    with ExitStack() as stage:
        m.stage = stage

        def sb(name, shape, dt=F32):
            return m.sb(f"ss_{name}", shape, dt, stage)

        def sem(name):
            return m.sem(f"ss_{name}")

        ZD = INNER + SH
        xn, xnT = sb("xn", [P, NT, D]), sb("xnT", [D, T])
        wzd, wx = sb("wzd", [D, ZD]), sb("wx", [D, CB, P])
        NV = CONV * CB + CB + 2
        rows, cols = sb("rows", [NV, P]), sb("cols", [P, NV])
        tap = cols[:, 0:CONV * CB].rearrange("p (k b) -> p k b", k=CONV)
        cbias, normw = cols[:, CONV * CB:CONV * CB + CB], cols[:, CONV * CB + CB:NV]
        wout = sb("wout", [P, 2, D])
        dtb, alog, dsk = sb("dtb", [P, SH]), sb("alog", [P, SH]), sb("dsk", [P, SH])
        raw = sb("raw", [P, CB, SEQS, SEQ + CONV - 1])
        xc = sb("xc", [P, CB, SEQS, SEQ])
        sz = sb("sz", [P, NT, INNER])
        dtr = sb("dtr", [P, NT, SH])
        sp_ = sb("softplus", [P, 8, NT, SH])
        dt, dec = sb("dt", [P, NT, SH]), sb("dec", [P, NT, SH])
        expo = sb("expo", [P, 3, NT, SH])
        xch = sb("chunk", [P, 2, CB, P])
        R = sb("R", [P, 2, SH, P])
        E = sb("E", [P, 2, SH, P])
        Gm, M = sb("Gm", [P, 2, P]), sb("M", [P, 2, SH, P])
        btok = sb("btok", [P, 2, P])
        dtx, wxx, dx = (sb(n, [P, 2, SH, SP_]) for n in ("dtx", "wxx", "dx"))
        y1, y2, y3 = (sb(n, [P, 2, SH, SP_]) for n in ("y1", "y2", "y3"))
        H, Ht = sb("H", [P, 2, SH, SP_]), sb("Ht", [P, 2, SH, SP_])
        yg = sb("yg", [P, NT, INNER])
        junk = sb("squares", [P, INNER])
        ssq = sb("ssq", [P, NT])
        rms = sb("rms", [P, 3, NT])
        ygT = sb("ygT", [P, 2, 2, 2, P])
        ps = m.ps("ss_ps", [P, 8, BANK], ctx=stage)

        ln = LayerNorm(m, "ss", xn, xnT, lambda q: ps[:, q % 2, :])
        w_loaded, v_loaded = sem("w_loaded"), sem("v_loaded")
        cols_turned, cols_ready = sem("cols_turned"), sem("cols_ready")
        zd_done, zd_read = sem("zd_done"), sem("zd_read")
        conv_done, conv_read, raw_ready = sem("conv_done"), sem("conv_read"), sem("raw_ready")
        padded = sem("padded")
        conv_order, conv_ready, silu_ready = sem("conv_order"), sem("conv_ready"), sem("silu_ready")
        dt_order, abs_ready, u_ready, aexp_ready = sem("dt_order"), sem("abs_ready"), sem("u_ready"), sem("aexp_ready")
        dec_ready, sums_done, expo_ready = sem("dec_ready"), sem("sums_done"), sem("expo_ready")
        h_zeroed, xs_ready = sem("h_zeroed"), sem("xs_ready")
        chunk_ready, R_ready = sem("chunk_ready"), sem("R_ready")
        tok_done, gt_done, seg_done = sem("tok_done"), sem("gt_done"), sem("seg_done")
        inter_done, intra_done, dh_done = sem("inter_done"), sem("intra_done"), sem("dh_done")
        E_ready, gm_ready, M_ready = sem("E_ready"), sem("gm_ready"), sem("M_ready")
        btok_ready, dtx_ready, dx_ready, wxx_ready = sem("btok_ready"), sem("dtx_ready"), sem("dx_ready"), sem("wxx_ready")
        y1_ready, y2_ready, y3_ready, yg_ready = sem("y1_ready"), sem("y2_ready"), sem("y3_ready"), sem("yg_ready")
        ht_ready, H_ready = sem("ht_ready"), sem("H_ready")
        ssq_ready, ms_ready, root_ready, rms_ready = sem("ssq_ready"), sem("ms_ready"), sem("root_ready"), sem("rms_ready")
        wout_ready = sem("wout_ready")
        yT_done, yT_ready, out_done, x_ready = sem("yT_done"), sem("yT_ready"), sem("out_done"), sem("x_ready")
        NU = NQ * CB
        NC = CHUNKS_ * SEQS

        with nc.Block() as block:
            @block.sync
            def _(sp):
                sp.dma_start(rows[0:CONV * CB, :], conv_w.rearrange("k (b c) -> (k b) c", c=P)).then_inc(v_loaded, 16)
                sp.dma_start(rows[CONV * CB:CONV * CB + CB, :], conv_b.rearrange("(b c) -> b c", c=P)).then_inc(v_loaded, 16)
                sp.dma_start(rows[CONV * CB + CB:NV, :], norm_w.rearrange("(b c) -> b c", c=P)).then_inc(v_loaded, 16)
                for t, src in ((dtb, dt_bias), (alog, A_log), (dsk, Dskip)):
                    sp.dma_start(t[:], src.rearrange("(a h) -> a h", a=1).broadcast_to([P, SH])).then_inc(v_loaded, 16)
                XB = INNER + CB * P
                sp.dma_start(wzd[:, 0:INNER], W_in[:, 0:INNER]).then_inc(w_loaded, 16)
                sp.dma_start(wzd[:, INNER:ZD], W_in[:, XB:XB + SH]).then_inc(w_loaded, 16)
                sp.dma_start(wx[:], W_in[:, INNER:XB].rearrange("d (b c) -> d b c", c=P)).then_inc(w_loaded, 16)
                sp.dma_start(wout[:], W_out.rearrange("(b c) d -> c b d", c=P)).then_inc(w_loaded, 16)
                sp.wait_ge(w_loaded, 64)

            @block.tensor
            def _(pe):
                mm = nc.tensor.matmul
                pe.wait_ge(v_loaded, 96)
                nc.tensor.transpose(ps[:, 7, 0:NV], rows[:], m.ident[0:NV, 0:NV]).then_inc(cols_turned, 1)
                ln.tensor(pe)
                pe.wait_ge(w_loaded, 64)
                for n in range(NU):
                    q, blk = n // CB, n % CB
                    if blk == 0:
                        pe.wait_ge(ln.ready, q + 1)
                    if n >= 2:
                        pe.wait_ge(conv_read, n - 1)
                    mm(ps[:, 2 + n % 2, :], wx[:, blk, :], xnT[:, q * BANK:(q + 1) * BANK],
                       start=True, stop=True).then_inc(conv_done, 1)
                    if n >= 2:
                        pe.wait_ge(zd_read, n - 1)
                    mm(ps[:, 4 + n % 2, 0:ZD], xnT[:, n * P:(n + 1) * P], wzd[:],
                       start=True, stop=True).then_inc(zd_done, 1)
                pe.wait_ge(dec_ready, 1)
                for k, mask in enumerate((m.upto, m.after, m.ones)):
                    last = mm(ps[:, 6, k * NT * SH:(k + 1) * NT * SH], mask[:],
                              dec[:].rearrange("p t h -> p (t h)"), start=True, stop=True)
                last.then_inc(sums_done, 1)
                pe.wait_ge(expo_ready, 1)

                with pe.Fori(0, CHUNKS_) as i:
                    for b in range(SEQS):
                        n = SEQS * i
                        pb = 4 * b
                        pe.wait_ge(chunk_ready, n + (b + 1))
                        for k in range(3):
                            last = nc.tensor.transpose(ps[:, pb + 1, k * P:(k + 1) * P], xch[:, b, k, :], m.ident[:])
                        last.then_inc(tok_done, 1)
                        pe.wait_ge(H_ready, n + (b + 1))
                        mm(ps[:, pb + 2, 0:P], xch[:, b, 2, :], xch[:, b, 3, :], start=True, stop=True).then_inc(gt_done, 1)
                        pe.wait_ge(R_ready, n + (b + 1))
                        mm(ps[:, pb, :], m.after[:], R[:, b, :, :].rearrange("p h i -> p (h i)"),
                           start=True, stop=True).then_inc(seg_done, 1)
                    for b in range(SEQS):
                        n = SEQS * i
                        pb = 4 * b
                        pe.wait_ge(gm_ready, n + (b + 1))
                        mm(ps[:, pb + 2, P:P + INNER], xch[:, b, 3, :], H[:, b, :, :].rearrange("p h c -> p (h c)"),
                           start=True, stop=True).then_inc(inter_done, 1)
                        pe.wait_ge(M_ready, n + (b + 1))
                        pe.wait_ge(dtx_ready, n + (b + 1))
                        for h in range(SH):
                            a = h // 2
                            last = mm(ps[:, pb + 3, h * P:(h + 1) * P], M[:, b, h, :],
                                      dtx[:, b, 2 * a:2 * a + 2, :].rearrange("p h c -> p (h c)"), start=True, stop=True)
                        last.then_inc(intra_done, 1)
                        pe.wait_ge(wxx_ready, n + (b + 1))
                        pe.wait_ge(btok_ready, n + (b + 1))
                        mm(ps[:, pb, 0:INNER], btok[:, b, :], wxx[:, b, :, :].rearrange("p h c -> p (h c)"),
                           start=True, stop=True).then_inc(dh_done, 1)
                pe.wait_ge(yg_ready, NC)
                pe.wait_ge(y2_ready, 2 * NC)
                pe.wait_ge(wout_ready, 2)
                for g in range(NT // 2 + 1):
                    if g < NT // 2:
                        if g >= 2:
                            pe.wait_ge(yT_ready, g - 1)
                        for j in range(2):
                            for c in range(2):
                                last = nc.tensor.transpose(ps[:, g % 2, (2 * j + c) * P:(2 * j + c + 1) * P],
                                                           yg[:, 2 * g + j, c * P:(c + 1) * P], m.ident[:])
                        last.then_inc(yT_done, 1)
                    if g >= 1:
                        f = g - 1
                        pe.wait_ge(yT_ready, f + 1)
                        if f >= 2:
                            pe.wait_ge(x_ready, 2 * f - 2)
                        for j in range(2):
                            for c in range(2):
                                last = mm(ps[:, 2 + f % 2, j * P:(j + 1) * P], ygT[:, f % 2, j, c, :], wout[:, c, :],
                                          start=(c == 0), stop=(c == 1))
                        last.then_inc(out_done, 1)

            @block.scalar
            def _(a):
                act = nc.scalar.activation
                ln.scalar_root(a)
                a.wait_ge(cols_turned, 1)
                nc.scalar.copy(cols[:], ps[:, 7, 0:NV]).then_inc(cols_ready, 1)
                ln.scalar_copy(a)
                a.wait_ge(cols_ready, 1)
                a.wait_ge(padded, 1)
                for n in range(NU):
                    q, blk = n // CB, n % CB
                    s, c0 = q // 2, (q % 2) * BANK
                    a.wait_ge(conv_done, n + 1)
                    act(xc[:, blk, s, c0:c0 + BANK], ps[:, 2 + n % 2, :], ACT.Identity,
                        bias=cbias[:, blk:blk + 1], scale=tap[:, CONV - 1, blk:blk + 1]).then_inc(raw_ready, 1)
                    nc.scalar.copy(raw[:, blk, s, CONV - 1 + c0:CONV - 1 + c0 + BANK],
                                   ps[:, 2 + n % 2, :]).then_inc(conv_read, 1)
                    a.wait_ge(zd_done, n + 1)
                    nc.scalar.copy(dtr[:, n, :], ps[:, 4 + n % 2, INNER:ZD]).then_inc(padded, 1)
                    act(sz[:, n, :], ps[:, 4 + n % 2, 0:INNER], ACT.Silu).then_inc(zd_read, 1)
                for n in range(NU):
                    q, blk = n // CB, n % CB
                    s, c0 = q // 2, (q % 2) * BANK
                    a.wait_ge(conv_ready, n + 1)
                    act(xc[:, blk, s, c0:c0 + BANK], xc[:, blk, s, c0:c0 + BANK], ACT.Silu).then_inc(silu_ready, 1)
                a.wait_ge(v_loaded, 96)
                act(alog[:], alog[:], ACT.Exp).then_inc(aexp_ready, 1)
                a.wait_ge(abs_ready, 1)
                act(sp_[:, 2, :, :], sp_[:, 1, :, :], ACT.Exp, scale=-1.0).then_inc(u_ready, 1)
                a.wait_ge(sums_done, 1)
                act(expo[:].rearrange("p a t h -> p (a t h)"), ps[:, 6, 0:3 * NT * SH], ACT.Exp).then_inc(expo_ready, 1)
                a.wait_ge(silu_ready, NU)
                for b in range(SEQS):
                    nc.scalar.copy(xch[:, b, :, :], xc[:, :, b, 0:P]).then_inc(chunk_ready, 1)
                with a.Fori(0, CHUNKS_ - 1) as i:
                    for b in range(SEQS):
                        n = SEQS * i
                        a.wait_ge(seg_done, n + (b + 1))
                        act(E[:, b, :, :], ps[:, 4 * b, :], ACT.Exp).then_inc(E_ready, 1)
                    for b in range(SEQS):
                        n = SEQS * i
                        a.wait_ge(inter_done, n + (b + 1))
                        nc.scalar.copy(xch[:, b, :, :], xc[:, :, b, bass.ds(P * i + P, P)]).then_inc(chunk_ready, 1)
                    for b in range(SEQS):
                        n = SEQS * i
                        a.wait_ge(M_ready, n + (b + 1))
                for b in range(SEQS):
                    n = SEQS * (CHUNKS_ - 1)
                    a.wait_ge(seg_done, n + (b + 1))
                    act(E[:, b, :, :], ps[:, 4 * b, :], ACT.Exp).then_inc(E_ready, 1)
                for c in range(NC):
                    t = (c % SEQS) * CHUNKS_ + c // SEQS
                    a.wait_ge(yg_ready, c + 1)
                    if c:
                        a.wait_ge(ssq_ready, c)
                    act(junk[:], yg[:, t, :], ACT.Square, accum_out=ssq[:, t:t + 1]).then_inc(ssq_ready, 1)
                a.wait_ge(ms_ready, 1)
                act(rms[:, 1, :], rms[:, 0, :], ACT.Sqrt).then_inc(root_ready, 1)
                for g in range(NT // 2):
                    a.wait_ge(yT_done, g + 1)
                    if g >= 2:
                        a.wait_ge(out_done, g - 1)
                    nc.scalar.copy(ygT[:, g % 2, :, :, :].rearrange("p j c t -> p (j c t)"), ps[:, g % 2, :]).then_inc(yT_ready, 1)

            @block.gpsimd
            def _(pool):
                tt = nc.gpsimd.tensor_tensor
                nc.gpsimd.memset(raw[:, :, :, 0:CONV - 1], 0.0).then_inc(padded, 1)
                pool.wait_ge(padded, 1)
                nc.gpsimd.memset(H[:], 0.0).then_inc(h_zeroed, 1)
                pool.wait_ge(h_zeroed, 1)
                for b in range(SEQS):
                    nc.gpsimd.memset(y3[:, b, :, :], 0.0).then_inc(y3_ready, 1)
                    pool.wait_ge(y3_ready, b + 1)
                pool.wait_ge(dec_ready, 1)
                pool.wait_ge(expo_ready, 1)

                def make_R(b, t):
                    tt(R[:, b, :, :], m.upto[:].unsqueeze(1).broadcast_to([P, SH, P]),
                       dec[:, t, :].rearrange("p t h -> p (t h)").unsqueeze(2).broadcast_to([P, SH, P]),
                       ALU.mult).then_inc(R_ready, 1)
                for b in range(SEQS):
                    make_R(b, slice(b * CHUNKS_, b * CHUNKS_ + 1))

                def body(i, more):
                    n = SEQS * i
                    for b in range(SEQS):
                        t = bass.ds(i + b * CHUNKS_, 1)
                        pool.wait_ge(dtx_ready, n + (b + 1))
                        tt(wxx[:, b, :, :], dtx[:, b, :, :],
                           expo[:, 1, t, :].rearrange("p t h -> p (t h)").unsqueeze(2).broadcast_to([P, SH, SP_]),
                           ALU.mult).then_inc(wxx_ready, 1)
                        if more:
                            pool.wait_ge(seg_done, n + (b + 1))
                            make_R(b, bass.ds(i + (b * CHUNKS_ + 1), 1))
                    for b in range(SEQS):
                        t = bass.ds(i + b * CHUNKS_, 1)
                        pool.wait_ge(y2_ready, 2 * n + (2 * b + 2))
                        pool.wait_ge(dx_ready, n + (b + 1))
                        tt(y3[:, b, :, :], y2[:, b, :, :], dx[:, b, :, :], ALU.add).then_inc(y3_ready, 1)
                        pool.wait_ge(y3_ready, n + (SEQS + b + 1))
                        yt = yg[:, t, :].rearrange("p t c -> p (t c)")
                        tt(yt, y3[:, b, :, :].rearrange("p h c -> p (h c)"),
                           sz[:, t, :].rearrange("p t c -> p (t c)"), ALU.mult).then_inc(yg_ready, 1)
                with pool.Fori(0, CHUNKS_ - 1) as i:
                    body(i, True)
                body(CHUNKS_ - 1, False)

            @block.vector
            def _(v):
                tt, ts, stt = nc.vector.tensor_tensor, nc.vector.tensor_scalar, nc.vector.scalar_tensor_tensor
                ln.vector(v)
                ch = Chain(v, conv_order)
                v.wait_ge(cols_ready, 1)
                for n in range(NU):
                    q, blk = n // CB, n % CB
                    s, c0 = q // 2, (q % 2) * BANK
                    v.wait_ge(raw_ready, n + 1)
                    v.wait_ge(conv_read, n + 1)
                    out = xc[:, blk, s, c0:c0 + BANK]
                    for k in range(CONV - 1):
                        ins = stt(out=out, in0=raw[:, blk, s, c0 + k:c0 + k + BANK], scalar=tap[:, k, blk:blk + 1],
                                  in1=out, op0=ALU.mult, op1=ALU.add)
                        if k < CONV - 2:
                            ch.link(ins)
                        else:
                            ins.then_inc(conv_ready, 1)
                ch = Chain(v, dt_order)
                v.wait_ge(v_loaded, 96)
                v.wait_ge(padded, 1 + NT)
                s, ab, u, den, r, r2, ser = (sp_[:, k, :, :] for k in range(7))
                shape = [P, NT, SH]

                def wide(t):
                    return t[:].unsqueeze(1).broadcast_to(shape)
                ch.link(tt(s, dtr[:], wide(dtb), ALU.add))
                stt(out=ab, in0=s, scalar=-1.0, in1=s, op0=ALU.mult, op1=ALU.max).then_inc(abs_ready, 1)
                v.wait_ge(u_ready, 1)
                ch.link(ts(den, u, 2.0, None, ALU.add))
                ch.link(nc.vector.reciprocal(r2, den))
                ch.link(tt(r, u, r2, ALU.mult))
                ch.link(tt(r2, r, r, ALU.mult))
                ch.link(ts(ser, r2, 1.0 / 15, None, ALU.mult))
                for odd in (13, 11, 9, 7, 5, 3):
                    ch.link(stt(out=ser, in0=ser, scalar=1.0 / odd, in1=r2, op0=ALU.add, op1=ALU.mult))
                ch.link(stt(out=ser, in0=ser, scalar=1.0, in1=r, op0=ALU.add, op1=ALU.mult))
                ch.link(ts(ser, ser, 2.0, None, ALU.mult))
                ch.link(stt(out=dt[:], in0=s, scalar=0.0, in1=ser, op0=ALU.max, op1=ALU.add))
                v.wait_ge(aexp_ready, 1)
                ch.link(tt(dec[:], dt[:], wide(alog), ALU.mult))
                ts(dec[:], dec[:], -1.0, DECAY_FLOOR, ALU.mult, ALU.max).then_inc(dec_ready, 1)
                for c in range(2):
                    v.wait_ge(w_loaded, 64)
                    ts(wout[:, c, :], wout[:, c, :], normw[:, c:c + 1], None, ALU.mult).then_inc(wout_ready, 1)
                tt(xn[:], xn[:], m.x[:], ALU.add).then_inc(xs_ready, 1)
                v.wait_ge(expo_ready, 1)
                v.wait_ge(h_zeroed, 1)
                for b in range(SEQS):
                    tt(Ht[:, b, :, :], H[:, b, :, :], H[:, b, :, :], ALU.mult).then_inc(H_ready, 1)

                with v.Fori(0, CHUNKS_) as i:
                    n = SEQS * i

                    def per_head(src, t):
                        return src[:, t, :].rearrange("p t h -> p (t h)").unsqueeze(2).broadcast_to([P, SH, SP_])
                    for b in range(SEQS):
                        t = bass.ds(i + b * CHUNKS_, 1)
                        pb = 4 * b
                        tok = ps[:, pb + 1, 0:INNER].rearrange("p (h c) -> p h c", h=SH)
                        v.wait_ge(tok_done, n + (b + 1))
                        v.wait_ge(H_ready, n + (b + 1))
                        tt(dtx[:, b, :, :], tok, per_head(dt, t), ALU.mult).then_inc(dtx_ready, 1)
                        nc.vector.tensor_copy(btok[:, b, :], ps[:, pb + 1, INNER:INNER + P]).then_inc(btok_ready, 1)
                        v.wait_ge(y3_ready, n + (b + 1))
                        tt(dx[:, b, :, :], tok, dsk[:].unsqueeze(2).broadcast_to([P, SH, SP_]), ALU.mult).then_inc(dx_ready, 1)
                        v.wait_ge(gt_done, n + (b + 1))
                        tt(Gm[:, b, :], ps[:, pb + 2, 0:P], m.upto[:], ALU.mult).then_inc(gm_ready, 1)
                        tt(Ht[:, b, :, :], H[:, b, :, :],
                           expo[:, 2, t, :].rearrange("p t h -> p (t h)").unsqueeze(2).broadcast_to([P, SH, SP_]),
                           ALU.mult).then_inc(ht_ready, 1)
                    for b in range(SEQS):
                        v.wait_ge(E_ready, n + (b + 1))
                        v.wait_ge(gm_ready, n + (b + 1))
                        tt(M[:, b, :, :], E[:, b, :, :], Gm[:, b, :].unsqueeze(1).broadcast_to([P, SH, P]),
                           ALU.mult).then_inc(M_ready, 1)
                    for b in range(SEQS):
                        t = bass.ds(i + b * CHUNKS_, 1)
                        pb = 4 * b
                        v.wait_ge(inter_done, n + (b + 1))
                        tt(y1[:, b, :, :], ps[:, pb + 2, P:P + INNER].rearrange("p (h c) -> p h c", h=SH),
                           expo[:, 0, t, :].rearrange("p t h -> p (t h)").unsqueeze(2).broadcast_to([P, SH, SP_]),
                           ALU.mult).then_inc(y1_ready, 1)
                        v.wait_ge(intra_done, n + (b + 1))
                        v.wait_ge(y1_ready, n + (b + 1))
                        for k in range(2):
                            own = ps[:, pb + 3, :].rearrange("p (a k h c) -> p a k h c", k=2, h=2, c=SP_)[:, :, k, k, :]
                            tt(y2[:, b, k::2, :], own, y1[:, b, k::2, :], ALU.add).then_inc(y2_ready, 1)
                        v.wait_ge(dh_done, n + (b + 1))
                        v.wait_ge(ht_ready, n + (b + 1))
                        tt(H[:, b, :, :], ps[:, pb, 0:INNER].rearrange("p (h c) -> p h c", h=SH), Ht[:, b, :, :],
                           ALU.add).then_inc(H_ready, 1)
                v.wait_ge(ssq_ready, NC)
                ch2 = Chain(v, dt_order, ch.n)
                ts(rms[:, 0, :], ssq[:], 1.0 / INNER, RMS_EPS, ALU.mult, ALU.add).then_inc(ms_ready, 1)
                v.wait_ge(root_ready, 1)
                ch2.link(nc.vector.reciprocal(rms[:, 2, :], rms[:, 1, :]))
                v.wait_ge(xs_ready, 1)
                for t in range(NT):
                    g = t // 2
                    v.wait_ge(out_done, g + 1)
                    stt(out=m.x[:, t, :], in0=ps[:, 2 + g % 2, (t % 2) * P:(t % 2 + 1) * P],
                        scalar=rms[:, 2, t:t + 1], in1=xn[:, t, :], op0=ALU.mult, op1=ALU.add).then_inc(x_ready, 1)
                v.wait_ge(x_ready, NT)


def hybrid_block(nc, x, w_in, offsets, amplitudes, sharpness, W_in, conv_w, conv_b, dt_bias, A_log, D_skip,
                 norm_w, W_out, router_w, correction_bias, up_w, down_w, shared_up_w, shared_down_w, out):
    with ExitStack() as ctx:
        m = Machine(nc, ctx)
        m.x = m.sb("x_rows", [P, NT, D])
        x_loaded = m.sem("x_loaded")
        with nc.Block() as block:
            @block.sync
            def _(sp):
                sp.dma_start(m.x[:], x.rearrange("b (t p) d -> p (b t) d", p=P)).then_inc(x_loaded, 16)
                sp.wait_ge(x_loaded, 16)
        build_constants(m)
        ffn = (router_w, correction_bias, up_w, down_w, shared_up_w, shared_down_w)
        attention(m, w_in, offsets, amplitudes, sharpness)
        m.end_stage()
        moe_ffn(m, "f1", *ffn)
        m.end_stage()
        mamba(m, W_in, conv_w, conv_b, dt_bias, A_log, D_skip, norm_w, W_out)
        m.end_stage()
        rows = out.rearrange("b (q t p) d -> (b q) p t d", p=P, t=QT)
        moe_ffn(m, "f2", *ffn, out=[rows[q] for q in range(NQ)])


_INS = ['L0_attn_a_x', 'L0_attn_a_w_in', 'L0_attn_a_kernel_offsets', 'L0_attn_a_kernel_amplitudes',
        'L0_attn_a_kernel_sharpness', 'L0_attn_b_W_in', 'L0_attn_b_conv_w', 'L0_attn_b_conv_b',
        'L0_attn_b_dt_bias', 'L0_attn_b_A_log', 'L0_attn_b_D', 'L0_attn_b_norm_w', 'L0_attn_b_W_out',
        'L0_ffn_router_w', 'L0_ffn_correction_bias', 'L0_ffn_up_w', 'L0_ffn_down_w',
        'L0_ffn_shared_up_w', 'L0_ffn_shared_down_w']
_OUTS = [((2, 1024, 128), 'float32')]


def kernel(**inputs):
    import numpy as _np
    import concourse.bacc as _bacc
    from concourse import mybir as _mybir
    from concourse.bass_utils import run_bass_kernel_spmd as _run

    nc = _bacc.Bacc("TRN2", target_bir_lowering=False, num_devices=1)
    arrays, args = {}, []
    for name in _INS:
        a = _np.ascontiguousarray(inputs[name])
        arrays[f"in_{name}_dram"] = a
        args.append(nc.dram_tensor(f"in_{name}_dram", a.shape, _mybir.dt.from_np(a.dtype), kind="ExternalInput").ap())
    for i, (shape, dtype) in enumerate(_OUTS):
        dt = _mybir.dt.from_np(_np.dtype(dtype))
        args.append(nc.dram_tensor(f"out_{i}_dram", shape, dt, kind="ExternalOutput").ap())
    hybrid_block(nc, *args)
    r = _run(nc, [arrays], core_ids=[0])
    return r.results[0]["out_0_dram"]
```

```python
import math
from contextlib import ExitStack

import concourse.bass as bass
from concourse import mybir

ALU = mybir.AluOpType
ACT = mybir.ActivationFunctionType
AX_X = mybir.AxisListType.X
F32 = mybir.dt.float32
BF16 = mybir.dt.bfloat16
F16 = mybir.dt.float16
F32R = mybir.dt.float32r

P = 128
D = 128
T = 2048
NT = T // P
BANK = 512
NQ = T // BANK
QT = BANK // P
LN_EPS = 1e-5


class Chain:

    def __init__(self, eng, sem, base=0):
        self.eng, self.sem, self.base, self.n = eng, sem, base, 0

    def add(self, ins):
        ins.then_inc(self.sem, 1)
        self.n += 1
        return ins

    def sync(self):
        self.eng.wait_ge(self.sem, self.base + self.n)

    def link(self, ins):
        self.add(ins)
        self.sync()


class Machine:

    def __init__(self, nc, ctx):
        self.nc, self.ctx = nc, ctx
        self.sems = []

    def sb(self, name, shape, dt=F32, ctx=None):
        return (ctx or self.ctx).enter_context(self.nc.sbuf_tensor(name, shape, dt))

    def ps(self, name, shape, dt=F32, ctx=None):
        return (ctx or self.ctx).enter_context(self.nc.psum_tensor(name, shape, dt))

    def sem(self, name):
        s = self.nc.alloc_semaphore(name=name)
        self.sems.append(s)
        return s

    def end_stage(self):
        self.nc.clear_and_free_semaphores(self.sems)
        self.sems = []
        self.nc.all_engine_barrier()


def allot_constants(m):
    m.ident = m.sb("ident", [P, P])
    m.ident16 = m.sb("ident16", [P, P], F16)
    m.identb = m.sb("identb", [P, P], BF16)
    m.flip_sum = m.sb("flip_sum", [P, 64], F16)
    m.upto = m.sb("upto", [P, P])
    m.after = m.sb("after", [P, P])
    m.ones = m.sb("ones", [P, P])
    m.before8 = m.sb("before8", [P, 8, 8])
    m.spread = m.sb("spread", [P, 64, 64], F16)
    m.ident_made = m.sem("ident_made")
    m.filled, m.made = m.sem("const_filled"), m.sem("const_made")


def pool_select(m, t, pattern, base, op, fill, mult):
    return m.nc.gpsimd.affine_select(out=t, in_=t, compare_op=op, fill=fill, base=base,
                                     pattern=pattern, channel_multiplier=mult)


def constants_first(m, pool):
    m.nc.gpsimd.memset(m.ident[:], 0.0).then_inc(m.filled, 1)
    pool.wait_ge(m.filled, 1)
    pool_select(m, m.ident[:], [[-1, P]], 0, ALU.not_equal, 1.0, 1).then_inc(m.ident_made, 1)


def constants_rest(m, pool):
    nc = m.nc
    zero = [m.ident16, m.identb, m.flip_sum, m.spread]
    one = [m.upto, m.after, m.ones, m.before8]
    for t in zero:
        nc.gpsimd.memset(t[:], 0.0).then_inc(m.filled, 1)
    for t in one:
        nc.gpsimd.memset(t[:], 1.0).then_inc(m.filled, 1)
    pool.wait_ge(m.filled, 1 + len(zero) + len(one))

    def select(*args):
        pool_select(m, *args).then_inc(m.made, 1)
    for t in (m.ident16, m.identb):
        select(t[:], [[-1, P]], 0, ALU.not_equal, 1.0, 1)
    select(m.flip_sum[:], [[1, 64]], -63, ALU.not_equal, 1.0, 1)
    select(m.upto[:], [[1, P]], 0, ALU.is_ge, 0.0, -1)
    select(m.after[:], [[-1, P]], -1, ALU.is_ge, 0.0, 1)
    select(m.before8[:], [[1, 8], [-1, 8]], -1, ALU.is_ge, 0.0, 0)
    select(m.spread[:], [[-1, 64], [0, 64]], 0, ALU.not_equal, 1.0, 1)
    pool.wait_ge(m.made, 7)
    select(m.spread[:], [[-1, 64], [0, 64]], -64, ALU.not_equal, 1.0, 1)
    select(m.flip_sum[:], [[1, 64]], -127, ALU.not_equal, 1.0, 1)
    pool.wait_ge(m.made, 9)


def build_constants(m):
    allot_constants(m)
    with m.nc.Block() as block:
        @block.gpsimd
        def _(pool):
            constants_first(m, pool)
            constants_rest(m, pool)


class LayerNorm:

    def __init__(self, m, tag, xn, xnT, bank):
        self.m, self.xn, self.xnT, self.bank = m, xn, xnT, bank
        self.stats = m.sb(f"{tag}_stats", [P, NT, 6], ctx=m.stage)
        self.tmp = m.sb(f"{tag}_tmp", [P, 8, NT], ctx=m.stage)
        self.stat = m.sem(f"{tag}_ln_order")
        self.var = m.sem(f"{tag}_var_ready")
        self.std = m.sem(f"{tag}_std_ready")
        self.norm = m.sem(f"{tag}_xn_ready")
        self.turned = m.sem(f"{tag}_turned")
        self.ready = m.sem(f"{tag}_xnT_ready")

    def vector(self, v, loaded=None):
        m, nc = self.m, self.m.nc
        ch = Chain(v, self.stat)
        for t in range(NT):
            if loaded and t % QT == 0:
                v.wait_ge(loaded[t // QT], 16)
            ch.add(nc.vector.bn_stats(self.stats[:, t, :], m.x[:, t, :]))
        ch.sync()
        me, mo = self.stats[:, :, 1], self.stats[:, :, 4]
        qe, qo = self.stats[:, :, 2], self.stats[:, :, 5]
        mean, dif, sq, m2, var, rstd = (self.tmp[:, i, :] for i in (0, 1, 2, 3, 4, 6))
        tt, ts = nc.vector.tensor_tensor, nc.vector.tensor_scalar
        ch.add(tt(mean, me, mo, ALU.add))
        ch.add(tt(dif, me, mo, ALU.subtract))
        ch.link(tt(m2, qe, qo, ALU.add))
        ch.link(tt(sq, dif, dif, ALU.mult))
        ch.add(ts(mean, mean, 0.5, None, ALU.mult))
        ch.link(nc.vector.scalar_tensor_tensor(out=var, in0=sq, scalar=D / 4.0, in1=m2,
                                               op0=ALU.mult, op1=ALU.add))
        ts(var, var, 1.0 / D, LN_EPS, ALU.mult, ALU.add).then_inc(self.var, 1)
        v.wait_ge(self.std, 1)
        ch.link(nc.vector.reciprocal(rstd, self.tmp[:, 5, :]))
        for t in range(NT):
            ts(self.xn[:, t, :], m.x[:, t, :], mean[:, t:t + 1], rstd[:, t:t + 1],
               ALU.subtract, ALU.mult).then_inc(self.norm, 1)

    def scalar_root(self, a):
        a.wait_ge(self.var, 1)
        self.m.nc.scalar.activation(self.tmp[:, 5, :], self.tmp[:, 4, :], ACT.Sqrt).then_inc(self.std, 1)

    def scalar_quarter(self, a, q):
        a.wait_ge(self.turned, q + 1)
        self.m.nc.scalar.copy(self.xnT[:, q * BANK:(q + 1) * BANK], self.bank(q)).then_inc(self.ready, 1)

    def scalar_copy(self, a):
        for q in range(NQ):
            self.scalar_quarter(a, q)

    def tensor_quarter(self, pe, q):
        pe.wait_ge(self.norm, QT * (q + 1))
        if q >= 2:
            pe.wait_ge(self.ready, q - 1)
        for k in range(QT):
            last = self.m.nc.tensor.transpose(self.bank(q)[:, k * P:(k + 1) * P],
                                              self.xn[:, QT * q + k, :], self.m.ident[:])
        last.then_inc(self.turned, 1)

    def tensor(self, pe):
        for q in range(NQ):
            self.tensor_quarter(pe, q)


E_ALL = 64
PAIRS = E_ALL // 2
HID = 64
GROUPS = 8
GE = E_ALL // GROUPS
TOP_GROUPS = 4
TOP_K = 8
ROUTE_SCALE = 2.5
SHARED = 2


def moe_ffn(m, tag, router_w, correction_bias, up_w, down_w, shared_up_w, shared_down_w, out=None):
    nc = m.nc
    with ExitStack() as stage:
        m.stage = stage

        def sb(name, shape, dt=F32):
            return m.sb(f"{tag}_{name}", shape, dt, stage)

        def sem(name):
            return m.sem(f"{tag}_{name}")

        xn, xnT = sb("xn", [P, NT, D]), sb("xnT", [D, T])
        acc = m.ps(f"{tag}_acc", [P, NQ, BANK], ctx=stage)
        work = m.ps(f"{tag}_work", [P, 4, BANK], ctx=stage)
        hid, cw, turn = work[:, 0:3, :], work[:, 3, :], work[:, 2:4, :]
        turn16 = turn.bitcast(F16)
        rw = sb("rw", [E_ALL, D])
        rwT = sb("rwT", [D, E_ALL])
        cbias = sb("cbias", [P, E_ALL])
        xh, xl = sb("x_high", [D, T], F32R), sb("x_low", [D, T], F32R)
        shu = sb("shu", [D, SHARED * P])
        shu_h, shu_l = sb("shu_high", [D, SHARED * P], F32R), sb("shu_low", [D, SHARED * P], F32R)
        wu_h, wu_l = sb("wu_high", [D, 2, 2 * HID], F32R), sb("wu_low", [D, 2, 2 * HID], F32R)
        shd = sb("shd", [P, SHARED, D])
        wu = sb("wu", [D, 2, 2 * HID])
        wd = sb("wd", [2 * HID, 2, D])
        score = sb("score", [P, NT, E_ALL])
        sfc = sb("sfc", [P, NT, E_ALL])
        masked = sb("masked", [P, NT, E_ALL])
        struck = sb("struck", [P, NT, E_ALL])
        top = sb("top", [P, NT, TOP_K])
        pairA, pairB = sb("pairA", [P, NT * GROUPS, 4]), sb("pairB", [P, NT * GROUPS, 4])
        quadA, quadB = sb("quadA", [P, NT * GROUPS, 2]), sb("quadB", [P, NT * GROUPS, 2])
        quadC = sb("quadC", [P, NT * GROUPS, 2])
        gbest = sb("gbest", [P, 4, NT * GROUPS])
        gsum = sb("gsum", [P, NT, GROUPS])
        cmp1, cmp2 = sb("cmp1", [P, NT, GROUPS, GROUPS]), sb("cmp2", [P, NT, GROUPS, GROUPS])
        rank = sb("rank", [P, NT, GROUPS])
        wsum = sb("wsum", [P, 2, NT])
        chl = sb("chl", [P, NT, 2, E_ALL], F16)
        cT = sb("cT", [P, T], F16)
        relu = sb("relu", [P, 2, BANK])
        gated = sb("gated", [P, 2, BANK])
        act = sb("act", [P, 4, BANK])
        act_h, act_l = sb("act_high", [P, 4, BANK], F32R), sb("act_low", [P, 4, BANK], F32R)
        wd_h, wd_l = sb("wd_high", [2 * HID, 2, D], F32R), sb("wd_low", [2 * HID, 2, D], F32R)
        outT = sb("outT", [P, NQ, BANK])

        ln = LayerNorm(m, tag, xn, xnT, lambda q: turn[:, q % 2, :])
        small_in = sem("small_in")
        up_in = [sem("even_up_in"), sem("odd_up_in")]
        down_in = [sem("even_down_in"), sem("odd_down_in")]
        rw_turned, rw_ready = sem("rw_turned"), sem("rw_ready")
        logits_ready, score_ready = sem("logits_ready"), sem("score_ready")
        route = sem("route_order")
        ch_ready = sem("weights_ready")
        cT_turned, cT_ready = sem("cT_turned"), sem("cT_ready")
        up_done, cw_done, down_done = sem("up_done"), sem("cw_done"), sem("down_done")
        relu_ready, gate_done, act_ready = sem("relu_ready"), sem("gate_done"), sem("act_ready")
        shared_ready = sem("shared_ready")
        x_high, x_low = sem("x_high_ready"), sem("x_low_ready")
        w_high, w_low = sem("w_high_ready"), sem("w_low_ready")
        wd_high, wd_low = sem("wd_high_ready"), sem("wd_low_ready")
        act_high, act_low = sem("act_high_ready"), sem("act_low_ready")
        shu_high, shu_low = sem("shu_high_ready"), sem("shu_low_ready")
        outT_ready, out_turned, x_ready = sem("outT_ready"), sem("out_turned"), sem("x_ready")
        stored = sem("stored")

        NS = SHARED * NQ
        NR = PAIRS * NQ
        BODY = 24
        HEAD = NR % BODY
        LAG = 4

        def each_unit(eng, unit):
            for j in range(HEAD):
                unit(0, j)
            with eng.Fori(0, NR // BODY - 1) as i:
                for j in range(HEAD, HEAD + BODY):
                    unit(i, j)
            for j in range(HEAD, HEAD + BODY):
                unit(NR // BODY - 1, j)

        def past(i, j, n):
            return not isinstance(i, int) or BODY * i + j >= n

        with nc.Block() as block:
            @block.sync
            def _(sp):
                sp.dma_start(rw[:], router_w).then_inc(small_in, 16)
                sp.dma_start(cbias[:], correction_bias.rearrange("(a e) -> a e", a=1).broadcast_to([P, E_ALL])).then_inc(small_in, 16)
                sp.dma_start(shu[:], shared_up_w).then_inc(small_in, 16)
                sp.dma_start(shd[:], shared_down_w.rearrange("(s p) d -> p s d", p=P)).then_inc(small_in, 16)

                def load_up(pair, slot):
                    sp.dma_start(wu[:, slot, :].rearrange("p (e i) -> p e i", e=2),
                                 up_w[bass.ds(2 * pair, 2), :, :].rearrange("e d i -> d e i")).then_inc(up_in[slot], 16)

                def load_down(pair, slot):
                    sp.dma_start(wd[:, slot, :],
                                 down_w[bass.ds(2 * pair, 2), :, :].rearrange("e i d -> (e i) d")).then_inc(down_in[slot], 16)
                for p in range(2):
                    load_up(p, p)
                    load_down(p, p)
                with sp.Fori(0, PAIRS // 2 - 1) as i:
                    for j in range(2):
                        sp.wait_ge(w_low, 2 * i + j + 1)
                        load_up(2 * i + 2 + j, j)
                        sp.wait_ge(wd_low, 2 * i + j + 1)
                        load_down(2 * i + 2 + j, j)
                if out is not None:
                    for q in range(NQ):
                        sp.wait_ge(x_ready, q + 1)
                        sp.dma_start(out[q], m.x[:, QT * q:QT * (q + 1), :]).then_inc(stored, 16)
                    sp.wait_ge(stored, 16 * NQ)

            @block.tensor
            def _(pe):
                mm = nc.tensor.matmul
                pe.wait_ge(small_in, 64)
                nc.tensor.transpose(hid[:, 0, 0:E_ALL], rw[:], m.ident[0:E_ALL, 0:E_ALL]).then_inc(rw_turned, 1)
                ln.tensor(pe)
                pe.wait_ge(rw_ready, 1)
                for t in range(NT):
                    pe.wait_ge(ln.ready, t // QT + 1)
                    last = mm(hid[:, t // 8, (t % 8) * E_ALL:(t % 8 + 1) * E_ALL],
                              xnT[:, t * P:(t + 1) * P], rwT[:], start=True, stop=True)
                last.then_inc(logits_ready, 1)

                def up(w_hi, w_lo, q, n):
                    cols = slice(q * BANK, (q + 1) * BANK)
                    mm(hid[:, n % 3, :], w_hi, xh[:, cols], start=True, stop=False)
                    mm(hid[:, n % 3, :], w_hi, xl[:, cols], start=False, stop=False)
                    mm(hid[:, n % 3, :], w_lo, xh[:, cols], start=False, stop=True).then_inc(up_done, 1)

                def down(w, q, n, start, stop):
                    mm(acc[:, q, :], w, act[:, n % 4, :], start=start, stop=stop,
                       skip_group_check=True).then_inc(down_done, 1)

                pe.wait_ge(score_ready, 1)
                pe.wait_ge(shu_low, 1)
                pe.wait_ge(x_low, NQ)
                for n in range(NS):
                    if n >= 3:
                        pe.wait_ge(relu_ready, n - 2)
                    blk = slice((n // NQ) * P, (n // NQ + 1) * P)
                    up(shu_h[:, blk], shu_l[:, blk], n % NQ, n)
                    if n >= 2:
                        k = n - 2
                        pe.wait_ge(shared_ready, k + 1)
                        down(shd[:, k // NQ, :], k % NQ, k, k < NQ, False)
                for k in range(NS - 2, NS):
                    pe.wait_ge(shared_ready, k + 1)
                    down(shd[:, k // NQ, :], k % NQ, k, False, False)
                pe.wait_ge(ch_ready, 1)
                pe.wait_ge(relu_ready, NS)
                for t in range(NT):
                    last = nc.tensor.transpose(turn16[:, t // 8, (t % 8) * P:(t % 8 + 1) * P],
                                               chl[:, t, :, :].rearrange("p a e -> p (a e)"), m.ident16[:])
                    if t % 8 == 7:
                        last.then_inc(cT_turned, 1)
                pe.wait_ge(cT_ready, 2)


                def down_routed(i, j):
                    if j % 4 == 0:
                        pe.wait_ge(wd_low, 6 * i + (j // 4 + 1))
                    pe.wait_ge(act_low, BODY * i + (j + 1))
                    slot = j // 4 % 2
                    for k, (w, x) in enumerate(((wd_h, act_h), (wd_h, act_l), (wd_l, act_h))):
                        last = mm(acc[:, j % 4, :], w[:, slot, :], x[:, j % 4, :], start=False,
                                  stop=(k == 2), skip_group_check=True)
                    last.then_inc(down_done, 1)

                def unit(i, j):
                    slot = j // 4 % 2
                    if j % 4 == 0:
                        pe.wait_ge(w_low, 6 * i + (j // 4 + 1))
                    if past(i, j, 3):
                        pe.wait_ge(act_ready, BODY * i + (j - 2))
                    up(wu_h[:, slot, :], wu_l[:, slot, :], j % 4, j)
                    if past(i, j, LAG):
                        down_routed(i, j - LAG)
                    if past(i, j, 1):
                        pe.wait_ge(gate_done, BODY * i + j)
                    e = 12 * i + 2 * (j // 4)
                    mm(cw, m.spread[:, bass.ds(e, 2), :].rearrange("p e j -> p (e j)"),
                       cT[:, (j % 4) * BANK:(j % 4 + 1) * BANK], start=True, stop=True).then_inc(cw_done, 1)
                each_unit(pe, unit)
                for j in range(LAG):
                    down_routed(NR // BODY - 1, HEAD + BODY - LAG + j)
                for q in range(NQ):
                    pe.wait_ge(outT_ready, q + 1)
                    if q >= 2:
                        pe.wait_ge(x_ready, q - 1)
                    for k in range(QT):
                        last = nc.tensor.transpose(hid[:, q % 2, k * P:(k + 1) * P],
                                                   outT[:, q, k * P:(k + 1) * P], m.ident[:])
                    last.then_inc(out_turned, 1)

            @block.scalar
            def _(a):
                ln.scalar_root(a)
                a.wait_ge(rw_turned, 1)
                nc.scalar.copy(rwT[:], hid[:, 0, 0:E_ALL]).then_inc(rw_ready, 1)
                ln.scalar_copy(a)
                a.wait_ge(small_in, 64)
                nc.scalar.copy(shu_h[:], shu[:]).then_inc(shu_high, 1)
                a.wait_ge(ln.ready, NQ)
                for q in range(NQ):
                    cols = slice(q * BANK, (q + 1) * BANK)
                    nc.scalar.copy(xh[:, cols], xnT[:, cols]).then_inc(x_high, 1)

                for p in range(2):
                    a.wait_ge(up_in[p], 16)
                    nc.scalar.copy(wu_h[:, p, :], wu[:, p, :]).then_inc(w_high, 1)
                a.wait_ge(logits_ready, 1)
                nc.scalar.activation(score[:].rearrange("p t e -> p (t e)"),
                                     hid[:, 0:2, :].rearrange("p a b -> p (a b)"), ACT.Sigmoid).then_inc(score_ready, 1)
                for n in range(NS):
                    a.wait_ge(up_done, n + 1)
                    if n >= 2:
                        a.wait_ge(shared_ready, n - 1)
                    nc.scalar.activation(relu[:, n % 2, :], hid[:, n % 3, :], ACT.Relu).then_inc(relu_ready, 1)
                    a.wait_ge(relu_ready, n + 1)
                    if n >= 4:
                        a.wait_ge(down_done, n - 3)
                    nc.scalar.activation(act[:, n % 4, :], relu[:, n % 2, :], ACT.Square).then_inc(shared_ready, 1)
                for h in range(2):
                    a.wait_ge(cT_turned, h + 1)
                    nc.scalar.copy(cT[:, h * 1024:(h + 1) * 1024], turn16[:, h, :]).then_inc(cT_ready, 1)
                a.wait_ge(shared_ready, NS)

                def high_part(i, j):
                    a.wait_ge(act_ready, BODY * i + (j + 1))
                    if past(i, j, 4):
                        a.wait_ge(down_done, BODY * i + (NS + j - 3))
                    nc.scalar.copy(act_h[:, j % 4, :], act[:, j % 4, :]).then_inc(act_high, 1)

                def unit(i, j):
                    pair = 6 * i + j // 4
                    a.wait_ge(up_done, BODY * i + (NS + j + 1))
                    if past(i, j, 2):
                        a.wait_ge(gate_done, BODY * i + (j - 1))
                    nc.scalar.activation(relu[:, j % 2, :], hid[:, j % 3, :], ACT.Relu).then_inc(relu_ready, 1)
                    if j % 4 == 0 and past(i, j, 4) and not (isinstance(i, int) and pair + 1 == PAIRS):
                        slot = (j // 4 + 1) % 2
                        a.wait_ge(up_in[slot], 48 * i + 16 * ((j // 4 + 1) // 2 + 1))
                        a.wait_ge(w_low, pair)
                        nc.scalar.copy(wu_h[:, slot, :], wu[:, slot, :]).then_inc(w_high, 1)
                    if j % 4 == 1:
                        slot = j // 4 % 2
                        a.wait_ge(down_in[slot], 48 * i + 16 * (j // 8 + 1))
                        if past(i, j, 8):
                            a.wait_ge(down_done, BODY * i + (NS + j - 5))
                            a.wait_ge(wd_low, pair - 1)
                        nc.scalar.copy(wd_h[:, slot, :], wd[:, slot, :]).then_inc(wd_high, 1)
                    if past(i, j, 1):
                        high_part(i, j - 1)
                each_unit(a, unit)
                high_part(NR // BODY - 1, HEAD + BODY - 1)
                for q in range(NQ):
                    a.wait_ge(down_done, NS + NR - NQ + q + 1)
                    nc.scalar.copy(outT[:, q, :], acc[:, q, :]).then_inc(outT_ready, 1)

            @block.gpsimd
            def _(pool):
                pool.wait_ge(shu_high, 1)
                nc.gpsimd.tensor_tensor(shu_l[:], shu[:], shu_h[:].bitcast(F32), ALU.subtract).then_inc(shu_low, 1)
                for q in range(NQ):
                    cols = slice(q * BANK, (q + 1) * BANK)
                    pool.wait_ge(x_high, q + 1)
                    nc.gpsimd.tensor_tensor(xl[:, cols], xnT[:, cols], xh[:, cols].bitcast(F32),
                                            ALU.subtract).then_inc(x_low, 1)
                with pool.Fori(0, NR // 4) as i:
                    for k in range(4):
                        pool.wait_ge(act_high, 4 * i + (k + 1))
                        nc.gpsimd.tensor_tensor(act_l[:, k, :], act[:, k, :], act_h[:, k, :].bitcast(F32),
                                                ALU.subtract).then_inc(act_low, 1)

            @block.vector
            def _(v):
                ln.vector(v)
                tt, ts = nc.vector.tensor_tensor, nc.vector.tensor_scalar
                ch = Chain(v, route)
                v.wait_ge(small_in, 64)
                v.wait_ge(score_ready, 1)
                ch.link(tt(sfc[:], score[:], cbias[:].unsqueeze(1).broadcast_to([P, NT, E_ALL]), ALU.add))
                s = sfc[:].rearrange("p t (g e) -> p (t g) e", g=GROUPS)
                ch.add(tt(pairA[:], s[:, :, 0:4], s[:, :, 4:8], ALU.max))
                ch.link(tt(pairB[:], s[:, :, 0:4], s[:, :, 4:8], ALU.min))
                ch.add(tt(quadA[:], pairA[:, :, 0:2], pairA[:, :, 2:4], ALU.max))
                ch.add(tt(quadB[:], pairA[:, :, 0:2], pairA[:, :, 2:4], ALU.min))
                ch.link(tt(quadC[:], pairB[:, :, 0:2], pairB[:, :, 2:4], ALU.max))
                ch.link(tt(quadB[:], quadB[:], quadC[:], ALU.max))
                ch.add(tt(gbest[:, 0, :], quadA[:, :, 0], quadA[:, :, 1], ALU.max))
                ch.add(tt(gbest[:, 1, :], quadA[:, :, 0], quadA[:, :, 1], ALU.min))
                ch.link(tt(gbest[:, 2, :], quadB[:, :, 0], quadB[:, :, 1], ALU.max))
                ch.link(tt(gbest[:, 3, :], gbest[:, 1, :], gbest[:, 2, :], ALU.max))
                ch.link(tt(gsum[:].rearrange("p t g -> p (t g)"), gbest[:, 0, :], gbest[:, 3, :], ALU.add))
                shape = [P, NT, GROUPS, GROUPS]
                other = gsum[:].unsqueeze(2).broadcast_to(shape)
                own = gsum[:].unsqueeze(3).broadcast_to(shape)
                ch.add(tt(cmp1[:], other, own, ALU.is_gt))
                ch.link(tt(cmp2[:], other, own, ALU.is_equal))
                ch.link(tt(cmp2[:], cmp2[:], m.before8[:].unsqueeze(1).broadcast_to(shape), ALU.mult))
                ch.link(tt(cmp1[:], cmp1[:], cmp2[:], ALU.add))
                ch.link(nc.vector.tensor_reduce(rank[:], cmp1[:], AX_X, ALU.add))
                ch.link(ts(rank[:], rank[:], TOP_GROUPS - 0.5, None, ALU.is_lt))
                ch.link(tt(masked[:].rearrange("p t (g e) -> p (t g) e", g=GROUPS), s,
                           rank[:].rearrange("p t g -> p (t g)").unsqueeze(2).broadcast_to([P, NT * GROUPS, GE]),
                           ALU.mult))
                for t in range(NT):
                    ch.add(nc.vector.max(top[:, t, :], masked[:, t, :]))
                ch.sync()
                for t in range(NT):
                    ch.add(nc.vector.match_replace(struck[:, t, :], top[:, t, :], masked[:, t, :], -1e30))
                ch.sync()
                ch.link(tt(struck[:], struck[:], masked[:], ALU.not_equal))
                ch.link(tt(masked[:], score[:], struck[:], ALU.mult))
                ch.link(nc.vector.tensor_reduce(wsum[:, 0, :], masked[:], AX_X, ALU.add))
                ch.link(ts(wsum[:, 0, :], wsum[:, 0, :], 1e-20, None, ALU.add))
                ch.link(nc.vector.reciprocal(wsum[:, 1, :], wsum[:, 0, :]))
                ch.link(tt(struck[:], masked[:], wsum[:, 1, :].unsqueeze(2).broadcast_to([P, NT, E_ALL]), ALU.mult))
                ch.link(ts(masked[:], struck[:], ROUTE_SCALE, None, ALU.mult))
                ch.link(nc.vector.tensor_copy(chl[:, :, 0, :], masked[:]))
                tt(chl[:, :, 1, :], masked[:], chl[:, :, 0, :], ALU.subtract).then_inc(ch_ready, 1)

                def low_part(raw, high, low, slot, ready, pairs, done):
                    v.wait_ge(ready, pairs)
                    tt(low[:, slot, :], raw[:, slot, :], high[:, slot, :].bitcast(F32), ALU.subtract).then_inc(done, 1)
                for p in range(2):
                    low_part(wu, wu_h, wu_l, p, w_high, p + 1, w_low)

                def unit(i, j):
                    pair = 6 * i + j // 4
                    v.wait_ge(relu_ready, BODY * i + (NS + j + 1))
                    v.wait_ge(cw_done, BODY * i + (j + 1))
                    if past(i, j, 2):
                        v.wait_ge(act_ready, BODY * i + (j - 1))
                    tt(gated[:, j % 2, :], relu[:, j % 2, :], cw, ALU.mult).then_inc(gate_done, 1)
                    v.wait_ge(gate_done, BODY * i + (j + 1))
                    if past(i, j, 4):
                        v.wait_ge(act_low, BODY * i + (j - 3))
                    else:
                        v.wait_ge(down_done, NS + j - 3)
                    tt(act[:, j % 4, :], gated[:, j % 2, :], hid[:, j % 3, :], ALU.mult).then_inc(act_ready, 1)
                    if j % 4 == 0 and past(i, j, 4) and not (isinstance(i, int) and pair + 1 == PAIRS):
                        low_part(wu, wu_h, wu_l, (j // 4 + 1) % 2, w_high, pair + 2, w_low)
                    if j % 4 == 1:
                        low_part(wd, wd_h, wd_l, j // 4 % 2, wd_high, pair + 1, wd_low)
                each_unit(v, unit)
                for q in range(NQ):
                    v.wait_ge(out_turned, q + 1)
                    rows = m.x[:, QT * q:QT * (q + 1), :].rearrange("p t d -> p (t d)")
                    tt(rows, hid[:, q % 2, :], rows, ALU.add).then_inc(x_ready, 1)
                v.wait_ge(x_ready, NQ)


HEADS = 16
HD = D // HEADS
KERNELS = 16
BATCH = 2
L = T // BATCH
LT = L // P
G4 = 4
ITERS = BATCH * HEADS // G4
PIECES = 3
QK_ROWS = PIECES * PIECES * HD
K_ROWS = 96
MAX_W = 2 * L - P
HALF = P // 2
COL_W = 2 * L - HALF
CHUNKS = 4
CW = COL_W // CHUNKS
STEPS = 2 * LT
UNITS = G4 * LT * 2
UNIT_FROM, UNIT_TO = 2, 14
STACK_DMAS = 2 * PIECES + 1


def step_columns(s, u):
    lh, mb = s // LT, LT - 1 - s % LT
    return lh * BANK - mb * P - u * HALF + L - HALF


def attention(m, x, w_in, offsets, amplitudes, sharpness):
    nc = m.nc
    with ExitStack() as stage:
        m.stage = stage

        def sb(name, shape, dt=F32, ctx=stage):
            return m.sb(f"at_{name}", shape, dt, ctx)

        def sem(name):
            return m.sem(f"at_{name}")

        kd = nc.dram_tensor("k_parts", [HEADS, PIECES * HD, T], BF16).ap()
        qd = nc.dram_tensor("q_parts", [HEADS, (2 * PIECES - 1) * HD, T], BF16).ap()
        bias_d = nc.dram_tensor("bias_rows", [3, HEADS, 2 * L], F16).ap()
        bias_hi, bias_lo = (bias_d[k] for k in (1, 2))

        s1 = m.ps("at_rows", [P, 2, BANK], ctx=stage)
        s2 = m.ps("at_cols", [P, 2, 2, BANK], ctx=stage)
        pv = m.ps("at_pv", [P, BANK], ctx=stage)
        tp = m.ps("at_tp", [P, BANK], ctx=stage)

        v_nat = sb("v_nat", [P, NT, D])
        q_st = sb("q_stack", [K_ROWS, 2, G4, L], BF16)
        k_st = sb("k_stack", [K_ROWS, 2, G4, L], BF16)
        vst = sb("v_stack", [P, 2, LT, G4, 32])
        zrow = sb("zero_rows", [PIECES * G4 * LT, P], BF16)
        preset = sem("preset")

        def presets(pool):
            for n, (t, value) in enumerate([
                    (q_st[64:K_ROWS], 0.0), (k_st[64:K_ROWS], 1.0), (zrow[:], 0.0),
                    (vst[:, :, :, :, HD:HD + 1], 1.0), (vst[:, :, :, :, HD + 1:32], 0.0)]):
                nc.gpsimd.memset(t, value).then_inc(preset, 1)
                pool.wait_ge(preset, n + 1)

        ops = Operands(sb, sem, kd, qd, bias_hi, bias_lo, q_st, k_st, zrow)
        prologue(m, sb, sem, s1, s2, pv, tp, x, w_in, offsets, amplitudes, sharpness,
                 kd, qd, bias_hi, bias_lo, v_nat, preset, presets, ops)
        attend(m, sb, sem, s1, s2, pv, tp, v_nat, vst, ops)


class Operands:

    STORES = BATCH * (3 * PIECES - 1)

    def __init__(self, sb, sem, kd, qd, bias_hi, bias_lo, q_st, k_st, zrow):
        self.kd, self.qd, self.bias_hi, self.bias_lo = kd, qd, bias_hi, bias_lo
        self.q_st, self.k_st, self.zrow = q_st, k_st, zrow
        self.t_col = sb("table_cols", [P, G4, COL_W], F16)
        self.t_max = sb("table_max", [P, G4, MAX_W], F16)
        self.parts = sb("parts", [P, BATCH, 2, PIECES, L], BF16)
        self.stored = sem("parts_out")
        self.v_copied = sem("v_copied")
        self.stack_in = [sem("stack_in_even"), sem("stack_in_odd")]
        self.max_tab_in = [sem(f"max_tab_in{h}") for h in range(G4)]
        self.tab_in = [sem(f"tab_in{c}") for c in range(CHUNKS)]

    def store_parts(self, sp, b):
        for kind, dst, blocks in ((0, self.kd, PIECES), (1, self.qd, 2 * PIECES - 1)):
            for a in range(blocks):
                sp.dma_start(dst[:, a * HD:(a + 1) * HD, b * L:(b + 1) * L],
                             self.parts[:, b, kind, a % PIECES, :]).then_inc(self.stored, 16)

    def toeplitz(self, row, g4, h0, nh, parts, c0, n):
        a = row[bass.ds(g4 + h0, nh), c0:c0 + n]
        return bass.AP(tensor=a.tensor, offset=a.offset, ap=[[1, parts], [2 * L, nh], [1, n]])

    def load_max_table(self, sp, g4, h):
        sp.dma_start(self.t_max[:, h:h + 1, :],
                     self.toeplitz(self.bias_hi, g4, h, 1, P, 0, MAX_W)).then_inc(self.max_tab_in[h], 16)

    def load_table(self, sp, g4, c):
        for r, row in ((0, self.bias_hi), (HALF, self.bias_lo)):
            sp.dma_start(self.t_col[r:r + HALF, :, c * CW:(c + 1) * CW],
                         self.toeplitz(row, g4, 0, G4, HALF, c * CW, CW)).then_inc(self.tab_in[c], 16)

    def load_stack(self, sp, g4, b):
        cols = slice(b * L, (b + 1) * L)
        rows = PIECES * HD
        for s in range(PIECES):
            for st, dram, r in ((self.q_st, self.qd, s * HD), (self.k_st, self.kd, 0)):
                sp.dma_start(st[s * rows:(s + 1) * rows, b, :, :],
                             dram[bass.ds(g4, G4), r:r + rows, cols].rearrange("h r l -> r h l")
                             ).then_inc(self.stack_in[b], 16)
        sp.dma_start(self.q_st[QK_ROWS:QK_ROWS + PIECES, b, :, :].rearrange("p h (t l) -> p (h t) l", l=P),
                     self.zrow[:]).then_inc(self.stack_in[b], 16)


def prologue(m, sb, sem, s1, s2, pv, tp, x, w_in, offsets, amplitudes, sharpness,
             kd, qd, bias_hi, bias_lo, v_nat, preset, presets, ops):
    nc = m.nc
    with ExitStack() as pro:
        def psb(name, shape, dt=F32):
            return sb(name, shape, dt, pro)
        m.stage = pro
        xn, xnT = psb("xn", [P, NT, D]), psb("xnT", [D, T])
        wraw, wT = psb("wraw", [P, 3, D]), psb("wT", [D, 3, D])
        HG = HEADS * KERNELS // P
        PH = P // KERNELS
        off, amp, shp = psb("off", [P, HG]), psb("amp", [P, HG]), psb("shp", [P, HG])
        ramp = psb("ramp", [P, 2 * L])
        gau = psb("gau", [P, HG, 2 * L])
        ramp_i = gau[:, 0, :].bitcast(mybir.dt.int32)
        amp_mask, amp_of = psb("amp_mask", [P, HG, HEADS]), psb("amp_of", [P, HG, HEADS])
        b_hi, b_lo = psb("b_hi", [HEADS, 2 * L], F16), psb("b_lo", [HEADS, 2 * L], F16)
        rest = psb("rest", [P, 2, BANK])
        parts, v_copied = ops.parts, ops.v_copied

        ln = LayerNorm(m, "at", xn, xnT, lambda q: s1[:, q % 2, :])
        w_loaded, small_loaded = sem("w_loaded"), sem("small_loaded")
        x_in = [sem(f"x_in{q}") for q in range(NQ)]
        w_turned, w_ready = sem("w_turned"), sem("w_ready")
        ramp_made, square_ready, gauss_ready = sem("ramp_made"), sem("square_ready"), sem("gauss_ready")
        mask_made, amp_ready, signs = sem("mask_made"), sem("amp_ready"), sem("signs_ready")
        bias_ready, parts_made = sem("bias_ready"), sem("bias_parts")
        bias_out = sem("bias_out")
        proj_done, proj_read, high_ready = sem("proj_done"), sem("proj_read"), sem("high_ready")
        split = sem("split_order")
        parts_ready = sem("parts_ready")
        v_done = sem("v_done")
        KINDS = 2 * NQ
        proj_bank = (pv, tp)
        with nc.Block() as block:
            @block.sync
            def _(sp):
                for t, src in ((off, offsets), (shp, sharpness), (amp, amplitudes)):
                    sp.dma_start(t[:], src.rearrange("(g h) k -> (h k) g", g=HG),
                                 allow_slow_non_contiguous=True).then_inc(small_loaded, 16)
                rows = x.rearrange("b (q t p) d -> (b q) p t d", p=P, t=QT)
                for q in range(NQ):
                    sp.dma_start(m.x[:, QT * q:QT * (q + 1), :], rows[q]).then_inc(x_in[q], 16)
                sp.dma_start(wraw[:], w_in.rearrange("(a e) d -> e a d", a=3)).then_inc(w_loaded, 16)
                sp.wait_ge(parts_ready, KINDS // 2)
                ops.store_parts(sp, 0)
                sp.wait_ge(parts_made, 2)
                sp.dma_start(bias_hi, b_hi[:]).then_inc(bias_out, 16)
                sp.dma_start(bias_lo, b_lo[:]).then_inc(bias_out, 16)
                sp.wait_ge(ops.stored, 16 * ops.STORES // BATCH)
                sp.wait_ge(preset, 5)
                ops.load_stack(sp, 0, 0)
                sp.wait_ge(bias_out, 32)
                for h in range(G4):
                    ops.load_max_table(sp, 0, h)

            @block.gpsimd
            def _(pool):
                nc.gpsimd.iota(ramp_i, [[1, 2 * L]], base=1 - L, channel_multiplier=0).then_inc(ramp_made, 1)
                constants_first(m, pool)
                nc.gpsimd.memset(amp_mask[:], 1.0).then_inc(mask_made, 1)
                pool.wait_ge(mask_made, 1)
                nc.gpsimd.affine_select(out=amp_mask[:], in_=amp_mask[:], compare_op=ALU.is_ge, fill=0.0, base=0,
                                        pattern=[[P, HG], [-KERNELS, HEADS]], channel_multiplier=1).then_inc(mask_made, 1)
                pool.wait_ge(mask_made, 2)
                nc.gpsimd.affine_select(out=amp_mask[:], in_=amp_mask[:], compare_op=ALU.is_ge, fill=0.0,
                                        base=KERNELS - 1, pattern=[[-P, HG], [KERNELS, HEADS]],
                                        channel_multiplier=-1).then_inc(mask_made, 1)
                constants_rest(m, pool)
                presets(pool)

            @block.tensor
            def _(pe):
                mm = nc.tensor.matmul

                def project(q):
                    pe.wait_ge(ln.ready, q + 1)
                    for n in (2 * q, 2 * q + 1):
                        if n >= 2:
                            pe.wait_ge(proj_read, n - 1)
                        mm(proj_bank[n % 2][:], wT[:, (0, 2)[n % 2], :], xnT[:, q * BANK:(q + 1) * BANK],
                           start=True, stop=True).then_inc(proj_done, 1)
                pe.wait_ge(w_loaded, 16)
                pe.wait_ge(m.ident_made, 1)
                for a in range(3):
                    last = nc.tensor.transpose(tp[:, a * P:(a + 1) * P], wraw[:, a, :], m.ident[:])
                last.then_inc(w_turned, 1)
                pe.wait_ge(w_ready, 2)
                for q in range(2):
                    ln.tensor_quarter(pe, q)
                for q in range(2):
                    project(q)
                for q in range(2, NQ):
                    ln.tensor_quarter(pe, q)
                pe.wait_ge(amp_ready, 1)
                pe.wait_ge(gauss_ready, HG)
                for c in range(4):
                    for g in range(HG):
                        last = mm(s2[0:HEADS, c // 2, c % 2, :], amp_of[:, g, :],
                                  gau[:, g, c * BANK:(c + 1) * BANK], start=(g == 0), stop=(g == HG - 1))
                last.then_inc(bias_ready, 1)
                for q in range(2, NQ):
                    project(q)
                for g in range(NQ):
                    if g >= 2:
                        pe.wait_ge(v_copied, g - 1)
                    for k in range(QT):
                        t = g * QT + k
                        last = mm(s1[:, g % 2, k * P:(k + 1) * P], xnT[:, t * P:(t + 1) * P], wT[:, 1, :],
                                  start=True, stop=True)
                    last.then_inc(v_done, 1)

            @block.scalar
            def _(a):
                act = nc.scalar.activation
                a.wait_ge(signs, 3)
                for g in range(HG):
                    act(gau[:, g, :], ramp[:], ACT.Square, bias=off[:, g:g + 1]).then_inc(square_ready, 1)
                ln.scalar_root(a)
                a.wait_ge(w_turned, 1)
                nc.scalar.copy(wT[:, 0:2, :].rearrange("p a d -> p (a d)"), tp[:, 0:2 * D]).then_inc(w_ready, 1)
                nc.scalar.mul(wT[:, 2, :], tp[:, 2 * D:3 * D], 1.0 / math.sqrt(HD)).then_inc(w_ready, 1)

                def high_part(n):
                    q = n // 2
                    b, c0 = q // 2, (q % 2) * BANK
                    a.wait_ge(proj_done, n + 1)
                    nc.scalar.copy(parts[:, b, n % 2, 0, c0:c0 + BANK], proj_bank[n % 2][:]).then_inc(high_ready, 1)
                def gaussian(g):
                    a.wait_ge(square_ready, g + 1)
                    act(gau[:, g, :], gau[:, g, :], ACT.Exp, scale=shp[:, g:g + 1]).then_inc(gauss_ready, 1)
                for q in range(2):
                    ln.scalar_quarter(a, q)
                high_part(0)
                high_part(1)
                gaussian(0)
                high_part(2)
                gaussian(1)
                high_part(3)
                for q in range(2, NQ):
                    ln.scalar_quarter(a, q)
                a.wait_ge(bias_ready, 1)
                nc.scalar.copy(b_hi[:], s2[0:HEADS].rearrange("p a b c -> p (a b c)")).then_inc(parts_made, 1)
                for n in range(KINDS // 2, KINDS):
                    high_part(n)
                for g in range(NQ):
                    a.wait_ge(v_done, g + 1)
                    nc.scalar.copy(v_nat[:, g * QT:(g + 1) * QT, :].rearrange("p t d -> p (t d)"),
                                   s1[:, g % 2, :]).then_inc(v_copied, 1)

            @block.vector
            def _(v):
                tt, ts = nc.vector.tensor_tensor, nc.vector.tensor_scalar
                v.wait_ge(ramp_made, 1)
                nc.vector.tensor_copy(ramp[:], ramp_i).then_inc(signs, 1)
                v.wait_ge(small_loaded, 48)
                ts(off[:], off[:], -1.0, None, ALU.mult).then_inc(signs, 1)
                nc.vector.scalar_tensor_tensor(out=shp[:], in0=shp[:], scalar=-1.0, in1=shp[:],
                                               op0=ALU.mult, op1=ALU.min).then_inc(signs, 1)
                v.wait_ge(mask_made, 3)
                tt(amp_of[:], amp_mask[:], amp[:].unsqueeze(2).broadcast_to([P, HG, HEADS]), ALU.mult).then_inc(amp_ready, 1)
                ln.vector(v, x_in)
                ch = Chain(v, split)
                for n in range(KINDS):
                    q = n // 2
                    b, c0 = q // 2, (q % 2) * BANK
                    hi, mid, lo = (parts[:, b, n % 2, k, c0:c0 + BANK] for k in range(PIECES))
                    v.wait_ge(high_ready, n + 1)
                    if n >= 2:
                        v.wait_ge(parts_ready, n - 1)
                    tt(rest[:, n % 2, :], proj_bank[n % 2][:], hi, ALU.subtract).then_inc(proj_read, 1)
                    v.wait_ge(proj_read, n + 1)
                    ch.link(nc.vector.tensor_copy(mid, rest[:, n % 2, :]))
                    tt(lo, rest[:, n % 2, :], mid, ALU.subtract).then_inc(parts_ready, 1)
                    if n == KINDS // 2 - 1:
                        v.wait_ge(parts_made, 1)
                        tt(b_lo[:], s2[0:HEADS].rearrange("p a b c -> p (a b c)"), b_hi[:], ALU.subtract).then_inc(parts_made, 1)
                v.wait_ge(parts_ready, KINDS)
                v.wait_ge(parts_made, 2)


def attend(m, sb, sem, s1, s2, pv, tp, v_nat, vst, ops):
    nc = m.nc
    q_st, k_st, t_col, t_max = ops.q_st, ops.k_st, ops.t_col, ops.t_max
    stack_in, max_tab_in, tab_in = ops.stack_in, ops.max_tab_in, ops.tab_in
    prob = sb("prob", [P, 2, G4, BANK])
    mx = sb("maxima", [P, G4 * LT, 2])
    mtop = sb("mtop", [P, 3, G4 * LT])
    negm = sb("negm", [P, PIECES, G4 * LT], BF16)
    negT = sb("negT", [PIECES * G4 * LT, P], BF16)
    oT = sb("oT", [P, BANK])
    rden = sb("rden", [P, QT, G4])
    onorm = sb("onorm", [P, QT, G4, HD])
    tpb = tp[:].bitcast(BF16)

    first_rows, first_max = sem("first_rows"), sem("first_max")
    rows_ready, max_done = sem("rows_ready"), sem("max_done")
    m_order, negm_ready, neg_turned, neg_copied = sem("m_order"), sem("negm_ready"), sem("neg_turned"), sem("neg_copied")
    max_in = [sem("max_in_even"), sem("max_in_odd")]
    cols_ready, exp_done, pv_done = sem("cols_ready"), sem("exp_done"), sem("pv_done")
    oT_ready, o_turned, o_read, x_added = sem("oT_ready"), sem("o_turned"), sem("o_read"), sem("x_added")
    o_order = sem("o_order")
    v_ready = sem("v_ready")

    def units_before(s):
        return UNITS * min(max(s - UNIT_FROM, 0), UNIT_TO - UNIT_FROM) // (UNIT_TO - UNIT_FROM)
    unit_steps = [range(units_before(s), units_before(s + 1)) for s in range(STEPS)]
    M_STEP = STEPS - 1
    O_STEP = (10, 2)

    def reads(s, c):
        return step_columns(s, 1) < (c + 1) * CW and step_columns(s, 0) + BANK > c * CW
    last_read = [max(s for s in range(STEPS) if reads(s, c)) for c in range(CHUNKS)]
    first_read = [min(s for s in range(STEPS) if reads(s, c)) for c in range(CHUNKS)]

    with nc.Block() as block:
        @block.sync
        def _(sp):
            ops.store_parts(sp, 1)
            for c in range(CHUNKS):
                ops.load_table(sp, 0, c)
            sp.wait_ge(ops.stored, 16 * ops.STORES)
            ops.load_stack(sp, 0, 1)
            with sp.Fori(0, ITERS // 2 - 1) as i:
                for h in range(G4):
                    sp.wait_ge(max_done, 2 * UNITS * i + (h + 1) * UNITS // G4)
                    ops.load_max_table(sp, G4 * i + G4, h)
                sp.wait_ge(cols_ready, 2 * 2 * STEPS * i + 2 * STEPS)
                ops.load_stack(sp, G4 * i + G4, 0)
                for c in range(CHUNKS):
                    sp.wait_ge(cols_ready, 2 * 2 * STEPS * i + (2 * STEPS + 2 * last_read[c] + 2))
                    ops.load_table(sp, G4 * i + G4, c)
                sp.wait_ge(cols_ready, 2 * 2 * STEPS * i + 4 * STEPS)
                ops.load_stack(sp, G4 * i + G4, 1)

        @block.gpsimd
        def _(pool):
            def take_v(b, c0):
                nc.gpsimd.tensor_copy(
                    vst[:, b, :, :, 0:HD],
                    v_nat[:, b * LT:(b + 1) * LT, bass.ds(c0, G4 * HD)].rearrange("p t (h d) -> p t h d", h=G4)
                ).then_inc(v_ready, 1)
            take_v(0, 0)
            take_v(1, 0)
            with pool.Fori(0, ITERS // 2 - 1) as i:
                for b in range(2):
                    pool.wait_ge(pv_done, 2 * STEPS * i + (b + 1) * STEPS)
                    take_v(b, G4 * HD * i + G4 * HD)

        def pe_unit(pe, k, it, b, g_count):
            h, lb, mh = k // (2 * LT), k // 2 % LT, k % 2
            if k == 0:
                pe.wait_ge(stack_in[b], 16 * STACK_DMAS * g_count)
            first = isinstance(it, int) and it == 1
            if not (first and k < 2):
                pe.wait_ge(max_done, UNITS * (it - 1) + (k - 1))
            nc.tensor.matmul(s1[:, k % 2, :], q_st[:, b, h, lb * P:(lb + 1) * P],
                             k_st[:, b, h, mh * BANK:(mh + 1) * BANK], start=True, stop=True).then_inc(rows_ready, 1)

        def pe_turn_max(pe, it):
            pe.wait_ge(negm_ready, it + 1)
            if not (isinstance(it, int) and it == 0):
                pe.wait_ge(o_read, 2 * it - 1)
            nc.tensor.transpose(tpb[0:PIECES * G4 * LT, 0:P], negm[:].rearrange("p a n -> p (a n)"),
                                m.identb[:]).then_inc(neg_turned, 1)

        def pe_cols(pe, s, h, it, b, g_count):
            n = STEPS * it + s
            hp, j = h // 2, h % 2
            first = isinstance(it, int) and it == 0 and s == 0
            if s == 0 and h == 0:
                pe.wait_ge(max_in[b], 16 * g_count)
            if b == 0 and h == 0:
                for c in range(CHUNKS):
                    if first_read[c] == s:
                        pe.wait_ge(tab_in[c], 32 * g_count)
            if not first and j == 0:
                pe.wait_ge(exp_done, 2 * n + (hp - 1))
            lh, mb = s // LT, LT - 1 - s % LT
            out = s2[:, hp, j, :]
            nc.tensor.matmul(out, k_st[:, b, h, mb * P:(mb + 1) * P],
                             q_st[:, b, h, lh * BANK:(lh + 1) * BANK], start=True, stop=False)
            for u in range(2):
                c = step_columns(s, u)
                last = nc.tensor.matmul(out[u * HALF:(u + 1) * HALF, :], m.flip_sum[:], t_col[:, h, c:c + BANK],
                                        start=False, stop=True)
            if j == 1:
                last.then_inc(cols_ready, 1)

        def pe_pv(pe, s, it, b):
            n = STEPS * it + s
            mb = LT - 1 - s % LT
            pe.wait_ge(exp_done, 2 * n + 2)
            if s == 0:
                pe.wait_ge(v_ready, it + 1)
            if s % LT == 0 and not (isinstance(it, int) and it == 0 and s == 0):
                pe.wait_ge(oT_ready, 2 * it + s // LT)
            for h in range(G4):
                last = nc.tensor.matmul(pv[32 * h:32 * h + 32, :], vst[:, b, mb, h, :], prob[:, s % 2, h, :],
                                        start=(s % LT == 0), stop=(s % LT == LT - 1))
            last.then_inc(pv_done, 1)

        def pe_out(pe, k, wait_neg):
            pe.wait_ge(oT_ready, k + 1)
            if wait_neg is not None:
                pe.wait_ge(neg_copied, wait_neg)
            if not (isinstance(k, int) and k == 0):
                pe.wait_ge(o_read, k)
            for t in range(QT):
                last = nc.tensor.transpose(tp[:, t * P:(t + 1) * P], oT[:, t * P:(t + 1) * P], m.ident[:])
            last.then_inc(o_turned, 1)

        def pe_iteration(pe, it, b, g_count, nxt_count, first=False, final=False):
            for s in range(STEPS):
                units = [] if final else list(unit_steps[s])
                if s == M_STEP and not final:
                    pe_turn_max(pe, it + 1)
                def unit(n):
                    if n < len(units):
                        pe_unit(pe, units[n], it + 1, 1 - b, nxt_count)
                for h in range(G4):
                    if h == 2:
                        if s > 0:
                            pe_pv(pe, s - 1, it, b)
                        elif not first:
                            pe_pv(pe, STEPS - 1, it - 1, 1 - b)
                        unit(2)
                    pe_cols(pe, s, h, it, b, g_count)
                    unit((0, 1, 3, 4)[h])
                unit(5)
                if s == O_STEP[0]:
                    pe_out(pe, 2 * it, None)
                if s == O_STEP[1] and not first:
                    pe_out(pe, 2 * it - 1, it + 1)

        @block.tensor
        def _(pe):
            pe.wait_ge(stack_in[0], 16 * STACK_DMAS)
            for k in range(UNITS // 2):
                h, lb = k // LT, k % LT
                if k >= 2:
                    pe.wait_ge(first_max, k - 1)
                for mh in range(2):
                    last = nc.tensor.matmul(s2[:, k % 2, mh, :], q_st[:, 0, h, lb * P:(lb + 1) * P],
                                            k_st[:, 0, h, mh * BANK:(mh + 1) * BANK], start=True, stop=True)
                last.then_inc(first_rows, 1)
            pe_turn_max(pe, 0)
            pe_iteration(pe, 0, 0, 1, 1, first=True)
            with pe.Fori(0, ITERS // 2 - 1) as i:
                pe_iteration(pe, 2 * i + 1, 1, i + 1, i + 2)
                pe_iteration(pe, 2 * i + 2, 0, i + 2, i + 2)
            pe_iteration(pe, ITERS - 1, 1, ITERS // 2, None, final=True)
            pe_pv(pe, STEPS - 1, ITERS - 1, 1)
            pe_out(pe, 2 * ITERS - 1, None)

        def act_negT(a, it, b):
            a.wait_ge(neg_turned, it + 1)
            if not (isinstance(it, int) and it < 1):
                a.wait_ge(max_in[1 - b], 16 * it_half(it, 1 - b))
            nc.scalar.copy(negT[:], tpb[0:PIECES * G4 * LT, 0:P]).then_inc(neg_copied, 1)
            a.wait_ge(neg_copied, it + 1)
            a.dma_start(q_st[QK_ROWS:QK_ROWS + PIECES, b, :, :].rearrange("p h (t l) -> p (h t) l", l=P),
                        negT[:]).then_inc(max_in[b], 16)

        def it_half(it, other):
            return halves[0]
        halves = [None]

        def act_iteration(a, it, b, other_count, first=False, final=False):
            for s in range(STEPS):
                n = STEPS * it + s
                if s == M_STEP and not final:
                    halves[0] = other_count
                    act_negT(a, it + 1, 1 - b)
                for hp in range(2):
                    a.wait_ge(cols_ready, 2 * n + (hp + 1))
                    if not (first and s < 2):
                        a.wait_ge(pv_done, n - 1)
                    nc.scalar.activation(prob[:, s % 2, 2 * hp:2 * hp + 2, :], s2[:, hp, :, :],
                                         ACT.Exp).then_inc(exp_done, 1)
                if s == LT:
                    act_oT(a, 2 * it, STEPS * it + LT)
                if s == 0 and not first:
                    act_oT(a, 2 * it - 1, STEPS * it)

        def act_oT(a, k, products):
            a.wait_ge(pv_done, products)
            if not (isinstance(k, int) and k == 0):
                a.wait_ge(o_turned, k)
            nc.scalar.copy(oT[:], pv[:]).then_inc(oT_ready, 1)

        @block.scalar
        def _(a):
            a.wait_ge(neg_turned, 1)
            nc.scalar.copy(negT[:], tpb[0:PIECES * G4 * LT, 0:P]).then_inc(neg_copied, 1)
            a.wait_ge(neg_copied, 1)
            a.dma_start(q_st[QK_ROWS:QK_ROWS + PIECES, 0, :, :].rearrange("p h (t l) -> p (h t) l", l=P),
                        negT[:]).then_inc(max_in[0], 16)
            act_iteration(a, 0, 0, 1, first=True)
            with a.Fori(0, ITERS // 2 - 1) as i:
                act_iteration(a, 2 * i + 1, 1, i + 1)
                act_iteration(a, 2 * i + 2, 0, i + 2)
            act_iteration(a, ITERS - 1, 1, None, final=True)
            act_oT(a, 2 * ITERS - 1, STEPS * ITERS)

        def dve_unit(v, k, it, g_count):
            h, lb, mh = k // (2 * LT), k // 2 % LT, k % 2
            if k % (2 * LT) == 0 and g_count is not None:
                v.wait_ge(max_tab_in[h], 16 * g_count)
            if isinstance(it, int):
                v.wait_ge(rows_ready, UNITS * (it - 1) + (k + 1))
            else:
                v.wait_ge(rows_ready, next_rows)
                v.reg_add(next_rows, next_rows, 1)
            c = lb * P - mh * BANK + L - BANK
            nc.vector.tensor_tensor_reduce(out=s1[:, k % 2, :], in0=s1[:, k % 2, :],
                                           in1=t_max[:, h, c:c + BANK][:, ::-1], scale=1.0, scalar=-3.0e38,
                                           op0=ALU.add, op1=ALU.max,
                                           accum_out=mx[:, k // 2, k % 2:k % 2 + 1]).then_inc(max_done, 1)

        M_OPS = 6

        def dve_negm(v, it):
            tt, stt = nc.vector.tensor_tensor, nc.vector.scalar_tensor_tensor
            first = isinstance(it, int) and it == 0
            if first:
                v.wait_ge(first_max, UNITS // 2)
            else:
                v.wait_ge(max_done, UNITS * it)
            ch = Chain(v, m_order, (M_OPS - 1) * it)
            if not (isinstance(it, int) and it == 0):
                v.wait_ge(neg_turned, it)
            ch.link(nc.vector.tensor_reduce(mtop[:, 0, :], mx[:, :, 0:1] if first else mx[:], AX_X, ALU.max))
            ch.link(nc.vector.tensor_scalar(negm[:, 0, :], mtop[:, 0, :], -1.0, None, ALU.mult))
            ch.link(stt(out=mtop[:, 1, :], in0=mtop[:, 0, :], scalar=-1.0, in1=negm[:, 0, :],
                        op0=ALU.mult, op1=ALU.subtract))
            ch.link(nc.vector.tensor_copy(negm[:, 1, :], mtop[:, 1, :]))
            ch.link(tt(mtop[:, 2, :], mtop[:, 1, :], negm[:, 1, :], ALU.subtract))
            nc.vector.tensor_copy(negm[:, 2, :], mtop[:, 2, :]).then_inc(negm_ready, 1)

        def dve_out(v, k, b, lh, c0):
            t4 = tp[:].rearrange("p (t h e) -> p t h e", t=QT, h=G4)
            v.wait_ge(o_turned, k + 1)
            if not (isinstance(k, int) and k == 0):
                v.wait_ge(x_added, k)
            nc.vector.reciprocal(rden[:], t4[:, :, :, HD]).then_inc(o_order, 1)
            v.wait_ge(o_order, k + 1)
            nc.vector.tensor_tensor(onorm[:], t4[:, :, :, 0:HD],
                                    rden[:].unsqueeze(3).broadcast_to([P, QT, G4, HD]), ALU.mult).then_inc(o_read, 1)
            v.wait_ge(o_read, k + 1)
            rows = m.x[:, b * LT + lh * QT:b * LT + (lh + 1) * QT, bass.ds(c0, G4 * HD)]
            nc.vector.tensor_tensor(rows, rows, onorm[:].rearrange("p t h e -> p t (h e)"),
                                    ALU.add).then_inc(x_added, 1)

        def dve_iteration(v, it, b, c0, prev_c0, nxt_count, first=False, final=False):
            for s in range(STEPS):
                if s == O_STEP[1] + 1 and not first:
                    dve_out(v, 2 * it - 1, 1 - b, 1, prev_c0)
                if s == O_STEP[0] + 1:
                    dve_out(v, 2 * it, b, 0, c0)
                if not final:
                    for k in unit_steps[s]:
                        dve_unit(v, k, it + 1, nxt_count)
                    if len(unit_steps[s]) and unit_steps[s][-1] == UNITS - 1:
                        dve_negm(v, it + 1)

        next_rows = nc.vector.alloc_register("next_rows")

        @block.vector
        def _(v):
            for k in range(UNITS // 2):
                h, lb = k // LT, k % LT
                if lb == 0:
                    v.wait_ge(max_tab_in[h], 16)
                v.wait_ge(first_rows, k + 1)
                scores = s2[:, k % 2, :, :].rearrange("p a b -> p (a b)")
                nc.vector.tensor_tensor_reduce(out=scores, in0=scores, in1=t_max[:, h, lb * P:lb * P + L][:, ::-1],
                                               scale=1.0, scalar=-3.0e38, op0=ALU.add, op1=ALU.max,
                                               accum_out=mx[:, k, 0:1]).then_inc(first_max, 1)
            dve_negm(v, 0)
            W = G4 * HD
            dve_iteration(v, 0, 0, 0, None, None, first=True)
            v.reg_mov(next_rows, UNITS + 1)
            with v.Fori(0, ITERS // 2 - 1) as i:
                dve_iteration(v, 2 * i + 1, 1, W * i, W * i, i + 2)
                dve_iteration(v, 2 * i + 2, 0, W * i + W, W * i, None)
            dve_iteration(v, ITERS - 1, 1, W * (ITERS // 2 - 1), W * (ITERS // 2 - 1), None, final=True)
            dve_out(v, 2 * ITERS - 1, 1, 1, W * (ITERS // 2 - 1))
            v.wait_ge(x_added, 2 * ITERS)


INNER = 256
STATE = 128
SH = 4
SP_ = INNER // SH
CONV = 4
CB = (INNER + 2 * STATE) // P
SEQS = 2
SEQ = T // SEQS
CHUNKS_ = SEQ // P
RMS_EPS = 1e-5
DECAY_FLOOR = -1e5


def mamba(m, W_in, conv_w, conv_b, dt_bias, A_log, Dskip, norm_w, W_out):
    nc = m.nc
    with ExitStack() as stage:
        m.stage = stage

        def sb(name, shape, dt=F32):
            return m.sb(f"ss_{name}", shape, dt, stage)

        def sem(name):
            return m.sem(f"ss_{name}")

        ZD = INNER + SH
        xn, xnT = sb("xn", [P, NT, D]), sb("xnT", [D, T])
        wzd, wx = sb("wzd", [D, ZD]), sb("wx", [D, CB, P])
        NV = CONV * CB + CB + 2
        rows, cols = sb("rows", [NV, P]), sb("cols", [P, NV])
        tap = cols[:, 0:CONV * CB].rearrange("p (k b) -> p k b", k=CONV)
        cbias, normw = cols[:, CONV * CB:CONV * CB + CB], cols[:, CONV * CB + CB:NV]
        wout = sb("wout", [P, 2, D])
        dtb, alog, dsk = sb("dtb", [P, SH]), sb("alog", [P, SH]), sb("dsk", [P, SH])
        raw = sb("raw", [P, CB, SEQS, SEQ + CONV - 1])
        xc = sb("xc", [P, CB, SEQS, SEQ])
        sz = sb("sz", [P, NT, INNER])
        dtr = sb("dtr", [P, NT, SH])
        sp_ = sb("softplus", [P, 8, NT, SH])
        dt, dec = sb("dt", [P, NT, SH]), sb("dec", [P, NT, SH])
        expo = sb("expo", [P, 3, NT, SH])
        xch = sb("chunk", [P, 2, CB, P])
        R = sb("R", [P, 2, SH, P])
        E = sb("E", [P, 2, SH, P])
        Gm, M = sb("Gm", [P, 2, P]), sb("M", [P, 2, SH, P])
        btok = sb("btok", [P, 2, P])
        dtx, wxx, dx = (sb(n, [P, 2, SH, SP_]) for n in ("dtx", "wxx", "dx"))
        y1, y2, y3 = (sb(n, [P, 2, SH, SP_]) for n in ("y1", "y2", "y3"))
        H, Ht = sb("H", [P, 2, SH, SP_]), sb("Ht", [P, 2, SH, SP_])
        yg = sb("yg", [P, NT, INNER])
        junk = sb("squares", [P, INNER])
        ssq = sb("ssq", [P, NT])
        rms = sb("rms", [P, 3, NT])
        ygT = sb("ygT", [P, 2, 2, 2, P])
        ps = m.ps("ss_ps", [P, 8, BANK], ctx=stage)

        ln = LayerNorm(m, "ss", xn, xnT, lambda q: ps[:, q % 2, :])
        w_loaded, v_loaded = sem("w_loaded"), sem("v_loaded")
        cols_turned, cols_ready = sem("cols_turned"), sem("cols_ready")
        zd_done, zd_read = sem("zd_done"), sem("zd_read")
        conv_done, conv_read, raw_ready = sem("conv_done"), sem("conv_read"), sem("raw_ready")
        padded = sem("padded")
        conv_order, conv_ready, silu_ready = sem("conv_order"), sem("conv_ready"), sem("silu_ready")
        dt_order, abs_ready, u_ready, aexp_ready = sem("dt_order"), sem("abs_ready"), sem("u_ready"), sem("aexp_ready")
        dec_ready, sums_done, expo_ready = sem("dec_ready"), sem("sums_done"), sem("expo_ready")
        h_zeroed, xs_ready = sem("h_zeroed"), sem("xs_ready")
        chunk_ready, R_ready = sem("chunk_ready"), sem("R_ready")
        tok_done, gt_done, seg_done = sem("tok_done"), sem("gt_done"), sem("seg_done")
        inter_done, intra_done, dh_done = sem("inter_done"), sem("intra_done"), sem("dh_done")
        E_ready, gm_ready, M_ready = sem("E_ready"), sem("gm_ready"), sem("M_ready")
        btok_ready, dtx_ready, dx_ready, wxx_ready = sem("btok_ready"), sem("dtx_ready"), sem("dx_ready"), sem("wxx_ready")
        y1_ready, y2_ready, y3_ready, yg_ready = sem("y1_ready"), sem("y2_ready"), sem("y3_ready"), sem("yg_ready")
        ht_ready, H_ready = sem("ht_ready"), sem("H_ready")
        ssq_ready, ms_ready, root_ready, rms_ready = sem("ssq_ready"), sem("ms_ready"), sem("root_ready"), sem("rms_ready")
        wout_ready = sem("wout_ready")
        yT_done, yT_ready, out_done, x_ready = sem("yT_done"), sem("yT_ready"), sem("out_done"), sem("x_ready")
        NU = NQ * CB
        NC = CHUNKS_ * SEQS

        with nc.Block() as block:
            @block.sync
            def _(sp):
                sp.dma_start(rows[0:CONV * CB, :], conv_w.rearrange("k (b c) -> (k b) c", c=P)).then_inc(v_loaded, 16)
                sp.dma_start(rows[CONV * CB:CONV * CB + CB, :], conv_b.rearrange("(b c) -> b c", c=P)).then_inc(v_loaded, 16)
                sp.dma_start(rows[CONV * CB + CB:NV, :], norm_w.rearrange("(b c) -> b c", c=P)).then_inc(v_loaded, 16)
                for t, src in ((dtb, dt_bias), (alog, A_log), (dsk, Dskip)):
                    sp.dma_start(t[:], src.rearrange("(a h) -> a h", a=1).broadcast_to([P, SH])).then_inc(v_loaded, 16)
                XB = INNER + CB * P
                sp.dma_start(wzd[:, 0:INNER], W_in[:, 0:INNER]).then_inc(w_loaded, 16)
                sp.dma_start(wzd[:, INNER:ZD], W_in[:, XB:XB + SH]).then_inc(w_loaded, 16)
                sp.dma_start(wx[:], W_in[:, INNER:XB].rearrange("d (b c) -> d b c", c=P)).then_inc(w_loaded, 16)
                sp.dma_start(wout[:], W_out.rearrange("(b c) d -> c b d", c=P)).then_inc(w_loaded, 16)
                sp.wait_ge(w_loaded, 64)

            @block.tensor
            def _(pe):
                mm = nc.tensor.matmul
                pe.wait_ge(v_loaded, 96)
                nc.tensor.transpose(ps[:, 7, 0:NV], rows[:], m.ident[0:NV, 0:NV]).then_inc(cols_turned, 1)
                ln.tensor(pe)
                pe.wait_ge(w_loaded, 64)
                for n in range(NU):
                    q, blk = n // CB, n % CB
                    if blk == 0:
                        pe.wait_ge(ln.ready, q + 1)
                    if n >= 2:
                        pe.wait_ge(conv_read, n - 1)
                    mm(ps[:, 2 + n % 2, :], wx[:, blk, :], xnT[:, q * BANK:(q + 1) * BANK],
                       start=True, stop=True).then_inc(conv_done, 1)
                    if n >= 2:
                        pe.wait_ge(zd_read, n - 1)
                    mm(ps[:, 4 + n % 2, 0:ZD], xnT[:, n * P:(n + 1) * P], wzd[:],
                       start=True, stop=True).then_inc(zd_done, 1)
                pe.wait_ge(dec_ready, 1)
                for k, mask in enumerate((m.upto, m.after, m.ones)):
                    last = mm(ps[:, 6, k * NT * SH:(k + 1) * NT * SH], mask[:],
                              dec[:].rearrange("p t h -> p (t h)"), start=True, stop=True)
                last.then_inc(sums_done, 1)
                pe.wait_ge(expo_ready, 1)

                with pe.Fori(0, CHUNKS_) as i:
                    for b in range(SEQS):
                        n = SEQS * i
                        pb = 4 * b
                        pe.wait_ge(chunk_ready, n + (b + 1))
                        for k in range(3):
                            last = nc.tensor.transpose(ps[:, pb + 1, k * P:(k + 1) * P], xch[:, b, k, :], m.ident[:])
                        last.then_inc(tok_done, 1)
                        pe.wait_ge(H_ready, n + (b + 1))
                        mm(ps[:, pb + 2, 0:P], xch[:, b, 2, :], xch[:, b, 3, :], start=True, stop=True).then_inc(gt_done, 1)
                        pe.wait_ge(R_ready, n + (b + 1))
                        mm(ps[:, pb, :], m.after[:], R[:, b, :, :].rearrange("p h i -> p (h i)"),
                           start=True, stop=True).then_inc(seg_done, 1)
                    for b in range(SEQS):
                        n = SEQS * i
                        pb = 4 * b
                        pe.wait_ge(gm_ready, n + (b + 1))
                        mm(ps[:, pb + 2, P:P + INNER], xch[:, b, 3, :], H[:, b, :, :].rearrange("p h c -> p (h c)"),
                           start=True, stop=True).then_inc(inter_done, 1)
                        pe.wait_ge(M_ready, n + (b + 1))
                        pe.wait_ge(dtx_ready, n + (b + 1))
                        for h in range(SH):
                            a = h // 2
                            last = mm(ps[:, pb + 3, h * P:(h + 1) * P], M[:, b, h, :],
                                      dtx[:, b, 2 * a:2 * a + 2, :].rearrange("p h c -> p (h c)"), start=True, stop=True)
                        last.then_inc(intra_done, 1)
                        pe.wait_ge(wxx_ready, n + (b + 1))
                        pe.wait_ge(btok_ready, n + (b + 1))
                        mm(ps[:, pb, 0:INNER], btok[:, b, :], wxx[:, b, :, :].rearrange("p h c -> p (h c)"),
                           start=True, stop=True).then_inc(dh_done, 1)
                pe.wait_ge(yg_ready, NC)
                pe.wait_ge(y2_ready, 2 * NC)
                pe.wait_ge(wout_ready, 2)
                for g in range(NT // 2 + 1):
                    if g < NT // 2:
                        if g >= 2:
                            pe.wait_ge(yT_ready, g - 1)
                        for j in range(2):
                            for c in range(2):
                                last = nc.tensor.transpose(ps[:, g % 2, (2 * j + c) * P:(2 * j + c + 1) * P],
                                                           yg[:, 2 * g + j, c * P:(c + 1) * P], m.ident[:])
                        last.then_inc(yT_done, 1)
                    if g >= 1:
                        f = g - 1
                        pe.wait_ge(yT_ready, f + 1)
                        if f >= 2:
                            pe.wait_ge(x_ready, 2 * f - 2)
                        for j in range(2):
                            for c in range(2):
                                last = mm(ps[:, 2 + f % 2, j * P:(j + 1) * P], ygT[:, f % 2, j, c, :], wout[:, c, :],
                                          start=(c == 0), stop=(c == 1))
                        last.then_inc(out_done, 1)

            @block.scalar
            def _(a):
                act = nc.scalar.activation
                ln.scalar_root(a)
                a.wait_ge(cols_turned, 1)
                nc.scalar.copy(cols[:], ps[:, 7, 0:NV]).then_inc(cols_ready, 1)
                ln.scalar_copy(a)
                a.wait_ge(cols_ready, 1)
                a.wait_ge(padded, 1)
                for n in range(NU):
                    q, blk = n // CB, n % CB
                    s, c0 = q // 2, (q % 2) * BANK
                    a.wait_ge(conv_done, n + 1)
                    act(xc[:, blk, s, c0:c0 + BANK], ps[:, 2 + n % 2, :], ACT.Identity,
                        bias=cbias[:, blk:blk + 1], scale=tap[:, CONV - 1, blk:blk + 1]).then_inc(raw_ready, 1)
                    nc.scalar.copy(raw[:, blk, s, CONV - 1 + c0:CONV - 1 + c0 + BANK],
                                   ps[:, 2 + n % 2, :]).then_inc(conv_read, 1)
                    a.wait_ge(zd_done, n + 1)
                    nc.scalar.copy(dtr[:, n, :], ps[:, 4 + n % 2, INNER:ZD]).then_inc(padded, 1)
                    act(sz[:, n, :], ps[:, 4 + n % 2, 0:INNER], ACT.Silu).then_inc(zd_read, 1)
                for n in range(NU):
                    q, blk = n // CB, n % CB
                    s, c0 = q // 2, (q % 2) * BANK
                    a.wait_ge(conv_ready, n + 1)
                    act(xc[:, blk, s, c0:c0 + BANK], xc[:, blk, s, c0:c0 + BANK], ACT.Silu).then_inc(silu_ready, 1)
                a.wait_ge(v_loaded, 96)
                act(alog[:], alog[:], ACT.Exp).then_inc(aexp_ready, 1)
                a.wait_ge(abs_ready, 1)
                act(sp_[:, 2, :, :], sp_[:, 1, :, :], ACT.Exp, scale=-1.0).then_inc(u_ready, 1)
                a.wait_ge(sums_done, 1)
                act(expo[:].rearrange("p a t h -> p (a t h)"), ps[:, 6, 0:3 * NT * SH], ACT.Exp).then_inc(expo_ready, 1)
                a.wait_ge(silu_ready, NU)
                for b in range(SEQS):
                    nc.scalar.copy(xch[:, b, :, :], xc[:, :, b, 0:P]).then_inc(chunk_ready, 1)
                with a.Fori(0, CHUNKS_ - 1) as i:
                    for b in range(SEQS):
                        n = SEQS * i
                        a.wait_ge(seg_done, n + (b + 1))
                        act(E[:, b, :, :], ps[:, 4 * b, :], ACT.Exp).then_inc(E_ready, 1)
                    for b in range(SEQS):
                        n = SEQS * i
                        a.wait_ge(inter_done, n + (b + 1))
                        nc.scalar.copy(xch[:, b, :, :], xc[:, :, b, bass.ds(P * i + P, P)]).then_inc(chunk_ready, 1)
                    for b in range(SEQS):
                        n = SEQS * i
                        a.wait_ge(M_ready, n + (b + 1))
                for b in range(SEQS):
                    n = SEQS * (CHUNKS_ - 1)
                    a.wait_ge(seg_done, n + (b + 1))
                    act(E[:, b, :, :], ps[:, 4 * b, :], ACT.Exp).then_inc(E_ready, 1)
                for c in range(NC):
                    t = (c % SEQS) * CHUNKS_ + c // SEQS
                    a.wait_ge(yg_ready, c + 1)
                    if c:
                        a.wait_ge(ssq_ready, c)
                    act(junk[:], yg[:, t, :], ACT.Square, accum_out=ssq[:, t:t + 1]).then_inc(ssq_ready, 1)
                a.wait_ge(ms_ready, 1)
                act(rms[:, 1, :], rms[:, 0, :], ACT.Sqrt).then_inc(root_ready, 1)
                for g in range(NT // 2):
                    a.wait_ge(yT_done, g + 1)
                    if g >= 2:
                        a.wait_ge(out_done, g - 1)
                    nc.scalar.copy(ygT[:, g % 2, :, :, :].rearrange("p j c t -> p (j c t)"), ps[:, g % 2, :]).then_inc(yT_ready, 1)

            @block.gpsimd
            def _(pool):
                tt = nc.gpsimd.tensor_tensor
                nc.gpsimd.memset(raw[:, :, :, 0:CONV - 1], 0.0).then_inc(padded, 1)
                pool.wait_ge(padded, 1)
                nc.gpsimd.memset(H[:], 0.0).then_inc(h_zeroed, 1)
                pool.wait_ge(h_zeroed, 1)
                for b in range(SEQS):
                    nc.gpsimd.memset(y3[:, b, :, :], 0.0).then_inc(y3_ready, 1)
                    pool.wait_ge(y3_ready, b + 1)
                pool.wait_ge(dec_ready, 1)
                pool.wait_ge(expo_ready, 1)

                def make_R(b, t):
                    tt(R[:, b, :, :], m.upto[:].unsqueeze(1).broadcast_to([P, SH, P]),
                       dec[:, t, :].rearrange("p t h -> p (t h)").unsqueeze(2).broadcast_to([P, SH, P]),
                       ALU.mult).then_inc(R_ready, 1)
                for b in range(SEQS):
                    make_R(b, slice(b * CHUNKS_, b * CHUNKS_ + 1))

                def body(i, more):
                    n = SEQS * i
                    for b in range(SEQS):
                        t = bass.ds(i + b * CHUNKS_, 1)
                        pool.wait_ge(dtx_ready, n + (b + 1))
                        tt(wxx[:, b, :, :], dtx[:, b, :, :],
                           expo[:, 1, t, :].rearrange("p t h -> p (t h)").unsqueeze(2).broadcast_to([P, SH, SP_]),
                           ALU.mult).then_inc(wxx_ready, 1)
                        if more:
                            pool.wait_ge(seg_done, n + (b + 1))
                            make_R(b, bass.ds(i + (b * CHUNKS_ + 1), 1))
                    for b in range(SEQS):
                        t = bass.ds(i + b * CHUNKS_, 1)
                        pool.wait_ge(y2_ready, 2 * n + (2 * b + 2))
                        pool.wait_ge(dx_ready, n + (b + 1))
                        tt(y3[:, b, :, :], y2[:, b, :, :], dx[:, b, :, :], ALU.add).then_inc(y3_ready, 1)
                        pool.wait_ge(y3_ready, n + (SEQS + b + 1))
                        yt = yg[:, t, :].rearrange("p t c -> p (t c)")
                        tt(yt, y3[:, b, :, :].rearrange("p h c -> p (h c)"),
                           sz[:, t, :].rearrange("p t c -> p (t c)"), ALU.mult).then_inc(yg_ready, 1)
                with pool.Fori(0, CHUNKS_ - 1) as i:
                    body(i, True)
                body(CHUNKS_ - 1, False)

            @block.vector
            def _(v):
                tt, ts, stt = nc.vector.tensor_tensor, nc.vector.tensor_scalar, nc.vector.scalar_tensor_tensor
                ln.vector(v)
                ch = Chain(v, conv_order)
                v.wait_ge(cols_ready, 1)
                for n in range(NU):
                    q, blk = n // CB, n % CB
                    s, c0 = q // 2, (q % 2) * BANK
                    v.wait_ge(raw_ready, n + 1)
                    v.wait_ge(conv_read, n + 1)
                    out = xc[:, blk, s, c0:c0 + BANK]
                    for k in range(CONV - 1):
                        ins = stt(out=out, in0=raw[:, blk, s, c0 + k:c0 + k + BANK], scalar=tap[:, k, blk:blk + 1],
                                  in1=out, op0=ALU.mult, op1=ALU.add)
                        if k < CONV - 2:
                            ch.link(ins)
                        else:
                            ins.then_inc(conv_ready, 1)
                ch = Chain(v, dt_order)
                v.wait_ge(v_loaded, 96)
                v.wait_ge(padded, 1 + NT)
                s, ab, u, den, r, r2, ser = (sp_[:, k, :, :] for k in range(7))
                shape = [P, NT, SH]

                def wide(t):
                    return t[:].unsqueeze(1).broadcast_to(shape)
                ch.link(tt(s, dtr[:], wide(dtb), ALU.add))
                stt(out=ab, in0=s, scalar=-1.0, in1=s, op0=ALU.mult, op1=ALU.max).then_inc(abs_ready, 1)
                v.wait_ge(u_ready, 1)
                ch.link(ts(den, u, 2.0, None, ALU.add))
                ch.link(nc.vector.reciprocal(r2, den))
                ch.link(tt(r, u, r2, ALU.mult))
                ch.link(tt(r2, r, r, ALU.mult))
                ch.link(ts(ser, r2, 1.0 / 15, None, ALU.mult))
                for odd in (13, 11, 9, 7, 5, 3):
                    ch.link(stt(out=ser, in0=ser, scalar=1.0 / odd, in1=r2, op0=ALU.add, op1=ALU.mult))
                ch.link(stt(out=ser, in0=ser, scalar=1.0, in1=r, op0=ALU.add, op1=ALU.mult))
                ch.link(ts(ser, ser, 2.0, None, ALU.mult))
                ch.link(stt(out=dt[:], in0=s, scalar=0.0, in1=ser, op0=ALU.max, op1=ALU.add))
                v.wait_ge(aexp_ready, 1)
                ch.link(tt(dec[:], dt[:], wide(alog), ALU.mult))
                ts(dec[:], dec[:], -1.0, DECAY_FLOOR, ALU.mult, ALU.max).then_inc(dec_ready, 1)
                for c in range(2):
                    v.wait_ge(w_loaded, 64)
                    ts(wout[:, c, :], wout[:, c, :], normw[:, c:c + 1], None, ALU.mult).then_inc(wout_ready, 1)
                tt(xn[:], xn[:], m.x[:], ALU.add).then_inc(xs_ready, 1)
                v.wait_ge(expo_ready, 1)
                v.wait_ge(h_zeroed, 1)
                for b in range(SEQS):
                    tt(Ht[:, b, :, :], H[:, b, :, :], H[:, b, :, :], ALU.mult).then_inc(H_ready, 1)

                with v.Fori(0, CHUNKS_) as i:
                    n = SEQS * i

                    def per_head(src, t):
                        return src[:, t, :].rearrange("p t h -> p (t h)").unsqueeze(2).broadcast_to([P, SH, SP_])
                    for b in range(SEQS):
                        t = bass.ds(i + b * CHUNKS_, 1)
                        pb = 4 * b
                        tok = ps[:, pb + 1, 0:INNER].rearrange("p (h c) -> p h c", h=SH)
                        v.wait_ge(tok_done, n + (b + 1))
                        v.wait_ge(H_ready, n + (b + 1))
                        tt(dtx[:, b, :, :], tok, per_head(dt, t), ALU.mult).then_inc(dtx_ready, 1)
                        nc.vector.tensor_copy(btok[:, b, :], ps[:, pb + 1, INNER:INNER + P]).then_inc(btok_ready, 1)
                        v.wait_ge(y3_ready, n + (b + 1))
                        tt(dx[:, b, :, :], tok, dsk[:].unsqueeze(2).broadcast_to([P, SH, SP_]), ALU.mult).then_inc(dx_ready, 1)
                        v.wait_ge(gt_done, n + (b + 1))
                        tt(Gm[:, b, :], ps[:, pb + 2, 0:P], m.upto[:], ALU.mult).then_inc(gm_ready, 1)
                        tt(Ht[:, b, :, :], H[:, b, :, :],
                           expo[:, 2, t, :].rearrange("p t h -> p (t h)").unsqueeze(2).broadcast_to([P, SH, SP_]),
                           ALU.mult).then_inc(ht_ready, 1)
                    for b in range(SEQS):
                        v.wait_ge(E_ready, n + (b + 1))
                        v.wait_ge(gm_ready, n + (b + 1))
                        tt(M[:, b, :, :], E[:, b, :, :], Gm[:, b, :].unsqueeze(1).broadcast_to([P, SH, P]),
                           ALU.mult).then_inc(M_ready, 1)
                    for b in range(SEQS):
                        t = bass.ds(i + b * CHUNKS_, 1)
                        pb = 4 * b
                        v.wait_ge(inter_done, n + (b + 1))
                        tt(y1[:, b, :, :], ps[:, pb + 2, P:P + INNER].rearrange("p (h c) -> p h c", h=SH),
                           expo[:, 0, t, :].rearrange("p t h -> p (t h)").unsqueeze(2).broadcast_to([P, SH, SP_]),
                           ALU.mult).then_inc(y1_ready, 1)
                        v.wait_ge(intra_done, n + (b + 1))
                        v.wait_ge(y1_ready, n + (b + 1))
                        for k in range(2):
                            own = ps[:, pb + 3, :].rearrange("p (a k h c) -> p a k h c", k=2, h=2, c=SP_)[:, :, k, k, :]
                            tt(y2[:, b, k::2, :], own, y1[:, b, k::2, :], ALU.add).then_inc(y2_ready, 1)
                        v.wait_ge(dh_done, n + (b + 1))
                        v.wait_ge(ht_ready, n + (b + 1))
                        tt(H[:, b, :, :], ps[:, pb, 0:INNER].rearrange("p (h c) -> p h c", h=SH), Ht[:, b, :, :],
                           ALU.add).then_inc(H_ready, 1)
                v.wait_ge(ssq_ready, NC)
                ch2 = Chain(v, dt_order, ch.n)
                ts(rms[:, 0, :], ssq[:], 1.0 / INNER, RMS_EPS, ALU.mult, ALU.add).then_inc(ms_ready, 1)
                v.wait_ge(root_ready, 1)
                ch2.link(nc.vector.reciprocal(rms[:, 2, :], rms[:, 1, :]))
                v.wait_ge(xs_ready, 1)
                for t in range(NT):
                    g = t // 2
                    v.wait_ge(out_done, g + 1)
                    stt(out=m.x[:, t, :], in0=ps[:, 2 + g % 2, (t % 2) * P:(t % 2 + 1) * P],
                        scalar=rms[:, 2, t:t + 1], in1=xn[:, t, :], op0=ALU.mult, op1=ALU.add).then_inc(x_ready, 1)
                v.wait_ge(x_ready, NT)


def hybrid_block(nc, x, w_in, offsets, amplitudes, sharpness, W_in, conv_w, conv_b, dt_bias, A_log, D_skip,
                 norm_w, W_out, router_w, correction_bias, up_w, down_w, shared_up_w, shared_down_w, out):
    with ExitStack() as ctx:
        m = Machine(nc, ctx)
        m.x = m.sb("x_rows", [P, NT, D])
        allot_constants(m)
        ffn = (router_w, correction_bias, up_w, down_w, shared_up_w, shared_down_w)
        attention(m, x, w_in, offsets, amplitudes, sharpness)
        m.end_stage()
        moe_ffn(m, "f1", *ffn)
        m.end_stage()
        mamba(m, W_in, conv_w, conv_b, dt_bias, A_log, D_skip, norm_w, W_out)
        m.end_stage()
        rows = out.rearrange("b (q t p) d -> (b q) p t d", p=P, t=QT)
        moe_ffn(m, "f2", *ffn, out=[rows[q] for q in range(NQ)])


_INS = ['L0_attn_a_x', 'L0_attn_a_w_in', 'L0_attn_a_kernel_offsets', 'L0_attn_a_kernel_amplitudes',
        'L0_attn_a_kernel_sharpness', 'L0_attn_b_W_in', 'L0_attn_b_conv_w', 'L0_attn_b_conv_b',
        'L0_attn_b_dt_bias', 'L0_attn_b_A_log', 'L0_attn_b_D', 'L0_attn_b_norm_w', 'L0_attn_b_W_out',
        'L0_ffn_router_w', 'L0_ffn_correction_bias', 'L0_ffn_up_w', 'L0_ffn_down_w',
        'L0_ffn_shared_up_w', 'L0_ffn_shared_down_w']
_OUTS = [((2, 1024, 128), 'float32')]


def kernel(**inputs):
    import numpy as _np
    import concourse.bacc as _bacc
    from concourse import mybir as _mybir
    from concourse.bass_utils import run_bass_kernel_spmd as _run

    nc = _bacc.Bacc("TRN2", target_bir_lowering=False, num_devices=1)
    arrays, args = {}, []
    for name in _INS:
        a = _np.ascontiguousarray(inputs[name])
        arrays[f"in_{name}_dram"] = a
        args.append(nc.dram_tensor(f"in_{name}_dram", a.shape, _mybir.dt.from_np(a.dtype), kind="ExternalInput").ap())
    for i, (shape, dtype) in enumerate(_OUTS):
        dt = _mybir.dt.from_np(_np.dtype(dtype))
        args.append(nc.dram_tensor(f"out_{i}_dram", shape, dt, kind="ExternalOutput").ap())
    hybrid_block(nc, *args)
    r = _run(nc, [arrays], core_ids=[0])
    return r.results[0]["out_0_dram"]
```

```python
import math
from contextlib import ExitStack

import concourse.bass as bass
from concourse import mybir

ALU = mybir.AluOpType
ACT = mybir.ActivationFunctionType
AX_X = mybir.AxisListType.X
F32 = mybir.dt.float32
BF16 = mybir.dt.bfloat16
F16 = mybir.dt.float16
F32R = mybir.dt.float32r

P = 128
D = 128
T = 2048
NT = T // P
BANK = 512
NQ = T // BANK
QT = BANK // P
LN_EPS = 1e-5


class Chain:

    def __init__(self, eng, sem, base=0):
        self.eng, self.sem, self.base, self.n = eng, sem, base, 0

    def add(self, ins):
        ins.then_inc(self.sem, 1)
        self.n += 1
        return ins

    def sync(self):
        self.eng.wait_ge(self.sem, self.base + self.n)

    def link(self, ins):
        self.add(ins)
        self.sync()


class Machine:

    def __init__(self, nc, ctx):
        self.nc, self.ctx = nc, ctx
        self.sems = []

    def sb(self, name, shape, dt=F32, ctx=None):
        return (ctx or self.ctx).enter_context(self.nc.sbuf_tensor(name, shape, dt))

    def ps(self, name, shape, dt=F32, ctx=None):
        return (ctx or self.ctx).enter_context(self.nc.psum_tensor(name, shape, dt))

    def sem(self, name):
        s = self.nc.alloc_semaphore(name=name)
        self.sems.append(s)
        return s

    def row_stats(self, t):
        return self.nc.vector.bn_stats(self.stats[:, t, :], self.x[:, t, :])

    def end_stage(self):
        self.nc.clear_and_free_semaphores(self.sems)
        self.sems = []
        self.nc.all_engine_barrier()


def allot_constants(m):
    m.ident = m.sb("ident", [P, P])
    m.ident16 = m.sb("ident16", [P, P], F16)
    m.identb = m.sb("identb", [P, P], BF16)
    m.flip_sum = m.sb("flip_sum", [P, 64], F16)
    m.upto = m.sb("upto", [P, P])
    m.after = m.sb("after", [P, P])
    m.ones = m.sb("ones", [P, P])
    m.spread = m.sb("spread", [P, 64, 64], F16)
    m.ident_made = m.sem("ident_made")
    m.filled, m.made = m.sem("const_filled"), m.sem("const_made")


def pool_select(m, t, pattern, base, op, fill, mult):
    return m.nc.gpsimd.affine_select(out=t, in_=t, compare_op=op, fill=fill, base=base,
                                     pattern=pattern, channel_multiplier=mult)


def constants_first(m, pool):
    m.nc.gpsimd.memset(m.ident[:], 0.0).then_inc(m.filled, 1)
    pool.wait_ge(m.filled, 1)
    pool_select(m, m.ident[:], [[-1, P]], 0, ALU.not_equal, 1.0, 1).then_inc(m.ident_made, 1)


def constants_rest(m, pool):
    nc = m.nc
    zero = [m.ident16, m.identb, m.flip_sum, m.spread]
    one = [m.upto, m.after, m.ones]
    for t in zero:
        nc.gpsimd.memset(t[:], 0.0).then_inc(m.filled, 1)
    for t in one:
        nc.gpsimd.memset(t[:], 1.0).then_inc(m.filled, 1)
    pool.wait_ge(m.filled, 1 + len(zero) + len(one))

    def select(*args):
        pool_select(m, *args).then_inc(m.made, 1)
    for t in (m.ident16, m.identb):
        select(t[:], [[-1, P]], 0, ALU.not_equal, 1.0, 1)
    select(m.flip_sum[:], [[1, 64]], -63, ALU.not_equal, 1.0, 1)
    select(m.upto[:], [[1, P]], 0, ALU.is_ge, 0.0, -1)
    select(m.after[:], [[-1, P]], -1, ALU.is_ge, 0.0, 1)
    select(m.spread[:], [[-1, 64], [0, 64]], 0, ALU.not_equal, 1.0, 1)
    pool.wait_ge(m.made, 6)
    select(m.spread[:], [[-1, 64], [0, 64]], -64, ALU.not_equal, 1.0, 1)
    select(m.flip_sum[:], [[1, 64]], -127, ALU.not_equal, 1.0, 1)
    pool.wait_ge(m.made, 8)


class LayerNorm:

    def __init__(self, m, tag, xn, xnT, bank):
        self.m, self.xn, self.xnT, self.bank = m, xn, xnT, bank
        self.tmp = m.sb(f"{tag}_tmp", [P, 8, NT], ctx=m.stage)
        self.stat = m.sem(f"{tag}_ln_order")
        self.var = m.sem(f"{tag}_var_ready")
        self.std = m.sem(f"{tag}_std_ready")
        self.norm = m.sem(f"{tag}_xn_ready")
        self.turned = m.sem(f"{tag}_turned")
        self.ready = m.sem(f"{tag}_xnT_ready")

    def vector(self, v, loaded=None):
        m, nc = self.m, self.m.nc
        ch = Chain(v, self.stat)
        if loaded:
            for t in range(NT):
                if t % QT == 0:
                    v.wait_ge(loaded[t // QT], 16)
                ch.add(m.row_stats(t))
            ch.sync()
        me, mo = m.stats[:, :, 1], m.stats[:, :, 4]
        qe, qo = m.stats[:, :, 2], m.stats[:, :, 5]
        mean, dif, sq, m2, var, rstd = (self.tmp[:, i, :] for i in (0, 1, 2, 3, 4, 6))
        tt, ts = nc.vector.tensor_tensor, nc.vector.tensor_scalar
        ch.add(tt(mean, me, mo, ALU.add))
        ch.add(tt(dif, me, mo, ALU.subtract))
        ch.link(tt(m2, qe, qo, ALU.add))
        ch.link(tt(sq, dif, dif, ALU.mult))
        ch.add(ts(mean, mean, 0.5, None, ALU.mult))
        ch.link(nc.vector.scalar_tensor_tensor(out=var, in0=sq, scalar=D / 4.0, in1=m2,
                                               op0=ALU.mult, op1=ALU.add))
        ts(var, var, 1.0 / D, LN_EPS, ALU.mult, ALU.add).then_inc(self.var, 1)
        v.wait_ge(self.std, 1)
        ch.link(nc.vector.reciprocal(rstd, self.tmp[:, 5, :]))
        for t in range(NT):
            ts(self.xn[:, t, :], m.x[:, t, :], mean[:, t:t + 1], rstd[:, t:t + 1],
               ALU.subtract, ALU.mult).then_inc(self.norm, 1)

    def scalar_root(self, a):
        a.wait_ge(self.var, 1)
        self.m.nc.scalar.activation(self.tmp[:, 5, :], self.tmp[:, 4, :], ACT.Sqrt).then_inc(self.std, 1)

    def scalar_quarter(self, a, q):
        a.wait_ge(self.turned, q + 1)
        self.m.nc.scalar.copy(self.xnT[:, q * BANK:(q + 1) * BANK], self.bank(q)).then_inc(self.ready, 1)

    def tensor_quarter(self, pe, q):
        pe.wait_ge(self.norm, QT * (q + 1))
        if q >= 2:
            pe.wait_ge(self.ready, q - 1)
        for k in range(QT):
            last = self.m.nc.tensor.transpose(self.bank(q)[:, k * P:(k + 1) * P],
                                              self.xn[:, QT * q + k, :], self.m.ident[:])
        last.then_inc(self.turned, 1)


E_ALL = 64
PAIRS = E_ALL // 2
HID = 64
GROUPS = 8
GE = E_ALL // GROUPS
TOP_GROUPS = 4
TOP_K = 8
ROUTE_SCALE = 2.5
SHARED = 2


def moe_ffn(m, tag, router_w, correction_bias, up_w, down_w, shared_up_w, shared_down_w, out=None):
    nc = m.nc
    with ExitStack() as stage:
        m.stage = stage

        def sb(name, shape, dt=F32):
            return m.sb(f"{tag}_{name}", shape, dt, stage)

        def sem(name):
            return m.sem(f"{tag}_{name}")

        xn, xnT = sb("xn", [P, NT, D]), sb("xnT", [D, T])
        acc = m.ps(f"{tag}_acc", [P, NQ, BANK], ctx=stage)
        work = m.ps(f"{tag}_work", [P, 4, BANK], ctx=stage)
        hid, cw, turn = work[:, 0:3, :], work[:, 3, :], work[:, 2:4, :]
        turn16 = turn.bitcast(F16)
        rw = sb("rw", [E_ALL, D])
        rwT = sb("rwT", [D, E_ALL])
        cbias = sb("cbias", [P, E_ALL])
        xh, xl = sb("x_high", [D, T], F32R), sb("x_low", [D, T], F32R)
        shu = sb("shu", [D, SHARED * P])
        shu_h, shu_l = sb("shu_high", [D, SHARED * P], F32R), sb("shu_low", [D, SHARED * P], F32R)
        wu_h, wu_l = sb("wu_high", [D, 2, 2 * HID], F32R), sb("wu_low", [D, 2, 2 * HID], F32R)
        shd = sb("shd", [P, SHARED, D])
        wu = sb("wu", [D, 2, 2 * HID])
        wd = sb("wd", [2 * HID, 2, D])
        score = sb("score", [P, NT, E_ALL])
        sfc = sb("sfc", [P, NT, E_ALL])
        masked = sb("masked", [P, NT, E_ALL])
        struck = sb("struck", [P, NT, E_ALL])
        top = sb("top", [P, NT, TOP_K])
        pairA, pairB = sb("pairA", [P, NT * GROUPS, 4]), sb("pairB", [P, NT * GROUPS, 4])
        quadA, quadB = sb("quadA", [P, NT * GROUPS, 2]), sb("quadB", [P, NT * GROUPS, 2])
        quadC = sb("quadC", [P, NT * GROUPS, 2])
        gbest = sb("gbest", [P, 4, NT * GROUPS])
        gsum = sb("gsum", [P, NT, GROUPS])
        ahead = sb("ahead", [P, NT, GROUPS, GROUPS])
        rank = sb("rank", [P, NT, GROUPS])
        wsum = sb("wsum", [P, 2, NT])
        chl = sb("chl", [P, NT, 2, E_ALL], F16)
        cT = sb("cT", [P, T], F16)
        relu = sb("relu", [P, 2, BANK])
        gated = sb("gated", [P, 2, BANK])
        act = sb("act", [P, 4, BANK])
        act_h, act_l = sb("act_high", [P, 4, BANK], F32R), sb("act_low", [P, 4, BANK], F32R)
        wd_h, wd_l = sb("wd_high", [2 * HID, 2, D], F32R), sb("wd_low", [2 * HID, 2, D], F32R)
        outT = sb("outT", [P, NQ, BANK])

        ln = LayerNorm(m, tag, xn, xnT, lambda q: turn[:, q % 2, :])
        small_in = sem("small_in")
        up_in = [sem("even_up_in"), sem("odd_up_in")]
        down_in = [sem("even_down_in"), sem("odd_down_in")]
        rw_turned, rw_ready = sem("rw_turned"), sem("rw_ready")
        logits_ready, score_ready = sem("logits_ready"), sem("score_ready")
        route = sem("route_order")
        ch_ready = sem("weights_ready")
        cT_turned, cT_ready = sem("cT_turned"), sem("cT_ready")
        up_done, cw_done, down_done = sem("up_done"), sem("cw_done"), sem("down_done")
        relu_ready, gate_done, act_ready = sem("relu_ready"), sem("gate_done"), sem("act_ready")
        shared_ready = sem("shared_ready")
        x_high, x_low = sem("x_high_ready"), sem("x_low_ready")
        w_high, w_low = sem("w_high_ready"), sem("w_low_ready")
        wd_high, wd_low = sem("wd_high_ready"), sem("wd_low_ready")
        act_high, act_low = sem("act_high_ready"), sem("act_low_ready")
        shu_high, shu_low = sem("shu_high_ready"), sem("shu_low_ready")
        outT_ready, out_turned, x_ready = sem("outT_ready"), sem("out_turned"), sem("x_ready")
        stored, stats_taken = sem("stored"), sem("stats_taken")

        NS = SHARED * NQ
        NR = PAIRS * NQ
        BODY = 24
        HEAD = NR % BODY
        LAG = 4

        def each_unit(eng, unit):
            for j in range(HEAD):
                unit(0, j)
            with eng.Fori(0, NR // BODY - 1) as i:
                for j in range(HEAD, HEAD + BODY):
                    unit(i, j)
            for j in range(HEAD, HEAD + BODY):
                unit(NR // BODY - 1, j)

        def past(i, j, n):
            return not isinstance(i, int) or BODY * i + j >= n

        with nc.Block() as block:
            @block.sync
            def _(sp):
                sp.dma_start(rw[:], router_w).then_inc(small_in, 16)
                sp.dma_start(cbias[:], correction_bias.rearrange("(a e) -> a e", a=1).broadcast_to([P, E_ALL])).then_inc(small_in, 16)
                sp.dma_start(shu[:], shared_up_w).then_inc(small_in, 16)
                sp.dma_start(shd[:], shared_down_w.rearrange("(s p) d -> p s d", p=P)).then_inc(small_in, 16)

                def load_up(pair, slot):
                    sp.dma_start(wu[:, slot, :].rearrange("p (e i) -> p e i", e=2),
                                 up_w[bass.ds(2 * pair, 2), :, :].rearrange("e d i -> d e i")).then_inc(up_in[slot], 16)

                def load_down(pair, slot):
                    sp.dma_start(wd[:, slot, :],
                                 down_w[bass.ds(2 * pair, 2), :, :].rearrange("e i d -> (e i) d")).then_inc(down_in[slot], 16)
                for p in range(2):
                    load_up(p, p)
                    load_down(p, p)
                with sp.Fori(0, PAIRS // 2 - 1) as i:
                    for j in range(2):
                        sp.wait_ge(w_low, 2 * i + j + 1)
                        load_up(2 * i + 2 + j, j)
                        sp.wait_ge(wd_low, 2 * i + j + 1)
                        load_down(2 * i + 2 + j, j)
                if out is not None:
                    for q in range(NQ):
                        sp.wait_ge(x_ready, q + 1)
                        sp.dma_start(out[q], m.x[:, QT * q:QT * (q + 1), :]).then_inc(stored, 16)
                    sp.wait_ge(stored, 16 * NQ)

            @block.tensor
            def _(pe):
                mm = nc.tensor.matmul
                for q in range(3):
                    ln.tensor_quarter(pe, q)
                pe.wait_ge(small_in, 64)
                nc.tensor.transpose(hid[:, 0, 0:E_ALL], rw[:], m.ident[0:E_ALL, 0:E_ALL]).then_inc(rw_turned, 1)
                ln.tensor_quarter(pe, 3)
                pe.wait_ge(rw_ready, 1)
                for t in range(NT):
                    pe.wait_ge(ln.ready, t // QT + 1)
                    last = mm(hid[:, t // 8, (t % 8) * E_ALL:(t % 8 + 1) * E_ALL],
                              xnT[:, t * P:(t + 1) * P], rwT[:], start=True, stop=True)
                last.then_inc(logits_ready, 1)

                def up(w_hi, w_lo, q, n):
                    cols = slice(q * BANK, (q + 1) * BANK)
                    mm(hid[:, n % 3, :], w_hi, xh[:, cols], start=True, stop=False)
                    mm(hid[:, n % 3, :], w_hi, xl[:, cols], start=False, stop=False)
                    mm(hid[:, n % 3, :], w_lo, xh[:, cols], start=False, stop=True).then_inc(up_done, 1)

                def down(w, q, n, start, stop):
                    mm(acc[:, q, :], w, act[:, n % 4, :], start=start, stop=stop,
                       skip_group_check=True).then_inc(down_done, 1)

                pe.wait_ge(score_ready, 1)
                pe.wait_ge(shu_low, 1)
                pe.wait_ge(x_low, NQ)
                for n in range(NS):
                    if n >= 3:
                        pe.wait_ge(relu_ready, n - 2)
                    blk = slice((n // NQ) * P, (n // NQ + 1) * P)
                    up(shu_h[:, blk], shu_l[:, blk], n % NQ, n)
                    if n >= 2:
                        k = n - 2
                        pe.wait_ge(shared_ready, k + 1)
                        down(shd[:, k // NQ, :], k % NQ, k, k < NQ, False)
                for k in range(NS - 2, NS):
                    pe.wait_ge(shared_ready, k + 1)
                    down(shd[:, k // NQ, :], k % NQ, k, False, False)
                pe.wait_ge(ch_ready, 1)
                pe.wait_ge(relu_ready, NS)
                for t in range(NT):
                    last = nc.tensor.transpose(turn16[:, t // 8, (t % 8) * P:(t % 8 + 1) * P],
                                               chl[:, t, :, :].rearrange("p a e -> p (a e)"), m.ident16[:])
                    if t % 8 == 7:
                        last.then_inc(cT_turned, 1)
                pe.wait_ge(cT_ready, 2)


                def down_routed(i, j):
                    if j % 4 == 0:
                        pe.wait_ge(wd_low, 6 * i + (j // 4 + 1))
                    pe.wait_ge(act_low, BODY * i + (j + 1))
                    slot = j // 4 % 2
                    for k, (w, x) in enumerate(((wd_h, act_h), (wd_h, act_l), (wd_l, act_h))):
                        last = mm(acc[:, j % 4, :], w[:, slot, :], x[:, j % 4, :], start=False,
                                  stop=(k == 2), skip_group_check=True)
                    last.then_inc(down_done, 1)

                def unit(i, j):
                    slot = j // 4 % 2
                    if j % 4 == 0:
                        pe.wait_ge(w_low, 6 * i + (j // 4 + 1))
                    if past(i, j, 3):
                        pe.wait_ge(act_ready, BODY * i + (j - 2))
                    up(wu_h[:, slot, :], wu_l[:, slot, :], j % 4, j)
                    if past(i, j, LAG):
                        down_routed(i, j - LAG)
                    if past(i, j, 1):
                        pe.wait_ge(gate_done, BODY * i + j)
                    e = 12 * i + 2 * (j // 4)
                    mm(cw, m.spread[:, bass.ds(e, 2), :].rearrange("p e j -> p (e j)"),
                       cT[:, (j % 4) * BANK:(j % 4 + 1) * BANK], start=True, stop=True).then_inc(cw_done, 1)
                each_unit(pe, unit)
                for j in range(LAG):
                    down_routed(NR // BODY - 1, HEAD + BODY - LAG + j)
                for q in range(NQ):
                    pe.wait_ge(outT_ready, q + 1)
                    if q >= 2:
                        pe.wait_ge(x_ready, q - 1)
                    for k in range(QT):
                        last = nc.tensor.transpose(hid[:, q % 2, k * P:(k + 1) * P],
                                                   outT[:, q, k * P:(k + 1) * P], m.ident[:])
                    last.then_inc(out_turned, 1)

            @block.scalar
            def _(a):
                ln.scalar_root(a)
                for q in range(3):
                    ln.scalar_quarter(a, q)
                a.wait_ge(rw_turned, 1)
                nc.scalar.copy(rwT[:], hid[:, 0, 0:E_ALL]).then_inc(rw_ready, 1)
                ln.scalar_quarter(a, 3)
                a.wait_ge(small_in, 64)
                nc.scalar.copy(shu_h[:], shu[:]).then_inc(shu_high, 1)
                a.wait_ge(ln.ready, NQ)
                for q in range(NQ):
                    cols = slice(q * BANK, (q + 1) * BANK)
                    nc.scalar.copy(xh[:, cols], xnT[:, cols]).then_inc(x_high, 1)

                for p in range(2):
                    a.wait_ge(up_in[p], 16)
                    nc.scalar.copy(wu_h[:, p, :], wu[:, p, :]).then_inc(w_high, 1)
                a.wait_ge(logits_ready, 1)
                nc.scalar.activation(score[:].rearrange("p t e -> p (t e)"),
                                     hid[:, 0:2, :].rearrange("p a b -> p (a b)"), ACT.Sigmoid).then_inc(score_ready, 1)
                for n in range(NS):
                    a.wait_ge(up_done, n + 1)
                    if n >= 2:
                        a.wait_ge(shared_ready, n - 1)
                    nc.scalar.activation(relu[:, n % 2, :], hid[:, n % 3, :], ACT.Relu).then_inc(relu_ready, 1)
                    a.wait_ge(relu_ready, n + 1)
                    if n >= 4:
                        a.wait_ge(down_done, n - 3)
                    nc.scalar.activation(act[:, n % 4, :], relu[:, n % 2, :], ACT.Square).then_inc(shared_ready, 1)
                a.wait_ge(cT_turned, 1)
                nc.scalar.copy(cT[:, 0:T // 2], turn16[:, 0, :]).then_inc(cT_ready, 1)
                a.wait_ge(shared_ready, NS)

                def high_part(i, j):
                    a.wait_ge(act_ready, BODY * i + (j + 1))
                    if past(i, j, 4):
                        a.wait_ge(down_done, BODY * i + (NS + j - 3))
                    nc.scalar.copy(act_h[:, j % 4, :], act[:, j % 4, :]).then_inc(act_high, 1)

                def unit(i, j):
                    pair = 6 * i + j // 4
                    a.wait_ge(up_done, BODY * i + (NS + j + 1))
                    if past(i, j, 2):
                        a.wait_ge(gate_done, BODY * i + (j - 1))
                    nc.scalar.activation(relu[:, j % 2, :], hid[:, j % 3, :], ACT.Relu).then_inc(relu_ready, 1)
                    if j % 4 == 0 and past(i, j, 4) and not (isinstance(i, int) and pair + 1 == PAIRS):
                        slot = (j // 4 + 1) % 2
                        a.wait_ge(up_in[slot], 48 * i + 16 * ((j // 4 + 1) // 2 + 1))
                        a.wait_ge(w_low, pair)
                        nc.scalar.copy(wu_h[:, slot, :], wu[:, slot, :]).then_inc(w_high, 1)
                    if j % 4 == 1:
                        slot = j // 4 % 2
                        a.wait_ge(down_in[slot], 48 * i + 16 * (j // 8 + 1))
                        if past(i, j, 8):
                            a.wait_ge(down_done, BODY * i + (NS + j - 5))
                            a.wait_ge(wd_low, pair - 1)
                        nc.scalar.copy(wd_h[:, slot, :], wd[:, slot, :]).then_inc(wd_high, 1)
                    if past(i, j, 1):
                        high_part(i, j - 1)
                each_unit(a, unit)
                high_part(NR // BODY - 1, HEAD + BODY - 1)
                for q in range(NQ):
                    a.wait_ge(down_done, NS + NR - NQ + q + 1)
                    nc.scalar.copy(outT[:, q, :], acc[:, q, :]).then_inc(outT_ready, 1)

            @block.gpsimd
            def _(pool):
                pool.wait_ge(shu_high, 1)
                nc.gpsimd.tensor_tensor(shu_l[:], shu[:], shu_h[:].bitcast(F32), ALU.subtract).then_inc(shu_low, 1)
                for q in range(NQ):
                    cols = slice(q * BANK, (q + 1) * BANK)
                    pool.wait_ge(x_high, q + 1)
                    nc.gpsimd.tensor_tensor(xl[:, cols], xnT[:, cols], xh[:, cols].bitcast(F32),
                                            ALU.subtract).then_inc(x_low, 1)
                with pool.Fori(0, NR // 4) as i:
                    for k in range(4):
                        pool.wait_ge(act_high, 4 * i + (k + 1))
                        nc.gpsimd.tensor_tensor(act_l[:, k, :], act[:, k, :], act_h[:, k, :].bitcast(F32),
                                                ALU.subtract).then_inc(act_low, 1)

            @block.vector
            def _(v):
                ln.vector(v)
                tt, ts = nc.vector.tensor_tensor, nc.vector.tensor_scalar
                ch = Chain(v, route)
                v.wait_ge(small_in, 64)
                v.wait_ge(score_ready, 1)
                ch.link(tt(sfc[:], score[:], cbias[:].unsqueeze(1).broadcast_to([P, NT, E_ALL]), ALU.add))
                s = sfc[:].rearrange("p t (g e) -> p (t g) e", g=GROUPS)
                ch.add(tt(pairA[:], s[:, :, 0:4], s[:, :, 4:8], ALU.max))
                ch.link(tt(pairB[:], s[:, :, 0:4], s[:, :, 4:8], ALU.min))
                ch.add(tt(quadA[:], pairA[:, :, 0:2], pairA[:, :, 2:4], ALU.max))
                ch.add(tt(quadB[:], pairA[:, :, 0:2], pairA[:, :, 2:4], ALU.min))
                ch.link(tt(quadC[:], pairB[:, :, 0:2], pairB[:, :, 2:4], ALU.max))
                ch.link(tt(quadB[:], quadB[:], quadC[:], ALU.max))
                ch.add(tt(gbest[:, 0, :], quadA[:, :, 0], quadA[:, :, 1], ALU.max))
                ch.add(tt(gbest[:, 1, :], quadA[:, :, 0], quadA[:, :, 1], ALU.min))
                ch.link(tt(gbest[:, 2, :], quadB[:, :, 0], quadB[:, :, 1], ALU.max))
                ch.link(tt(gbest[:, 3, :], gbest[:, 1, :], gbest[:, 2, :], ALU.max))
                ch.link(tt(gsum[:].rearrange("p t g -> p (t g)"), gbest[:, 0, :], gbest[:, 3, :], ALU.add))
                for g in range(GROUPS):
                    if g:
                        ch.add(tt(ahead[:, :, g, 0:g], gsum[:, :, 0:g],
                                  gsum[:, :, g:g + 1].broadcast_to([P, NT, g]), ALU.is_ge))
                    ch.add(tt(ahead[:, :, g, g:], gsum[:, :, g:],
                              gsum[:, :, g:g + 1].broadcast_to([P, NT, GROUPS - g]), ALU.is_gt))
                ch.sync()
                ch.link(nc.vector.tensor_reduce(rank[:], ahead[:], AX_X, ALU.add))
                ch.link(ts(rank[:], rank[:], TOP_GROUPS - 0.5, None, ALU.is_lt))
                ch.link(tt(masked[:].rearrange("p t (g e) -> p (t g) e", g=GROUPS), s,
                           rank[:].rearrange("p t g -> p (t g)").unsqueeze(2).broadcast_to([P, NT * GROUPS, GE]),
                           ALU.mult))
                for t in range(NT):
                    ch.add(nc.vector.max(top[:, t, :], masked[:, t, :]))
                ch.sync()
                for t in range(NT):
                    ch.add(nc.vector.match_replace(struck[:, t, :], top[:, t, :], masked[:, t, :], -1e30))
                ch.sync()
                ch.link(tt(struck[:], struck[:], masked[:], ALU.not_equal))
                ch.link(tt(masked[:], score[:], struck[:], ALU.mult))
                ch.link(nc.vector.tensor_reduce(wsum[:, 0, :], masked[:], AX_X, ALU.add))
                ch.link(ts(wsum[:, 0, :], wsum[:, 0, :], 1e-20, None, ALU.add))
                ch.link(nc.vector.reciprocal(wsum[:, 1, :], wsum[:, 0, :]))
                ch.link(ts(wsum[:, 0, :], wsum[:, 1, :], ROUTE_SCALE, None, ALU.mult))
                ch.link(tt(struck[:], masked[:], wsum[:, 0, :].unsqueeze(2).broadcast_to([P, NT, E_ALL]), ALU.mult))
                ch.link(nc.vector.tensor_copy(chl[:, :, 0, :], struck[:]))
                tt(chl[:, :, 1, :], struck[:], chl[:, :, 0, :], ALU.subtract).then_inc(ch_ready, 1)
                v.wait_ge(cT_turned, 2)
                nc.vector.tensor_copy(cT[:, T // 2:T], turn16[:, 1, :]).then_inc(cT_ready, 1)

                def low_part(raw, high, low, slot, ready, pairs, done):
                    v.wait_ge(ready, pairs)
                    tt(low[:, slot, :], raw[:, slot, :], high[:, slot, :].bitcast(F32), ALU.subtract).then_inc(done, 1)
                for p in range(2):
                    low_part(wu, wu_h, wu_l, p, w_high, p + 1, w_low)

                def unit(i, j):
                    pair = 6 * i + j // 4
                    v.wait_ge(relu_ready, BODY * i + (NS + j + 1))
                    v.wait_ge(cw_done, BODY * i + (j + 1))
                    if past(i, j, 2):
                        v.wait_ge(act_ready, BODY * i + (j - 1))
                    tt(gated[:, j % 2, :], relu[:, j % 2, :], cw, ALU.mult).then_inc(gate_done, 1)
                    v.wait_ge(gate_done, BODY * i + (j + 1))
                    if past(i, j, 4):
                        v.wait_ge(act_low, BODY * i + (j - 3))
                    else:
                        v.wait_ge(down_done, NS + j - 3)
                    tt(act[:, j % 4, :], gated[:, j % 2, :], hid[:, j % 3, :], ALU.mult).then_inc(act_ready, 1)
                    if j % 4 == 0 and past(i, j, 4) and not (isinstance(i, int) and pair + 1 == PAIRS):
                        low_part(wu, wu_h, wu_l, (j // 4 + 1) % 2, w_high, pair + 2, w_low)
                    if j % 4 == 1:
                        low_part(wd, wd_h, wd_l, j // 4 % 2, wd_high, pair + 1, wd_low)
                each_unit(v, unit)
                for q in range(NQ):
                    v.wait_ge(out_turned, q + 1)
                    rows = m.x[:, QT * q:QT * (q + 1), :].rearrange("p t d -> p (t d)")
                    tt(rows, hid[:, q % 2, :], rows, ALU.add).then_inc(x_ready, 1)
                    v.wait_ge(x_ready, q + 1)
                    if out is None:
                        for t in range(QT * q, QT * (q + 1)):
                            m.row_stats(t).then_inc(stats_taken, 1)
                if out is None:
                    v.wait_ge(stats_taken, NT)


HEADS = 16
HD = D // HEADS
KERNELS = 16
BATCH = 2
L = T // BATCH
LT = L // P
G4 = 4
ITERS = BATCH * HEADS // G4
PIECES = 3
QK_ROWS = PIECES * PIECES * HD
K_ROWS = 96
MAX_W = 2 * L - P
HALF = P // 2
COL_W = 2 * L - HALF
CHUNKS = 4
CW = COL_W // CHUNKS
STEPS = 2 * LT
UNITS = G4 * LT * 2
UNIT_FROM, UNIT_TO = 0, 14
EARLY = G4 * LT // 2
REST = 3 * LT // 2
STACK_DMAS = 2 * PIECES + 1


def step_columns(s, u):
    lh, mb = s // LT, LT - 1 - s % LT
    return lh * BANK - mb * P - u * HALF + L - HALF


def unit_of(k):
    if k < EARLY:
        return k // (LT // 2), k % (LT // 2), 1
    h, r = (k - EARLY) // REST, (k - EARLY) % REST
    if r < LT // 2:
        return h, r, 0
    return h, LT // 2 + (r - LT // 2) // 2, r % 2


def attention(m, x, w_in, offsets, amplitudes, sharpness):
    nc = m.nc
    with ExitStack() as stage:
        m.stage = stage

        def sb(name, shape, dt=F32, ctx=stage):
            return m.sb(f"at_{name}", shape, dt, ctx)

        def sem(name):
            return m.sem(f"at_{name}")

        kd = nc.dram_tensor("k_parts", [HEADS, PIECES * HD, T], BF16).ap()
        qd = nc.dram_tensor("q_parts", [HEADS, (2 * PIECES - 1) * HD, T], BF16).ap()
        bias_d = nc.dram_tensor("bias_rows", [2, HEADS, 2 * L], F16).ap()
        bias_lo, bias_hi = (bias_d[k] for k in range(2))

        s1 = m.ps("at_rows", [P, 2, BANK], ctx=stage)
        s2 = m.ps("at_cols", [P, 2, 2, BANK], ctx=stage)
        pv = m.ps("at_pv", [P, BANK], ctx=stage)
        tp = m.ps("at_tp", [P, BANK], ctx=stage)

        v_nat = sb("v_nat", [P, NT, D])
        q_st = sb("q_stack", [K_ROWS, 2, G4, L], BF16)
        k_st = sb("k_stack", [K_ROWS, 2, G4, L], BF16)
        vst = sb("v_stack", [P, 2, LT, G4, 32])
        zrow = sb("zero_rows", [PIECES, BANK], BF16)
        preset = sem("preset")

        def presets(pool):
            for n, (t, value) in enumerate([
                    (q_st[64:K_ROWS], 0.0), (k_st[64:K_ROWS], 1.0), (zrow[:], 0.0),
                    (vst[:, :, :, :, HD:HD + 1], 1.0), (vst[:, :, :, :, HD + 1:32], 0.0)]):
                nc.gpsimd.memset(t, value).then_inc(preset, 1)
                pool.wait_ge(preset, n + 1)

        ops = Operands(sb, sem, kd, qd, bias_hi, bias_lo, q_st, k_st, zrow)
        prologue(m, sb, sem, s1, s2, pv, tp, x, w_in, offsets, amplitudes, sharpness,
                 kd, qd, bias_hi, bias_lo, v_nat, preset, presets, ops)
        attend(m, sb, sem, s1, s2, pv, tp, v_nat, vst, ops)


class Operands:

    STORES = BATCH * (3 * PIECES - 1)

    def __init__(self, sb, sem, kd, qd, bias_hi, bias_lo, q_st, k_st, zrow):
        self.kd, self.qd, self.bias_hi, self.bias_lo = kd, qd, bias_hi, bias_lo
        self.q_st, self.k_st, self.zrow = q_st, k_st, zrow
        self.t_col = sb("table_cols", [P, G4, COL_W], F16)
        self.t_max = sb("table_max", [P, G4, MAX_W], F16)
        self.parts = sb("parts", [P, BATCH, 2, PIECES, L], BF16)
        self.stored = sem("parts_out")
        self.v_copied = sem("v_copied")
        self.early_in = [sem("early_in_even"), sem("early_in_odd")]
        self.late_in = [sem("late_in_even"), sem("late_in_odd")]
        self.max_tab_in = [sem(f"max_tab_in{h}") for h in range(G4)]
        self.tab_in = [sem(f"tab_in{c}") for c in range(CHUNKS)]

    def store_parts(self, sp, b):
        for kind, dst, blocks in ((0, self.kd, PIECES), (1, self.qd, 2 * PIECES - 1)):
            for a in range(blocks):
                sp.dma_start(dst[:, a * HD:(a + 1) * HD, b * L:(b + 1) * L],
                             self.parts[:, b, kind, a % PIECES, :]).then_inc(self.stored, 16)

    def toeplitz(self, row, g4, h0, nh, parts, c0, n):
        a = row[bass.ds(g4 + h0, nh), c0:c0 + n]
        return bass.AP(tensor=a.tensor, offset=a.offset, ap=[[1, parts], [2 * L, nh], [1, n]])

    def load_max_table(self, sp, g4, h):
        sp.dma_start(self.t_max[:, h:h + 1, :],
                     self.toeplitz(self.bias_hi, g4, h, 1, P, 0, MAX_W)).then_inc(self.max_tab_in[h], 16)

    def load_table(self, sp, g4, c):
        for r, row in ((0, self.bias_hi), (HALF, self.bias_lo)):
            sp.dma_start(self.t_col[r:r + HALF, :, c * CW:(c + 1) * CW],
                         self.toeplitz(row, g4, 0, G4, HALF, c * CW, CW)).then_inc(self.tab_in[c], 16)

    def load_rows(self, sp, st, dram, g4, b, half, done):
        rows = PIECES * HD
        c0 = b * L + half * BANK
        for s in range(PIECES):
            r = s * HD if dram is self.qd else 0
            sp.dma_start(st[s * rows:(s + 1) * rows, b, :, half * BANK:(half + 1) * BANK],
                         dram[bass.ds(g4, G4), r:r + rows, c0:c0 + BANK].rearrange("h r l -> r h l")
                         ).then_inc(done[b], 16)

    def load_q(self, sp, g4, b, half):
        done = (self.early_in, self.late_in)[half]
        self.load_rows(sp, self.q_st, self.qd, g4, b, half, done)
        sp.dma_start(self.q_st[QK_ROWS:QK_ROWS + PIECES, b, :, half * BANK:(half + 1) * BANK],
                     self.zrow[:].unsqueeze(1).broadcast_to([PIECES, G4, BANK])).then_inc(done[b], 16)

    def load_k(self, sp, g4, b, half):
        self.load_rows(sp, self.k_st, self.kd, g4, b, half, (self.late_in, self.early_in)[half])

    def load_stack(self, sp, g4, b):
        self.load_q(sp, g4, b, 0)
        self.load_k(sp, g4, b, 1)
        self.load_q(sp, g4, b, 1)
        self.load_k(sp, g4, b, 0)


def prologue(m, sb, sem, s1, s2, pv, tp, x, w_in, offsets, amplitudes, sharpness,
             kd, qd, bias_hi, bias_lo, v_nat, preset, presets, ops):
    nc = m.nc
    with ExitStack() as pro:
        def psb(name, shape, dt=F32):
            return sb(name, shape, dt, pro)
        m.stage = pro
        xn, xnT = psb("xn", [P, NT, D]), psb("xnT", [D, T])
        wraw, wT = psb("wraw", [P, 3, D]), psb("wT", [D, 3, D])
        HG = HEADS * KERNELS // P
        off, amp, shp = psb("off", [P, HG]), psb("amp", [P, HG]), psb("shp", [P, HG])
        ramp = psb("ramp", [P, 2 * L])
        gau = psb("gau", [P, HG, 2 * L])
        ramp_i = gau[:, 0, :].bitcast(mybir.dt.int32)
        amp_mask, amp_of = psb("amp_mask", [P, HG, HEADS]), psb("amp_of", [P, HG, HEADS])
        b_hi, b_lo = psb("b_hi", [HEADS, 2 * L], F16), psb("b_lo", [HEADS, 2 * L], F16)
        rest = psb("rest", [P, 2, BANK])
        parts, v_copied = ops.parts, ops.v_copied

        ln = LayerNorm(m, "at", xn, xnT, lambda q: s1[:, q % 2, :])
        w_loaded, small_loaded = sem("w_loaded"), sem("small_loaded")
        x_in = [sem(f"x_in{q}") for q in range(NQ)]
        w_turned, w_ready = sem("w_turned"), sem("w_ready")
        ramp_made, square_ready, gauss_ready = sem("ramp_made"), sem("square_ready"), sem("gauss_ready")
        mask_made, amp_ready, signs = sem("mask_made"), sem("amp_ready"), sem("signs_ready")
        bias_ready, parts_made = sem("bias_ready"), sem("bias_parts")
        bias_out = sem("bias_out")
        proj_done, proj_read, high_ready = sem("proj_done"), sem("proj_read"), sem("high_ready")
        split = sem("split_order")
        parts_ready = sem("parts_ready")
        v_done = sem("v_done")
        KINDS = 2 * NQ
        proj_bank = (pv, tp)
        with nc.Block() as block:
            @block.sync
            def _(sp):
                for t, src in ((off, offsets), (shp, sharpness), (amp, amplitudes)):
                    sp.dma_start(t[:], src.rearrange("(g h) k -> (h k) g", g=HG),
                                 allow_slow_non_contiguous=True).then_inc(small_loaded, 16)
                rows = x.rearrange("b (q t p) d -> (b q) p t d", p=P, t=QT)
                for q in range(NQ):
                    sp.dma_start(m.x[:, QT * q:QT * (q + 1), :], rows[q]).then_inc(x_in[q], 16)
                sp.dma_start(wraw[:], w_in.rearrange("(a e) d -> e a d", a=3)).then_inc(w_loaded, 16)
                sp.wait_ge(parts_ready, KINDS // 2)
                ops.store_parts(sp, 0)
                sp.wait_ge(parts_made, 2)
                sp.dma_start(bias_hi, b_hi[:]).then_inc(bias_out, 16)
                sp.dma_start(bias_lo, b_lo[:]).then_inc(bias_out, 16)
                sp.wait_ge(ops.stored, 16 * ops.STORES // BATCH)
                sp.wait_ge(preset, 5)
                ops.load_stack(sp, 0, 0)
                sp.wait_ge(bias_out, 32)
                for h in range(G4):
                    ops.load_max_table(sp, 0, h)

            @block.gpsimd
            def _(pool):
                nc.gpsimd.iota(ramp_i, [[1, 2 * L]], base=1 - L, channel_multiplier=0).then_inc(ramp_made, 1)
                constants_first(m, pool)
                nc.gpsimd.memset(amp_mask[:], 1.0).then_inc(mask_made, 1)
                pool.wait_ge(mask_made, 1)
                nc.gpsimd.affine_select(out=amp_mask[:], in_=amp_mask[:], compare_op=ALU.is_ge, fill=0.0, base=0,
                                        pattern=[[P, HG], [-KERNELS, HEADS]], channel_multiplier=1).then_inc(mask_made, 1)
                pool.wait_ge(mask_made, 2)
                nc.gpsimd.affine_select(out=amp_mask[:], in_=amp_mask[:], compare_op=ALU.is_ge, fill=0.0,
                                        base=KERNELS - 1, pattern=[[-P, HG], [KERNELS, HEADS]],
                                        channel_multiplier=-1).then_inc(mask_made, 1)
                constants_rest(m, pool)
                presets(pool)

            @block.tensor
            def _(pe):
                mm = nc.tensor.matmul

                def project(q):
                    pe.wait_ge(ln.ready, q + 1)
                    for n in (2 * q, 2 * q + 1):
                        if n >= 2:
                            pe.wait_ge(proj_read, n - 1)
                        mm(proj_bank[n % 2][:], wT[:, (0, 2)[n % 2], :], xnT[:, q * BANK:(q + 1) * BANK],
                           start=True, stop=True).then_inc(proj_done, 1)
                pe.wait_ge(w_loaded, 16)
                pe.wait_ge(m.ident_made, 1)
                for a in range(3):
                    last = nc.tensor.transpose(tp[:, a * P:(a + 1) * P], wraw[:, a, :], m.ident[:])
                last.then_inc(w_turned, 1)
                pe.wait_ge(w_ready, 2)
                for q in range(2):
                    ln.tensor_quarter(pe, q)
                for q in range(2):
                    project(q)
                for q in range(2, NQ):
                    ln.tensor_quarter(pe, q)
                pe.wait_ge(amp_ready, 1)
                pe.wait_ge(gauss_ready, HG)
                for c in range(4):
                    for g in range(HG):
                        last = mm(s2[0:HEADS, c // 2, c % 2, :], amp_of[:, g, :],
                                  gau[:, g, c * BANK:(c + 1) * BANK], start=(g == 0), stop=(g == HG - 1))
                last.then_inc(bias_ready, 1)
                for q in range(2, NQ):
                    project(q)
                for g in range(NQ):
                    if g >= 2:
                        pe.wait_ge(v_copied, g - 1)
                    for k in range(QT):
                        t = g * QT + k
                        last = mm(s1[:, g % 2, k * P:(k + 1) * P], xnT[:, t * P:(t + 1) * P], wT[:, 1, :],
                                  start=True, stop=True)
                    last.then_inc(v_done, 1)

            @block.scalar
            def _(a):
                act = nc.scalar.activation
                a.wait_ge(signs, 3)
                for g in range(HG):
                    act(gau[:, g, :], ramp[:], ACT.Square, bias=off[:, g:g + 1]).then_inc(square_ready, 1)
                ln.scalar_root(a)
                a.wait_ge(w_turned, 1)
                nc.scalar.copy(wT[:, 0:2, :].rearrange("p a d -> p (a d)"), tp[:, 0:2 * D]).then_inc(w_ready, 1)
                nc.scalar.mul(wT[:, 2, :], tp[:, 2 * D:3 * D], 1.0 / math.sqrt(HD)).then_inc(w_ready, 1)

                def high_part(n):
                    q = n // 2
                    b, c0 = q // 2, (q % 2) * BANK
                    a.wait_ge(proj_done, n + 1)
                    nc.scalar.copy(parts[:, b, n % 2, 0, c0:c0 + BANK], proj_bank[n % 2][:]).then_inc(high_ready, 1)
                def gaussian(g):
                    a.wait_ge(square_ready, g + 1)
                    act(gau[:, g, :], gau[:, g, :], ACT.Exp, scale=shp[:, g:g + 1]).then_inc(gauss_ready, 1)
                for q in range(2):
                    ln.scalar_quarter(a, q)
                high_part(0)
                high_part(1)
                gaussian(0)
                high_part(2)
                gaussian(1)
                high_part(3)
                for q in range(2, NQ):
                    ln.scalar_quarter(a, q)
                a.wait_ge(bias_ready, 1)
                nc.scalar.copy(b_hi[:], s2[0:HEADS].rearrange("p a b c -> p (a b c)")).then_inc(parts_made, 1)
                for n in range(KINDS // 2, KINDS):
                    high_part(n)
                for g in range(NQ):
                    a.wait_ge(v_done, g + 1)
                    nc.scalar.copy(v_nat[:, g * QT:(g + 1) * QT, :].rearrange("p t d -> p (t d)"),
                                   s1[:, g % 2, :]).then_inc(v_copied, 1)

            @block.vector
            def _(v):
                tt, ts = nc.vector.tensor_tensor, nc.vector.tensor_scalar
                v.wait_ge(ramp_made, 1)
                nc.vector.tensor_copy(ramp[:], ramp_i).then_inc(signs, 1)
                v.wait_ge(small_loaded, 48)
                ts(off[:], off[:], -1.0, None, ALU.mult).then_inc(signs, 1)
                nc.vector.scalar_tensor_tensor(out=shp[:], in0=shp[:], scalar=-1.0, in1=shp[:],
                                               op0=ALU.mult, op1=ALU.min).then_inc(signs, 1)
                v.wait_ge(mask_made, 3)
                tt(amp_of[:], amp_mask[:], amp[:].unsqueeze(2).broadcast_to([P, HG, HEADS]), ALU.mult).then_inc(amp_ready, 1)
                ln.vector(v, x_in)
                ch = Chain(v, split)
                for n in range(KINDS):
                    q = n // 2
                    b, c0 = q // 2, (q % 2) * BANK
                    hi, mid, lo = (parts[:, b, n % 2, k, c0:c0 + BANK] for k in range(PIECES))
                    v.wait_ge(high_ready, n + 1)
                    if n >= 2:
                        v.wait_ge(parts_ready, n - 1)
                    tt(rest[:, n % 2, :], proj_bank[n % 2][:], hi, ALU.subtract).then_inc(proj_read, 1)
                    v.wait_ge(proj_read, n + 1)
                    ch.link(nc.vector.tensor_copy(mid, rest[:, n % 2, :]))
                    tt(lo, rest[:, n % 2, :], mid, ALU.subtract).then_inc(parts_ready, 1)
                    if n == KINDS // 2 - 1:
                        v.wait_ge(parts_made, 1)
                        tt(b_lo[:], s2[0:HEADS].rearrange("p a b c -> p (a b c)"), b_hi[:], ALU.subtract).then_inc(parts_made, 1)
                v.wait_ge(parts_ready, KINDS)
                v.wait_ge(parts_made, 2)


def attend(m, sb, sem, s1, s2, pv, tp, v_nat, vst, ops):
    nc = m.nc
    q_st, k_st, t_col, t_max = ops.q_st, ops.k_st, ops.t_col, ops.t_max
    early_in, late_in, max_tab_in, tab_in = ops.early_in, ops.late_in, ops.max_tab_in, ops.tab_in
    prob = sb("prob", [P, 2, G4, BANK])
    mx = sb("maxima", [P, G4 * LT, 2])
    mtop = sb("mtop", [P, 3, G4 * LT])
    negm = sb("negm", [P, PIECES, G4 * LT], BF16)
    negT = sb("negT", [PIECES * G4 * LT, P], BF16)
    oT = sb("oT", [P, BANK])
    rden = sb("rden", [P, QT, G4])
    onorm = sb("onorm", [P, QT, G4, HD])
    tpb = tp[:].bitcast(BF16)

    first_rows, first_max = sem("first_rows"), sem("first_max")
    rows_ready, max_done = sem("rows_ready"), sem("max_done")
    m_order, negm_ready, neg_turned, neg_copied = sem("m_order"), sem("negm_ready"), sem("neg_turned"), sem("neg_copied")
    max_in = [sem("max_in_even"), sem("max_in_odd")]
    cols_ready, exp_done, pv_done = sem("cols_ready"), sem("exp_done"), sem("pv_done")
    oT_ready, o_turned, o_read, x_added = sem("oT_ready"), sem("o_turned"), sem("o_read"), sem("x_added")
    o_order = sem("o_order")
    v_ready = sem("v_ready")
    stats_taken = sem("stats_taken")

    def units_before(s):
        return UNITS * min(max(s - UNIT_FROM, 0), UNIT_TO - UNIT_FROM) // (UNIT_TO - UNIT_FROM)
    unit_steps = [range(units_before(s), units_before(s + 1)) for s in range(STEPS)]
    M_STEP = STEPS - 1
    O_STEP = (10, 2)

    def reads(s, c):
        return step_columns(s, 1) < (c + 1) * CW and step_columns(s, 0) + BANK > c * CW
    last_read = [max(s for s in range(STEPS) if reads(s, c)) for c in range(CHUNKS)]
    first_read = [min(s for s in range(STEPS) if reads(s, c)) for c in range(CHUNKS)]

    with nc.Block() as block:
        @block.sync
        def _(sp):
            ops.store_parts(sp, 1)
            for c in range(CHUNKS):
                ops.load_table(sp, 0, c)
            sp.wait_ge(ops.stored, 16 * ops.STORES)
            ops.load_stack(sp, 0, 1)
            with sp.Fori(0, ITERS // 2 - 1) as i:
                g4 = G4 * i + G4

                def step_done(b, s):
                    sp.wait_ge(cols_ready, 4 * STEPS * i + 2 * (b * STEPS + s + 1))

                def max_table(h):
                    sp.wait_ge(max_done, 2 * UNITS * i + (EARLY + (h + 1) * REST))
                    ops.load_max_table(sp, g4, h)

                def stack(b, s):
                    step_done(b, s)
                    if s == LT - 1:
                        ops.load_q(sp, g4, b, 0)
                    elif s == LT + 3:
                        ops.load_k(sp, g4, b, 1)
                    else:
                        ops.load_q(sp, g4, b, 1)
                        ops.load_k(sp, g4, b, 0)
                max_table(0)
                stack(0, LT - 1)
                max_table(1)
                max_table(2)
                stack(0, LT + 3)
                max_table(3)
                stack(0, STEPS - 1)
                for s in range(STEPS):
                    for c in range(CHUNKS):
                        if last_read[c] == s:
                            step_done(1, s)
                            ops.load_table(sp, g4, c)
                    if s in (LT - 1, LT + 3, STEPS - 1):
                        stack(1, s)

        @block.gpsimd
        def _(pool):
            def take_v(b, c0):
                nc.gpsimd.tensor_copy(
                    vst[:, b, :, :, 0:HD],
                    v_nat[:, b * LT:(b + 1) * LT, bass.ds(c0, G4 * HD)].rearrange("p t (h d) -> p t h d", h=G4)
                ).then_inc(v_ready, 1)
            take_v(0, 0)
            take_v(1, 0)
            with pool.Fori(0, ITERS // 2 - 1) as i:
                for b in range(2):
                    pool.wait_ge(pv_done, 2 * STEPS * i + (b + 1) * STEPS)
                    take_v(b, G4 * HD * i + G4 * HD)

        def pe_unit(pe, k, it, b, g_count):
            h, lb, mh = unit_of(k)
            if k == 0:
                pe.wait_ge(early_in[b], 16 * STACK_DMAS * g_count)
            if k == EARLY:
                pe.wait_ge(late_in[b], 16 * STACK_DMAS * g_count)
            first = isinstance(it, int) and it == 1
            if not (first and k < 2):
                pe.wait_ge(max_done, UNITS * (it - 1) + (k - 1))
            nc.tensor.matmul(s1[:, k % 2, :], q_st[:, b, h, lb * P:(lb + 1) * P],
                             k_st[:, b, h, mh * BANK:(mh + 1) * BANK], start=True, stop=True).then_inc(rows_ready, 1)

        def pe_turn_max(pe, it):
            pe.wait_ge(negm_ready, it + 1)
            if not (isinstance(it, int) and it == 0):
                pe.wait_ge(o_read, 2 * it - 1)
            nc.tensor.transpose(tpb[0:PIECES * G4 * LT, 0:P], negm[:].rearrange("p a n -> p (a n)"),
                                m.identb[:]).then_inc(neg_turned, 1)

        def pe_cols(pe, s, h, it, b, g_count):
            n = STEPS * it + s
            hp, j = h // 2, h % 2
            first = isinstance(it, int) and it == 0 and s == 0
            if s == 0 and h == 0:
                pe.wait_ge(max_in[b], 16 * g_count)
            if b == 0 and h == 0:
                for c in range(CHUNKS):
                    if first_read[c] == s:
                        pe.wait_ge(tab_in[c], 32 * g_count)
            if not first and j == 0:
                pe.wait_ge(exp_done, 2 * n + (hp - 1))
            lh, mb = s // LT, LT - 1 - s % LT
            out = s2[:, hp, j, :]
            nc.tensor.matmul(out, k_st[:, b, h, mb * P:(mb + 1) * P],
                             q_st[:, b, h, lh * BANK:(lh + 1) * BANK], start=True, stop=False)
            for u in range(2):
                c = step_columns(s, u)
                last = nc.tensor.matmul(out[u * HALF:(u + 1) * HALF, :], m.flip_sum[:], t_col[:, h, c:c + BANK],
                                        start=False, stop=True)
            if j == 1:
                last.then_inc(cols_ready, 1)

        def pe_pv(pe, s, it, b):
            n = STEPS * it + s
            mb = LT - 1 - s % LT
            pe.wait_ge(exp_done, 2 * n + 2)
            if s == 0:
                pe.wait_ge(v_ready, it + 1)
            if s % LT == 0 and not (isinstance(it, int) and it == 0 and s == 0):
                pe.wait_ge(oT_ready, 2 * it + s // LT)
            for h in range(G4):
                last = nc.tensor.matmul(pv[32 * h:32 * h + 32, :], vst[:, b, mb, h, :], prob[:, s % 2, h, :],
                                        start=(s % LT == 0), stop=(s % LT == LT - 1))
            last.then_inc(pv_done, 1)

        def pe_out(pe, k, wait_neg):
            pe.wait_ge(oT_ready, k + 1)
            if wait_neg is not None:
                pe.wait_ge(neg_copied, wait_neg)
            if not (isinstance(k, int) and k == 0):
                pe.wait_ge(o_read, k)
            for t in range(QT):
                last = nc.tensor.transpose(tp[:, t * P:(t + 1) * P], oT[:, t * P:(t + 1) * P], m.ident[:])
            last.then_inc(o_turned, 1)

        def pe_iteration(pe, it, b, g_count, nxt_count, first=False, final=False):
            for s in range(STEPS):
                units = [] if final else list(unit_steps[s])
                if s == M_STEP and not final:
                    pe_turn_max(pe, it + 1)
                def unit(n):
                    if n < len(units):
                        pe_unit(pe, units[n], it + 1, 1 - b, nxt_count)
                for h in range(G4):
                    if h == 2:
                        if s > 0:
                            pe_pv(pe, s - 1, it, b)
                        elif not first:
                            pe_pv(pe, STEPS - 1, it - 1, 1 - b)
                        unit(2)
                    pe_cols(pe, s, h, it, b, g_count)
                    unit((0, 1, 3, 4)[h])
                unit(5)
                if s == O_STEP[0]:
                    pe_out(pe, 2 * it, None)
                if s == O_STEP[1] and not first:
                    pe_out(pe, 2 * it - 1, it + 1)

        @block.tensor
        def _(pe):
            pe.wait_ge(early_in[0], 16 * STACK_DMAS)
            pe.wait_ge(late_in[0], 16 * STACK_DMAS)
            for k in range(UNITS // 2):
                h, lb = k // LT, k % LT
                if k >= 2:
                    pe.wait_ge(first_max, k - 1)
                for mh in range(2):
                    last = nc.tensor.matmul(s2[:, k % 2, mh, :], q_st[:, 0, h, lb * P:(lb + 1) * P],
                                            k_st[:, 0, h, mh * BANK:(mh + 1) * BANK], start=True, stop=True)
                last.then_inc(first_rows, 1)
            pe_turn_max(pe, 0)
            pe_iteration(pe, 0, 0, 1, 1, first=True)
            with pe.Fori(0, ITERS // 2 - 1) as i:
                pe_iteration(pe, 2 * i + 1, 1, i + 1, i + 2)
                pe_iteration(pe, 2 * i + 2, 0, i + 2, i + 2)
            pe_iteration(pe, ITERS - 1, 1, ITERS // 2, None, final=True)
            pe_pv(pe, STEPS - 1, ITERS - 1, 1)
            pe_out(pe, 2 * ITERS - 1, None)

        def act_negT(a, it, b, sent):
            a.wait_ge(neg_turned, it + 1)
            if sent is not None:
                a.wait_ge(max_in[1 - b], 16 * sent)
            nc.scalar.copy(negT[:], tpb[0:PIECES * G4 * LT, 0:P]).then_inc(neg_copied, 1)
            a.wait_ge(neg_copied, it + 1)
            a.dma_start(q_st[QK_ROWS:QK_ROWS + PIECES, b, :, :].rearrange("p h (t l) -> p (h t) l", l=P),
                        negT[:]).then_inc(max_in[b], 16)

        def act_iteration(a, it, b, sent, first=False, final=False):
            for s in range(STEPS):
                n = STEPS * it + s
                if s == M_STEP and not final:
                    act_negT(a, it + 1, 1 - b, sent)
                for hp in range(2):
                    a.wait_ge(cols_ready, 2 * n + (hp + 1))
                    if not (first and s < 2):
                        a.wait_ge(pv_done, n - 1)
                    nc.scalar.activation(prob[:, s % 2, 2 * hp:2 * hp + 2, :], s2[:, hp, :, :],
                                         ACT.Exp).then_inc(exp_done, 1)
                if s == LT:
                    act_oT(a, 2 * it, STEPS * it + LT)
                if s == 0 and not first:
                    act_oT(a, 2 * it - 1, STEPS * it)

        def act_oT(a, k, products):
            a.wait_ge(pv_done, products)
            if not (isinstance(k, int) and k == 0):
                a.wait_ge(o_turned, k)
            nc.scalar.copy(oT[:], pv[:]).then_inc(oT_ready, 1)

        @block.scalar
        def _(a):
            act_negT(a, 0, 0, None)
            act_iteration(a, 0, 0, 1, first=True)
            with a.Fori(0, ITERS // 2 - 1) as i:
                act_iteration(a, 2 * i + 1, 1, i + 1)
                act_iteration(a, 2 * i + 2, 0, i + 2)
            act_iteration(a, ITERS - 1, 1, None, final=True)
            act_oT(a, 2 * ITERS - 1, STEPS * ITERS)

        def dve_unit(v, k, it, g_count):
            h, lb, mh = unit_of(k)
            if k < EARLY and lb == 0 and g_count is not None:
                v.wait_ge(max_tab_in[h], 16 * g_count)
            if isinstance(it, int):
                v.wait_ge(rows_ready, UNITS * (it - 1) + (k + 1))
            else:
                v.wait_ge(rows_ready, next_rows)
                v.reg_add(next_rows, next_rows, 1)
            c = lb * P - mh * BANK + L - BANK
            nc.vector.tensor_tensor_reduce(out=s1[:, k % 2, :], in0=s1[:, k % 2, :],
                                           in1=t_max[:, h, c:c + BANK][:, ::-1], scale=1.0, scalar=-3.0e38,
                                           op0=ALU.add, op1=ALU.max,
                                           accum_out=mx[:, h * LT + lb, mh:mh + 1]).then_inc(max_done, 1)

        NEGM_LINKS = 5

        def dve_negm(v, it):
            tt, stt = nc.vector.tensor_tensor, nc.vector.scalar_tensor_tensor
            first = isinstance(it, int) and it == 0
            if first:
                v.wait_ge(first_max, UNITS // 2)
            else:
                v.wait_ge(max_done, UNITS * it)
            ch = Chain(v, m_order, NEGM_LINKS * it)
            if not (isinstance(it, int) and it == 0):
                v.wait_ge(neg_turned, it)
            ch.link(nc.vector.tensor_reduce(mtop[:, 0, :], mx[:, :, 0:1] if first else mx[:], AX_X, ALU.max))
            ch.link(nc.vector.tensor_scalar(negm[:, 0, :], mtop[:, 0, :], -1.0, None, ALU.mult))
            ch.link(stt(out=mtop[:, 1, :], in0=mtop[:, 0, :], scalar=-1.0, in1=negm[:, 0, :],
                        op0=ALU.mult, op1=ALU.subtract))
            ch.link(nc.vector.tensor_copy(negm[:, 1, :], mtop[:, 1, :]))
            ch.link(tt(mtop[:, 2, :], mtop[:, 1, :], negm[:, 1, :], ALU.subtract))
            nc.vector.tensor_copy(negm[:, 2, :], mtop[:, 2, :]).then_inc(negm_ready, 1)

        def dve_out(v, k, b, lh, c0):
            t4 = tp[:].rearrange("p (t h e) -> p t h e", t=QT, h=G4)
            v.wait_ge(o_turned, k + 1)
            if not (isinstance(k, int) and k == 0):
                v.wait_ge(x_added, k)
            nc.vector.reciprocal(rden[:], t4[:, :, :, HD]).then_inc(o_order, 1)
            v.wait_ge(o_order, k + 1)
            nc.vector.tensor_tensor(onorm[:], t4[:, :, :, 0:HD],
                                    rden[:].unsqueeze(3).broadcast_to([P, QT, G4, HD]), ALU.mult).then_inc(o_read, 1)
            v.wait_ge(o_read, k + 1)
            rows = m.x[:, b * LT + lh * QT:b * LT + (lh + 1) * QT, bass.ds(c0, G4 * HD)]
            nc.vector.tensor_tensor(rows, rows, onorm[:].rearrange("p t h e -> p t (h e)"),
                                    ALU.add).then_inc(x_added, 1)

        def dve_stats(v, added, tiles):
            v.wait_ge(x_added, added)
            for t in tiles:
                m.row_stats(t).then_inc(stats_taken, 1)

        def dve_iteration(v, it, b, c0, prev_c0, nxt_count, first=False, final=False):
            for s in range(STEPS):
                if s == O_STEP[1] + 1 and not first:
                    dve_out(v, 2 * it - 1, 1 - b, 1, prev_c0)
                    if final:
                        dve_stats(v, 2 * it, range(LT))
                if s == O_STEP[0] + 1:
                    dve_out(v, 2 * it, b, 0, c0)
                    if final:
                        dve_stats(v, 2 * it + 1, range(LT, LT + QT))
                if not final:
                    for k in unit_steps[s]:
                        dve_unit(v, k, it + 1, nxt_count)
                    if len(unit_steps[s]) and unit_steps[s][-1] == UNITS - 1:
                        dve_negm(v, it + 1)

        next_rows = nc.vector.alloc_register("next_rows")

        @block.vector
        def _(v):
            for k in range(UNITS // 2):
                h, lb = k // LT, k % LT
                if lb == 0:
                    v.wait_ge(max_tab_in[h], 16)
                v.wait_ge(first_rows, k + 1)
                scores = s2[:, k % 2, :, :].rearrange("p a b -> p (a b)")
                nc.vector.tensor_tensor_reduce(out=scores, in0=scores, in1=t_max[:, h, lb * P:lb * P + L][:, ::-1],
                                               scale=1.0, scalar=-3.0e38, op0=ALU.add, op1=ALU.max,
                                               accum_out=mx[:, k, 0:1]).then_inc(first_max, 1)
            dve_negm(v, 0)
            W = G4 * HD
            dve_iteration(v, 0, 0, 0, None, None, first=True)
            v.reg_mov(next_rows, UNITS + 1)
            with v.Fori(0, ITERS // 2 - 1) as i:
                dve_iteration(v, 2 * i + 1, 1, W * i, W * i, i + 2)
                dve_iteration(v, 2 * i + 2, 0, W * i + W, W * i, None)
            dve_iteration(v, ITERS - 1, 1, W * (ITERS // 2 - 1), W * (ITERS // 2 - 1), None, final=True)
            dve_out(v, 2 * ITERS - 1, 1, 1, W * (ITERS // 2 - 1))
            dve_stats(v, 2 * ITERS, range(LT + QT, NT))
            v.wait_ge(stats_taken, NT)


INNER = 256
STATE = 128
SH = 4
HEAD_COLS = INNER // SH
CONV = 4
CB = (INNER + 2 * STATE) // P
SEQS = 2
SEQ = T // SEQS
SEQ_CHUNKS = SEQ // P
RMS_EPS = 1e-5
DECAY_FLOOR = -1e5


def mamba(m, W_in, conv_w, conv_b, dt_bias, A_log, Dskip, norm_w, W_out):
    nc = m.nc
    with ExitStack() as stage:
        m.stage = stage

        def sb(name, shape, dt=F32):
            return m.sb(f"ss_{name}", shape, dt, stage)

        def sem(name):
            return m.sem(f"ss_{name}")

        ZD = INNER + SH
        xn, xnT = sb("xn", [P, NT, D]), sb("xnT", [D, T])
        wzd, wx = sb("wzd", [D, ZD]), sb("wx", [D, CB, P])
        NV = CONV * CB + CB + 2
        rows, cols = sb("rows", [NV, P]), sb("cols", [P, NV])
        tap = cols[:, 0:CONV * CB].rearrange("p (k b) -> p k b", k=CONV)
        cbias, normw = cols[:, CONV * CB:CONV * CB + CB], cols[:, CONV * CB + CB:NV]
        wout = sb("wout", [P, 2, D])
        dtb, alog, dsk = sb("dtb", [P, SH]), sb("alog", [P, SH]), sb("dsk", [P, SH])
        raw = sb("raw", [P, CB, SEQS, SEQ + CONV - 1])
        xc = sb("xc", [P, CB, SEQS, SEQ])
        sz = sb("sz", [P, NT, INNER])
        dtr = sb("dtr", [P, NT, SH])
        softplus = sb("softplus", [P, 9, NT, SH])
        dt, dec = sb("dt", [P, NT, SH]), sb("dec", [P, NT, SH])
        expo = sb("expo", [P, 3, NT, SH])
        xch = sb("chunk", [P, 2, CB, P])
        R = sb("R", [P, 2, SH, P])
        E = sb("E", [P, 2, SH, P])
        Gm, M = sb("Gm", [P, 2, P]), sb("M", [P, 2, SH, P])
        btok = sb("btok", [P, 2, P])
        dtx, wxx, dx = (sb(n, [P, 2, SH, HEAD_COLS]) for n in ("dtx", "wxx", "dx"))
        y1, y2, y3 = (sb(n, [P, 2, SH, HEAD_COLS]) for n in ("y1", "y2", "y3"))
        H, Ht = sb("H", [P, 2, SH, HEAD_COLS]), sb("Ht", [P, 2, SH, HEAD_COLS])
        yg = sb("yg", [P, NT, INNER])
        junk = sb("squares", [P, INNER])
        ssq = sb("ssq", [P, NT])
        rms = sb("rms", [P, 3, NT])
        ygT = sb("ygT", [P, 2, 2, 2, P])
        ps = m.ps("ss_ps", [P, 8, BANK], ctx=stage)

        ln = LayerNorm(m, "ss", xn, xnT, lambda q: ps[:, q % 2, :])
        w_loaded, v_loaded = sem("w_loaded"), sem("v_loaded")
        cols_turned, cols_ready = sem("cols_turned"), sem("cols_ready")
        zd_done, zd_read = sem("zd_done"), sem("zd_read")
        conv_done, conv_read, raw_ready = sem("conv_done"), sem("conv_read"), sem("raw_ready")
        padded = sem("padded")
        conv_order, conv_ready, silu_ready = sem("conv_order"), sem("conv_ready"), sem("silu_ready")
        sum_ready, sides_ready = sem("sum_ready"), sem("sides_ready")
        den_ready, recip_ready = sem("den_ready"), sem("recip_ready")
        dt_order, abs_ready, u_ready, aexp_ready = sem("dt_order"), sem("abs_ready"), sem("u_ready"), sem("aexp_ready")
        dec_ready, sums_done, expo_ready = sem("dec_ready"), sem("sums_done"), sem("expo_ready")
        xs_ready = sem("xs_ready")
        chunk_ready, R_ready = sem("chunk_ready"), sem("R_ready")
        tok_done, gt_done, seg_done = sem("tok_done"), sem("gt_done"), sem("seg_done")
        inter_done, intra_done, dh_done = sem("inter_done"), sem("intra_done"), sem("dh_done")
        E_ready, gm_ready, M_ready = sem("E_ready"), sem("gm_ready"), sem("M_ready")
        btok_ready, dtx_ready, dx_ready, wxx_ready = sem("btok_ready"), sem("dtx_ready"), sem("dx_ready"), sem("wxx_ready")
        y1_ready, y2_ready, y3_ready, yg_ready = sem("y1_ready"), sem("y2_ready"), sem("y3_ready"), sem("yg_ready")
        ht_ready, H_ready = sem("ht_ready"), sem("H_ready")
        ssq_ready, ms_ready, root_ready, rms_ready = sem("ssq_ready"), sem("ms_ready"), sem("root_ready"), sem("rms_ready")
        wout_ready = sem("wout_ready")
        yT_done, yT_ready, out_done, x_ready = sem("yT_done"), sem("yT_ready"), sem("out_done"), sem("x_ready")
        stats_taken = sem("stats_taken")
        NU = NQ * CB
        RECIP_AT = 11
        NC = SEQ_CHUNKS * SEQS

        with nc.Block() as block:
            @block.sync
            def _(sp):
                sp.dma_start(rows[0:CONV * CB, :], conv_w.rearrange("k (b c) -> (k b) c", c=P)).then_inc(v_loaded, 16)
                sp.dma_start(rows[CONV * CB:CONV * CB + CB, :], conv_b.rearrange("(b c) -> b c", c=P)).then_inc(v_loaded, 16)
                sp.dma_start(rows[CONV * CB + CB:NV, :], norm_w.rearrange("(b c) -> b c", c=P)).then_inc(v_loaded, 16)
                for t, src in ((dtb, dt_bias), (alog, A_log), (dsk, Dskip)):
                    sp.dma_start(t[:], src.rearrange("(a h) -> a h", a=1).broadcast_to([P, SH])).then_inc(v_loaded, 16)
                XB = INNER + CB * P
                sp.dma_start(wzd[:, 0:INNER], W_in[:, 0:INNER]).then_inc(w_loaded, 16)
                sp.dma_start(wzd[:, INNER:ZD], W_in[:, XB:XB + SH]).then_inc(w_loaded, 16)
                sp.dma_start(wx[:], W_in[:, INNER:XB].rearrange("d (b c) -> d b c", c=P)).then_inc(w_loaded, 16)
                sp.dma_start(wout[:], W_out.rearrange("(b c) d -> c b d", c=P)).then_inc(w_loaded, 16)
                sp.wait_ge(w_loaded, 64)

            @block.tensor
            def _(pe):
                mm = nc.tensor.matmul
                for q in range(2):
                    ln.tensor_quarter(pe, q)
                pe.wait_ge(v_loaded, 96)
                nc.tensor.transpose(ps[:, 7, 0:NV], rows[:], m.ident[0:NV, 0:NV]).then_inc(cols_turned, 1)
                for q in range(2, NQ):
                    ln.tensor_quarter(pe, q)
                pe.wait_ge(w_loaded, 64)
                for n in range(NU):
                    q, blk = n // CB, n % CB
                    if blk == 0:
                        pe.wait_ge(ln.ready, q + 1)
                    if n >= 2:
                        pe.wait_ge(conv_read, n - 1)
                    mm(ps[:, 2 + n % 2, :], wx[:, blk, :], xnT[:, q * BANK:(q + 1) * BANK],
                       start=True, stop=True).then_inc(conv_done, 1)
                    if n >= 2:
                        pe.wait_ge(zd_read, n - 1)
                    mm(ps[:, 4 + n % 2, 0:ZD], xnT[:, n * P:(n + 1) * P], wzd[:],
                       start=True, stop=True).then_inc(zd_done, 1)
                pe.wait_ge(dec_ready, 1)
                for k, mask in enumerate((m.upto, m.after, m.ones)):
                    last = mm(ps[:, 6, k * NT * SH:(k + 1) * NT * SH], mask[:],
                              dec[:].rearrange("p t h -> p (t h)"), start=True, stop=True)
                last.then_inc(sums_done, 1)
                pe.wait_ge(expo_ready, 1)

                with pe.Fori(0, SEQ_CHUNKS) as i:
                    for b in range(SEQS):
                        n = SEQS * i
                        pb = 4 * b
                        pe.wait_ge(chunk_ready, n + (b + 1))
                        for k in range(3):
                            last = nc.tensor.transpose(ps[:, pb + 1, k * P:(k + 1) * P], xch[:, b, k, :], m.ident[:])
                        last.then_inc(tok_done, 1)
                        pe.wait_ge(H_ready, n + (b + 1))
                        mm(ps[:, pb + 2, 0:P], xch[:, b, 2, :], xch[:, b, 3, :], start=True, stop=True).then_inc(gt_done, 1)
                        pe.wait_ge(R_ready, n + (b + 1))
                        mm(ps[:, pb, :], m.after[:], R[:, b, :, :].rearrange("p h i -> p (h i)"),
                           start=True, stop=True).then_inc(seg_done, 1)
                    for b in range(SEQS):
                        n = SEQS * i
                        pb = 4 * b
                        pe.wait_ge(gm_ready, n + (b + 1))
                        mm(ps[:, pb + 2, P:P + INNER], xch[:, b, 3, :], H[:, b, :, :].rearrange("p h c -> p (h c)"),
                           start=True, stop=True).then_inc(inter_done, 1)
                        pe.wait_ge(M_ready, n + (b + 1))
                        pe.wait_ge(dtx_ready, n + (b + 1))
                        for h in range(SH):
                            a = h // 2
                            last = mm(ps[:, pb + 3, h * P:(h + 1) * P], M[:, b, h, :],
                                      dtx[:, b, 2 * a:2 * a + 2, :].rearrange("p h c -> p (h c)"), start=True, stop=True)
                        last.then_inc(intra_done, 1)
                        pe.wait_ge(wxx_ready, n + (b + 1))
                        pe.wait_ge(btok_ready, n + (b + 1))
                        mm(ps[:, pb, 0:INNER], btok[:, b, :], wxx[:, b, :, :].rearrange("p h c -> p (h c)"),
                           start=True, stop=True).then_inc(dh_done, 1)
                pe.wait_ge(yg_ready, NC)
                pe.wait_ge(y2_ready, 2 * NC)
                pe.wait_ge(wout_ready, 2)
                for g in range(NT // 2 + 1):
                    if g < NT // 2:
                        if g >= 2:
                            pe.wait_ge(yT_ready, g - 1)
                        for j in range(2):
                            for c in range(2):
                                last = nc.tensor.transpose(ps[:, g % 2, (2 * j + c) * P:(2 * j + c + 1) * P],
                                                           yg[:, 2 * g + j, c * P:(c + 1) * P], m.ident[:])
                        last.then_inc(yT_done, 1)
                    if g >= 1:
                        f = g - 1
                        pe.wait_ge(yT_ready, f + 1)
                        if f >= 2:
                            pe.wait_ge(x_ready, 2 * f - 2)
                        for j in range(2):
                            for c in range(2):
                                last = mm(ps[:, 2 + f % 2, j * P:(j + 1) * P], ygT[:, f % 2, j, c, :], wout[:, c, :],
                                          start=(c == 0), stop=(c == 1))
                        last.then_inc(out_done, 1)

            @block.scalar
            def _(a):
                act = nc.scalar.activation
                ln.scalar_root(a)
                for q in range(2):
                    ln.scalar_quarter(a, q)
                a.wait_ge(cols_turned, 1)
                nc.scalar.copy(cols[:], ps[:, 7, 0:NV]).then_inc(cols_ready, 1)
                for q in range(2, NQ):
                    ln.scalar_quarter(a, q)
                a.wait_ge(cols_ready, 1)
                a.wait_ge(padded, 1)
                for n in range(NU):
                    q, blk = n // CB, n % CB
                    s, c0 = q // 2, (q % 2) * BANK
                    a.wait_ge(conv_done, n + 1)
                    act(xc[:, blk, s, c0:c0 + BANK], ps[:, 2 + n % 2, :], ACT.Identity,
                        bias=cbias[:, blk:blk + 1], scale=tap[:, CONV - 1, blk:blk + 1]).then_inc(raw_ready, 1)
                    nc.scalar.copy(raw[:, blk, s, CONV - 1 + c0:CONV - 1 + c0 + BANK],
                                   ps[:, 2 + n % 2, :]).then_inc(conv_read, 1)
                    a.wait_ge(zd_done, n + 1)
                    nc.scalar.copy(dtr[:, n, :], ps[:, 4 + n % 2, INNER:ZD]).then_inc(padded, 1)
                    act(sz[:, n, :], ps[:, 4 + n % 2, 0:INNER], ACT.Silu).then_inc(zd_read, 1)
                a.wait_ge(v_loaded, 96)
                act(alog[:], alog[:], ACT.Exp).then_inc(aexp_ready, 1)
                a.wait_ge(sum_ready, 1)
                act(softplus[:, 7, :, :], softplus[:, 0, :, :], ACT.Relu).then_inc(sides_ready, 1)
                act(softplus[:, 8, :, :], softplus[:, 0, :, :], ACT.Relu, scale=-1.0).then_inc(sides_ready, 1)
                a.wait_ge(abs_ready, 1)
                act(softplus[:, 2, :, :], softplus[:, 1, :, :], ACT.Exp, scale=-1.0).then_inc(u_ready, 1)
                for n in range(NU):
                    q, blk = n // CB, n % CB
                    s, c0 = q // 2, (q % 2) * BANK
                    a.wait_ge(conv_ready, n + 1)
                    act(xc[:, blk, s, c0:c0 + BANK], xc[:, blk, s, c0:c0 + BANK], ACT.Silu).then_inc(silu_ready, 1)
                a.wait_ge(sums_done, 1)
                act(expo[:].rearrange("p a t h -> p (a t h)"), ps[:, 6, 0:3 * NT * SH], ACT.Exp).then_inc(expo_ready, 1)
                a.wait_ge(silu_ready, NU)
                for b in range(SEQS):
                    nc.scalar.copy(xch[:, b, :, :], xc[:, :, b, 0:P]).then_inc(chunk_ready, 1)

                def square(i, b):
                    n = SEQS * i
                    t = bass.ds(i + b * SEQ_CHUNKS, 1)
                    a.wait_ge(yg_ready, n + (b + 1))
                    a.wait_ge(ssq_ready, n + (b + 1))
                    act(junk[:], yg[:, t, :].rearrange("p t c -> p (t c)"), ACT.Square,
                        accum_out=ssq[:, t]).then_inc(ssq_ready, 1)

                def body(i, first=False, final=False):
                    n = SEQS * i
                    for b in range(SEQS):
                        a.wait_ge(seg_done, n + (b + 1))
                        act(E[:, b, :, :], ps[:, 4 * b, :], ACT.Exp).then_inc(E_ready, 1)
                    for b in range(SEQS):
                        if not final:
                            a.wait_ge(inter_done, n + (b + 1))
                            nc.scalar.copy(xch[:, b, :, :], xc[:, :, b, bass.ds(P * i + P, P)]).then_inc(chunk_ready, 1)
                        if not first:
                            square(i - 1, b)
                    if not final:
                        for b in range(SEQS):
                            a.wait_ge(M_ready, n + (b + 1))
                body(0, first=True)
                with a.Fori(0, SEQ_CHUNKS - 2) as i:
                    body(i + 1)
                body(SEQ_CHUNKS - 1, final=True)
                for b in range(SEQS):
                    square(SEQ_CHUNKS - 1, b)
                a.wait_ge(ms_ready, 1)
                act(rms[:, 1, :], rms[:, 0, :], ACT.Sqrt).then_inc(root_ready, 1)
                for g in range(NT // 2):
                    a.wait_ge(yT_done, g + 1)
                    if g >= 2:
                        a.wait_ge(out_done, g - 1)
                    nc.scalar.copy(ygT[:, g % 2, :, :, :].rearrange("p j c t -> p (j c t)"), ps[:, g % 2, :]).then_inc(yT_ready, 1)

            @block.gpsimd
            def _(pool):
                tt = nc.gpsimd.tensor_tensor
                nc.gpsimd.memset(raw[:, :, :, 0:CONV - 1], 0.0).then_inc(padded, 1)
                pool.wait_ge(padded, 1)
                nc.gpsimd.memset(junk[:], 0.0).then_inc(ssq_ready, 1)
                pool.wait_ge(ssq_ready, 1)
                for b in range(SEQS):
                    nc.gpsimd.memset(y3[:, b, :, :], 0.0).then_inc(y3_ready, 1)
                    pool.wait_ge(y3_ready, b + 1)
                pool.wait_ge(ln.ready, NQ)
                tt(xn[:], xn[:], m.x[:], ALU.add).then_inc(xs_ready, 1)
                ts = nc.gpsimd.tensor_scalar
                ch = Chain(pool, dt_order)
                pool.wait_ge(v_loaded, 96)
                pool.wait_ge(padded, 1 + NT)
                s, ab, u, den, r, r2, ser, plus, minus = (softplus[:, k, :, :] for k in range(9))
                shape = [P, NT, SH]

                def wide(t):
                    return t[:].unsqueeze(1).broadcast_to(shape)
                tt(s, dtr[:], wide(dtb), ALU.add).then_inc(sum_ready, 1)
                pool.wait_ge(sides_ready, 2)
                tt(ab, plus, minus, ALU.add).then_inc(abs_ready, 1)
                pool.wait_ge(u_ready, 1)
                ts(den, u, 2.0, None, ALU.add).then_inc(den_ready, 1)
                pool.wait_ge(recip_ready, 1)
                ch.link(tt(r, u, r2, ALU.mult))
                ch.link(tt(r2, r, r, ALU.mult))
                ch.link(ts(ser, r2, 1.0 / 15, None, ALU.mult))
                for odd in (13, 11, 9, 7, 5, 3):
                    ch.link(ts(ser, ser, 1.0 / odd, None, ALU.add))
                    ch.link(tt(ser, ser, r2, ALU.mult))
                ch.link(ts(ser, ser, 1.0, None, ALU.add))
                ch.link(tt(ser, ser, r, ALU.mult))
                ch.link(ts(ser, ser, 2.0, None, ALU.mult))
                ch.link(tt(dt[:], plus, ser, ALU.add))
                pool.wait_ge(aexp_ready, 1)
                ch.link(tt(dec[:], dt[:], wide(alog), ALU.mult))
                ts(dec[:], dec[:], -1.0, DECAY_FLOOR, ALU.mult, ALU.max).then_inc(dec_ready, 1)
                pool.wait_ge(dec_ready, 1)
                pool.wait_ge(expo_ready, 1)

                def make_R(b, t):
                    tt(R[:, b, :, :], m.upto[:].unsqueeze(1).broadcast_to([P, SH, P]),
                       dec[:, t, :].rearrange("p t h -> p (t h)").unsqueeze(2).broadcast_to([P, SH, P]),
                       ALU.mult).then_inc(R_ready, 1)
                for b in range(SEQS):
                    make_R(b, slice(b * SEQ_CHUNKS, b * SEQ_CHUNKS + 1))

                def body(i, more):
                    n = SEQS * i
                    for b in range(SEQS):
                        t = bass.ds(i + b * SEQ_CHUNKS, 1)
                        pool.wait_ge(dtx_ready, n + (b + 1))
                        tt(wxx[:, b, :, :], dtx[:, b, :, :],
                           expo[:, 1, t, :].rearrange("p t h -> p (t h)").unsqueeze(2).broadcast_to([P, SH, HEAD_COLS]),
                           ALU.mult).then_inc(wxx_ready, 1)
                        if more:
                            pool.wait_ge(seg_done, n + (b + 1))
                            make_R(b, bass.ds(i + (b * SEQ_CHUNKS + 1), 1))
                    for b in range(SEQS):
                        t = bass.ds(i + b * SEQ_CHUNKS, 1)
                        pool.wait_ge(y2_ready, 2 * n + (2 * b + 2))
                        pool.wait_ge(dx_ready, n + (b + 1))
                        tt(y3[:, b, :, :], y2[:, b, :, :], dx[:, b, :, :], ALU.add).then_inc(y3_ready, 1)
                        pool.wait_ge(y3_ready, n + (SEQS + b + 1))
                        yt = yg[:, t, :].rearrange("p t c -> p (t c)")
                        tt(yt, y3[:, b, :, :].rearrange("p h c -> p (h c)"),
                           sz[:, t, :].rearrange("p t c -> p (t c)"), ALU.mult).then_inc(yg_ready, 1)
                with pool.Fori(0, SEQ_CHUNKS - 1) as i:
                    body(i, True)
                body(SEQ_CHUNKS - 1, False)

            @block.vector
            def _(v):
                tt, ts, stt = nc.vector.tensor_tensor, nc.vector.tensor_scalar, nc.vector.scalar_tensor_tensor
                ln.vector(v)
                ch = Chain(v, conv_order)
                v.wait_ge(cols_ready, 1)
                for n in range(NU):
                    q, blk = n // CB, n % CB
                    s, c0 = q // 2, (q % 2) * BANK
                    v.wait_ge(raw_ready, n + 1)
                    v.wait_ge(conv_read, n + 1)
                    out = xc[:, blk, s, c0:c0 + BANK]
                    for k in range(CONV - 1):
                        ins = stt(out=out, in0=raw[:, blk, s, c0 + k:c0 + k + BANK], scalar=tap[:, k, blk:blk + 1],
                                  in1=out, op0=ALU.mult, op1=ALU.add)
                        if k < CONV - 2:
                            ch.link(ins)
                        else:
                            ins.then_inc(conv_ready, 1)
                    if n == RECIP_AT:
                        v.wait_ge(den_ready, 1)
                        nc.vector.reciprocal(softplus[:, 5, :, :], softplus[:, 3, :, :]).then_inc(recip_ready, 1)
                for c in range(2):
                    v.wait_ge(w_loaded, 64)
                    ts(wout[:, c, :], wout[:, c, :], normw[:, c:c + 1], None, ALU.mult).then_inc(wout_ready, 1)
                v.wait_ge(expo_ready, 1)
                for b in range(SEQS):
                    nc.vector.memset(H[:, b, :, :], 0.0).then_inc(H_ready, 1)

                with v.Fori(0, SEQ_CHUNKS) as i:
                    n = SEQS * i

                    def per_head(src, t):
                        return src[:, t, :].rearrange("p t h -> p (t h)").unsqueeze(2).broadcast_to([P, SH, HEAD_COLS])
                    for b in range(SEQS):
                        t = bass.ds(i + b * SEQ_CHUNKS, 1)
                        pb = 4 * b
                        tok = ps[:, pb + 1, 0:INNER].rearrange("p (h c) -> p h c", h=SH)
                        v.wait_ge(tok_done, n + (b + 1))
                        v.wait_ge(H_ready, n + (b + 1))
                        tt(dtx[:, b, :, :], tok, per_head(dt, t), ALU.mult).then_inc(dtx_ready, 1)
                        nc.vector.tensor_copy(btok[:, b, :], ps[:, pb + 1, INNER:INNER + P]).then_inc(btok_ready, 1)
                        v.wait_ge(y3_ready, n + (b + 1))
                        tt(dx[:, b, :, :], tok, dsk[:].unsqueeze(2).broadcast_to([P, SH, HEAD_COLS]), ALU.mult).then_inc(dx_ready, 1)
                        v.wait_ge(gt_done, n + (b + 1))
                        tt(Gm[:, b, :], ps[:, pb + 2, 0:P], m.upto[:], ALU.mult).then_inc(gm_ready, 1)
                        tt(Ht[:, b, :, :], H[:, b, :, :],
                           expo[:, 2, t, :].rearrange("p t h -> p (t h)").unsqueeze(2).broadcast_to([P, SH, HEAD_COLS]),
                           ALU.mult).then_inc(ht_ready, 1)
                    for b in range(SEQS):
                        v.wait_ge(E_ready, n + (b + 1))
                        v.wait_ge(gm_ready, n + (b + 1))
                        tt(M[:, b, :, :], E[:, b, :, :], Gm[:, b, :].unsqueeze(1).broadcast_to([P, SH, P]),
                           ALU.mult).then_inc(M_ready, 1)
                    for b in range(SEQS):
                        t = bass.ds(i + b * SEQ_CHUNKS, 1)
                        pb = 4 * b
                        v.wait_ge(inter_done, n + (b + 1))
                        tt(y1[:, b, :, :], ps[:, pb + 2, P:P + INNER].rearrange("p (h c) -> p h c", h=SH),
                           expo[:, 0, t, :].rearrange("p t h -> p (t h)").unsqueeze(2).broadcast_to([P, SH, HEAD_COLS]),
                           ALU.mult).then_inc(y1_ready, 1)
                        v.wait_ge(intra_done, n + (b + 1))
                        v.wait_ge(y1_ready, n + (b + 1))
                        for k in range(2):
                            own = ps[:, pb + 3, :].rearrange("p (a k h c) -> p a k h c", k=2, h=2, c=HEAD_COLS)[:, :, k, k, :]
                            tt(y2[:, b, k::2, :], own, y1[:, b, k::2, :], ALU.add).then_inc(y2_ready, 1)
                        v.wait_ge(dh_done, n + (b + 1))
                        v.wait_ge(ht_ready, n + (b + 1))
                        tt(H[:, b, :, :], ps[:, pb, 0:INNER].rearrange("p (h c) -> p h c", h=SH), Ht[:, b, :, :],
                           ALU.add).then_inc(H_ready, 1)
                v.wait_ge(ssq_ready, NC + 1)
                ch2 = Chain(v, conv_order, ch.n)
                ts(rms[:, 0, :], ssq[:], 1.0 / INNER, RMS_EPS, ALU.mult, ALU.add).then_inc(ms_ready, 1)
                v.wait_ge(root_ready, 1)
                ch2.link(nc.vector.reciprocal(rms[:, 2, :], rms[:, 1, :]))
                v.wait_ge(xs_ready, 1)
                for t in range(NT):
                    g = t // 2
                    v.wait_ge(out_done, g + 1)
                    stt(out=m.x[:, t, :], in0=ps[:, 2 + g % 2, (t % 2) * P:(t % 2 + 1) * P],
                        scalar=rms[:, 2, t:t + 1], in1=xn[:, t, :], op0=ALU.mult, op1=ALU.add).then_inc(x_ready, 1)
                    if t:
                        v.wait_ge(x_ready, t)
                        m.row_stats(t - 1).then_inc(stats_taken, 1)
                v.wait_ge(x_ready, NT)
                m.row_stats(NT - 1).then_inc(stats_taken, 1)
                v.wait_ge(stats_taken, NT)


def hybrid_block(nc, x, w_in, offsets, amplitudes, sharpness, W_in, conv_w, conv_b, dt_bias, A_log, D_skip,
                 norm_w, W_out, router_w, correction_bias, up_w, down_w, shared_up_w, shared_down_w, out):
    with ExitStack() as ctx:
        m = Machine(nc, ctx)
        m.x = m.sb("x_rows", [P, NT, D])
        m.stats = m.sb("x_stats", [P, NT, 6])
        allot_constants(m)
        ffn = (router_w, correction_bias, up_w, down_w, shared_up_w, shared_down_w)
        attention(m, x, w_in, offsets, amplitudes, sharpness)
        m.end_stage()
        moe_ffn(m, "f1", *ffn)
        m.end_stage()
        mamba(m, W_in, conv_w, conv_b, dt_bias, A_log, D_skip, norm_w, W_out)
        m.end_stage()
        rows = out.rearrange("b (q t p) d -> (b q) p t d", p=P, t=QT)
        moe_ffn(m, "f2", *ffn, out=[rows[q] for q in range(NQ)])


_INS = ['L0_attn_a_x', 'L0_attn_a_w_in', 'L0_attn_a_kernel_offsets', 'L0_attn_a_kernel_amplitudes',
        'L0_attn_a_kernel_sharpness', 'L0_attn_b_W_in', 'L0_attn_b_conv_w', 'L0_attn_b_conv_b',
        'L0_attn_b_dt_bias', 'L0_attn_b_A_log', 'L0_attn_b_D', 'L0_attn_b_norm_w', 'L0_attn_b_W_out',
        'L0_ffn_router_w', 'L0_ffn_correction_bias', 'L0_ffn_up_w', 'L0_ffn_down_w',
        'L0_ffn_shared_up_w', 'L0_ffn_shared_down_w']
_OUTS = [((2, 1024, 128), 'float32')]


def kernel(**inputs):
    import numpy as _np
    import concourse.bacc as _bacc
    from concourse import mybir as _mybir
    from concourse.bass_utils import run_bass_kernel_spmd as _run

    nc = _bacc.Bacc("TRN2", target_bir_lowering=False, num_devices=1)
    arrays, args = {}, []
    for name in _INS:
        a = _np.ascontiguousarray(inputs[name])
        arrays[f"in_{name}_dram"] = a
        args.append(nc.dram_tensor(f"in_{name}_dram", a.shape, _mybir.dt.from_np(a.dtype), kind="ExternalInput").ap())
    for i, (shape, dtype) in enumerate(_OUTS):
        dt = _mybir.dt.from_np(_np.dtype(dtype))
        args.append(nc.dram_tensor(f"out_{i}_dram", shape, dt, kind="ExternalOutput").ap())
    hybrid_block(nc, *args)
    r = _run(nc, [arrays], core_ids=[0])
    return r.results[0]["out_0_dram"]
```
